# Optimizing a Trainium2 kernel written in Bass

```python
import numpy as np
import jax
import jax.numpy as jnp

def _softmax(x, axis=-1):
    return jax.nn.softmax(x, axis=axis)

def _gelu(x):
    return jax.nn.gelu(x, approximate=True)

def _silu(x):
    return jax.nn.silu(x)

def _sigmoid(x):
    return jax.nn.sigmoid(x)

def _layernorm(x, axis=-1, eps=1e-05):
    m = jnp.mean(x, axis=axis, keepdims=True)
    v = jnp.var(x, axis=axis, keepdims=True)
    return (x - m) / jnp.sqrt(v + eps)

def _scatter_add(tgt, idx, src, axis=0):
    return tgt.at[idx].add(src)

def _segment_sum(src, seg, n):
    return jax.ops.segment_sum(src, seg, n)
kernel_name = 'mk_gnn_preln_d4_gnn_r32_8f73ed'

def setup_inputs(seed: int=0):
    np.random.seed(seed)
    _w = jnp.asarray

    def _rec_inputs():
        import jax
        import jax.numpy as jnp
        _gk = jax.random.key(seed)
        x = -3.282e-05 + 0.08839 * jax.random.normal(jax.random.fold_in(_gk, 1), (3125, 128), jnp.float32)
        src = jax.random.randint(jax.random.fold_in(_gk, 2), (100000,), 0, 3125, jnp.int32)
        dst = jax.random.randint(jax.random.fold_in(_gk, 3), (100000,), 0, 3125, jnp.int32)
        _o = jnp.argsort(dst, stable=True)
        src = src[_o]
        dst = dst[_o]
        edge_weight = jax.random.uniform(jax.random.fold_in(_gk, 13), (100000,), jnp.float32, 0.0, 0.999999)
        return (x, src, dst, edge_weight)
    x, src, dst, edge_weight = _rec_inputs()

    def _L0_gnn_setup():
        import jax, jax.numpy as jnp
        import numpy as np
        N_NODES = 3125
        HIDDEN = 128
        N_EDGES = 25000
        key = jax.random.key(seed)
        ks = jax.random.split(key, 8)
        s = 1.0 / np.sqrt(HIDDEN)
        inp = {'emb': jax.random.normal(ks[0], (N_NODES, HIDDEN), jnp.float32) * s, 'Wl1': jax.random.normal(ks[1], (HIDDEN, HIDDEN), jnp.float32) * s, 'bl1': jnp.zeros((HIDDEN,), jnp.float32), 'Wr1': jax.random.normal(ks[2], (HIDDEN, HIDDEN), jnp.float32) * s, 'Wl2': jax.random.normal(ks[3], (HIDDEN, HIDDEN), jnp.float32) * s, 'bl2': jnp.zeros((HIDDEN,), jnp.float32), 'Wr2': jax.random.normal(ks[4], (HIDDEN, HIDDEN), jnp.float32) * s, 'edge_index': jax.random.randint(ks[5], (2, N_EDGES), 0, N_NODES, jnp.int64)}
        return inp
    _L0_gnn_all = _L0_gnn_setup()
    _L0_gnn_in = {k: v for k, v in _L0_gnn_all.items() if k in ('Wl1', 'bl1', 'Wr1', 'Wl2', 'bl2', 'Wr2')}
    del _L0_gnn_all

    def _L1_gnn_setup():
        import jax, jax.numpy as jnp
        import numpy as np
        N_NODES = 3125
        N_EDGES = 50000
        NODE_DIM = 128
        HIDDEN = 128
        N_LAYERS = 4
        LN_EPS = 1e-05

        def _layernorm(x, g, b):
            mu = jnp.mean(x, axis=-1, keepdims=True)
            var = jnp.mean(jnp.square(x - mu), axis=-1, keepdims=True)
            return (x - mu) * jax.lax.rsqrt(var + LN_EPS) * g + b
        key = jax.random.key(seed)
        ks = jax.random.split(key, 16)
        s = 1.0 / np.sqrt(HIDDEN)
        inp = {'x': jax.random.normal(ks[0], (N_NODES, NODE_DIM), dtype=jnp.float32), 'edge_index': jax.random.randint(ks[1], (2, N_EDGES), 0, N_NODES, dtype=jnp.int64), 'Wn': jax.random.normal(ks[2], (NODE_DIM, HIDDEN), dtype=jnp.float32) / np.sqrt(NODE_DIM), 'bn': jnp.zeros((HIDDEN,), dtype=jnp.float32), 'WQ': jax.random.normal(ks[3], (N_LAYERS, HIDDEN, HIDDEN), dtype=jnp.float32) * s, 'bQ': jnp.zeros((N_LAYERS, HIDDEN), dtype=jnp.float32), 'WK': jax.random.normal(ks[4], (N_LAYERS, HIDDEN, HIDDEN), dtype=jnp.float32) * s, 'bK': jnp.zeros((N_LAYERS, HIDDEN), dtype=jnp.float32), 'WV': jax.random.normal(ks[5], (N_LAYERS, HIDDEN, HIDDEN), dtype=jnp.float32) * s, 'bV': jnp.zeros((N_LAYERS, HIDDEN), dtype=jnp.float32), 'WO': jax.random.normal(ks[6], (N_LAYERS, HIDDEN, HIDDEN), dtype=jnp.float32) * s, 'bO': jnp.zeros((N_LAYERS, HIDDEN), dtype=jnp.float32), 'ln_g': jnp.ones((N_LAYERS, HIDDEN), dtype=jnp.float32), 'ln_b': jnp.zeros((N_LAYERS, HIDDEN), dtype=jnp.float32), 'Wout': jax.random.normal(ks[7], (HIDDEN, NODE_DIM), dtype=jnp.float32) * s, 'bout': jnp.zeros((NODE_DIM,), dtype=jnp.float32)}
        return inp
    _L1_gnn_all = _L1_gnn_setup()
    _L1_gnn_in = {k: v for k, v in _L1_gnn_all.items() if k in ('Wn', 'bn', 'WQ', 'bQ', 'WK', 'bK', 'WV', 'bV', 'WO', 'bO', 'ln_g', 'ln_b', 'Wout', 'bout')}
    del _L1_gnn_all

    def _L2_gnn_setup():
        import jax, jax.numpy as jnp
        import numpy as np
        N = 3125
        E = 50000
        D = 128
        key = jax.random.key(seed)
        k1, k2, k3, k4, k5 = jax.random.split(key, 5)
        x = jax.random.normal(k1, (N, D), dtype=jnp.float32)
        weight_low = jax.random.normal(k2, (D, D), dtype=jnp.float32) * (1.0 / np.sqrt(D))
        edge_vals = jax.random.uniform(k3, (E,), dtype=jnp.float32)
        edge_row = jax.random.randint(k4, (E,), 0, N, dtype=jnp.int64)
        edge_col = jax.random.randint(k5, (E,), 0, N, dtype=jnp.int64)
        return {'x': x, 'weight_low': weight_low, 'edge_vals': edge_vals, 'edge_row': edge_row, 'edge_col': edge_col}
    _L2_gnn_all = _L2_gnn_setup()
    _L2_gnn_in = {k: v for k, v in _L2_gnn_all.items() if k in ('weight_low',)}
    del _L2_gnn_all

    def _L3_gnn_setup():
        import jax, jax.numpy as jnp
        import numpy as np
        N_NODES = 3125
        N_EDGES = 50000
        F_IN, F_HID, F_OUT = (128, 64, 128)

        def _gcn_conv(x, W, b, src, dst, num_nodes):
            h = x @ W
            ones = jnp.ones(src.shape[0], dtype=h.dtype)
            deg = jax.ops.segment_sum(ones, dst, num_segments=num_nodes) + 1.0
            norm = jax.lax.rsqrt(deg)
            agg = jax.ops.segment_sum(h[src] * norm[src, None], dst, num_segments=num_nodes)
            return norm[:, None] * agg + (norm * norm)[:, None] * h + b
        key = jax.random.key(seed)
        k_x, k_e, k_w1, k_w2 = jax.random.split(key, 4)
        x = jax.random.normal(k_x, (N_NODES, F_IN), dtype=jnp.float32)
        edge_index = jax.random.randint(k_e, (2, N_EDGES), 0, N_NODES, dtype=jnp.int32)
        W1 = jax.random.normal(k_w1, (F_IN, F_HID), dtype=jnp.float32) * (1.0 / np.sqrt(F_IN))
        b1 = jnp.zeros((F_HID,), dtype=jnp.float32)
        W2 = jax.random.normal(k_w2, (F_HID, F_OUT), dtype=jnp.float32) * (1.0 / np.sqrt(F_HID))
        b2 = jnp.zeros((F_OUT,), dtype=jnp.float32)
        return {'x': x, 'edge_index': edge_index, 'W1': W1, 'b1': b1, 'W2': W2, 'b2': b2}
    _L3_gnn_all = _L3_gnn_setup()
    _L3_gnn_in = {k: v for k, v in _L3_gnn_all.items() if k in ('W1', 'b1', 'W2', 'b2')}
    del _L3_gnn_all
    return {'x': x, 'src': src, 'dst': dst, 'edge_weight': edge_weight, 'L0_gnn_Wl1': _L0_gnn_in['Wl1'], 'L0_gnn_bl1': _L0_gnn_in['bl1'], 'L0_gnn_Wr1': _L0_gnn_in['Wr1'], 'L0_gnn_Wl2': _L0_gnn_in['Wl2'], 'L0_gnn_bl2': _L0_gnn_in['bl2'], 'L0_gnn_Wr2': _L0_gnn_in['Wr2'], 'L1_gnn_Wn': _L1_gnn_in['Wn'], 'L1_gnn_bn': _L1_gnn_in['bn'], 'L1_gnn_WQ': _L1_gnn_in['WQ'], 'L1_gnn_bQ': _L1_gnn_in['bQ'], 'L1_gnn_WK': _L1_gnn_in['WK'], 'L1_gnn_bK': _L1_gnn_in['bK'], 'L1_gnn_WV': _L1_gnn_in['WV'], 'L1_gnn_bV': _L1_gnn_in['bV'], 'L1_gnn_WO': _L1_gnn_in['WO'], 'L1_gnn_bO': _L1_gnn_in['bO'], 'L1_gnn_ln_g': _L1_gnn_in['ln_g'], 'L1_gnn_ln_b': _L1_gnn_in['ln_b'], 'L1_gnn_Wout': _L1_gnn_in['Wout'], 'L1_gnn_bout': _L1_gnn_in['bout'], 'L2_gnn_weight_low': _L2_gnn_in['weight_low'], 'L3_gnn_W1': _L3_gnn_in['W1'], 'L3_gnn_b1': _L3_gnn_in['b1'], 'L3_gnn_W2': _L3_gnn_in['W2'], 'L3_gnn_b2': _L3_gnn_in['b2']}

def reference(x, src, dst, edge_weight, L0_gnn_Wl1, L0_gnn_bl1, L0_gnn_Wr1, L0_gnn_Wl2, L0_gnn_bl2, L0_gnn_Wr2, L1_gnn_Wn, L1_gnn_bn, L1_gnn_WQ, L1_gnn_bQ, L1_gnn_WK, L1_gnn_bK, L1_gnn_WV, L1_gnn_bV, L1_gnn_WO, L1_gnn_bO, L1_gnn_ln_g, L1_gnn_ln_b, L1_gnn_Wout, L1_gnn_bout, L2_gnn_weight_low, L3_gnn_W1, L3_gnn_b1, L3_gnn_W2, L3_gnn_b2):
    import jax
    import jax.numpy as jnp

    def _L0_gnn_ref(emb, Wl1, bl1, Wr1, Wl2, bl2, Wr2, edge_index):
        import jax, jax.numpy as jnp
        import numpy as np
        N_NODES = 3125
        HIDDEN = 128
        N_EDGES = 25000
        src, dst = (edge_index[0], edge_index[1])
        n = emb.shape[0]
        deg = jax.ops.segment_sum(jnp.ones_like(dst, jnp.float32), dst, num_segments=n)
        inv_deg = (1.0 / jnp.clip(deg, 1.0))[:, None]

        def sage_conv(x, Wl, bl, Wr):
            agg = jax.ops.segment_sum(x[src], dst, num_segments=n) * inv_deg
            return agg @ Wl.T + bl + x @ Wr.T
        x = jax.nn.relu(sage_conv(emb, Wl1, bl1, Wr1))
        x = jax.nn.relu(sage_conv(x, Wl2, bl2, Wr2))
        return x

    def _L1_gnn_ref(x, edge_index, Wn, bn, WQ, bQ, WK, bK, WV, bV, WO, bO, ln_g, ln_b, Wout, bout):
        import jax, jax.numpy as jnp
        import numpy as np
        N_NODES = 3125
        N_EDGES = 50000
        NODE_DIM = 128
        HIDDEN = 128
        N_LAYERS = 4
        LN_EPS = 1e-05

        def _layernorm(x, g, b):
            mu = jnp.mean(x, axis=-1, keepdims=True)
            var = jnp.mean(jnp.square(x - mu), axis=-1, keepdims=True)
            return (x - mu) * jax.lax.rsqrt(var + LN_EPS) * g + b
        n = x.shape[0]
        src, dst = (edge_index[0], edge_index[1])
        scale = 1.0 / np.sqrt(HIDDEN)
        h = x @ Wn + bn
        for l in range(N_LAYERS):
            Q = h @ WQ[l] + bQ[l]
            K = h @ WK[l] + bK[l]
            V = h @ WV[l] + bV[l]
            scores = jnp.sum(Q[dst] * K[src], axis=-1) * scale
            seg_max = jax.ops.segment_max(scores, dst, num_segments=n)
            e = jnp.exp(scores - seg_max[dst])
            seg_sum = jax.ops.segment_sum(e, dst, num_segments=n)
            attn = e / seg_sum[dst]
            messages = jax.ops.segment_sum(attn[:, None] * V[src], dst, num_segments=n)
            out = messages @ WO[l] + bO[l]
            h = _layernorm(h + out, ln_g[l], ln_b[l])
        return h @ Wout + bout

    def _L2_gnn_ref(x, weight_low, edge_vals, edge_row, edge_col):
        import jax, jax.numpy as jnp
        import numpy as np
        N = 3125
        E = 50000
        D = 128
        support = x @ weight_low
        messages = edge_vals[:, None] * support[edge_col]
        out = jax.ops.segment_sum(messages, edge_row, num_segments=x.shape[0])
        return out

    def _L3_gnn_ref(x, edge_index, W1, b1, W2, b2):
        import jax, jax.numpy as jnp
        import numpy as np
        N_NODES = 3125
        N_EDGES = 50000
        F_IN, F_HID, F_OUT = (128, 64, 128)

        def _gcn_conv(x, W, b, src, dst, num_nodes):
            h = x @ W
            ones = jnp.ones(src.shape[0], dtype=h.dtype)
            deg = jax.ops.segment_sum(ones, dst, num_segments=num_nodes) + 1.0
            norm = jax.lax.rsqrt(deg)
            agg = jax.ops.segment_sum(h[src] * norm[src, None], dst, num_segments=num_nodes)
            return norm[:, None] * agg + (norm * norm)[:, None] * h + b
        src, dst = (edge_index[0], edge_index[1])
        n = x.shape[0]
        h = jax.nn.relu(_gcn_conv(x, W1, b1, src, dst, n))
        return _gcn_conv(h, W2, b2, src, dst, n)
    edge_index = jnp.stack([src, dst])
    h = jnp.maximum(_layernorm(x, axis=-1), 0.0)
    x = x + _L0_gnn_ref(h, L0_gnn_Wl1, L0_gnn_bl1, L0_gnn_Wr1, L0_gnn_Wl2, L0_gnn_bl2, L0_gnn_Wr2, edge_index)
    h = jnp.maximum(_layernorm(x, axis=-1), 0.0)
    x = x + _L1_gnn_ref(h, edge_index, L1_gnn_Wn, L1_gnn_bn, L1_gnn_WQ, L1_gnn_bQ, L1_gnn_WK, L1_gnn_bK, L1_gnn_WV, L1_gnn_bV, L1_gnn_WO, L1_gnn_bO, L1_gnn_ln_g, L1_gnn_ln_b, L1_gnn_Wout, L1_gnn_bout)
    h = jnp.maximum(_layernorm(x, axis=-1), 0.0)
    x = x + _L2_gnn_ref(h, L2_gnn_weight_low, edge_weight, src, dst)
    h = jnp.maximum(_layernorm(x, axis=-1), 0.0)
    x = x + _L3_gnn_ref(h, edge_index, L3_gnn_W1, L3_gnn_b1, L3_gnn_W2, L3_gnn_b2)
    return x

_drawn_inputs = setup_inputs


def setup_inputs(seed=0):
    import zlib

    import numpy as np

    out = dict(_drawn_inputs(seed))
    spreads = {'L0_gnn_bl1': (0.0, 0.1),
     'L0_gnn_bl2': (0.0, 0.1),
     'L1_gnn_bn': (0.0, 0.1),
     'L1_gnn_bQ': (0.0, 0.8),
     'L1_gnn_bK': (0.0, 0.8),
     'L1_gnn_bV': (0.0, 0.1),
     'L1_gnn_bO': (0.0, 0.1),
     'L1_gnn_ln_g': (1.0, 0.2),
     'L1_gnn_ln_b': (0.0, 0.1),
     'L1_gnn_bout': (0.0, 0.1),
     'L3_gnn_b1': (0.0, 0.8),
     'L3_gnn_b2': (0.0, 0.8)}
    factors = {}
    for name, (base, spread) in spreads.items():
        noise = np.random.default_rng([zlib.crc32(name.encode()), seed]).standard_normal(out[name].shape)
        drawn = base * np.exp(spread * noise) if base else spread * noise
        out[name] = jnp.asarray(drawn.astype(out[name].dtype))
    for name, factor in factors.items():
        out[name] = (out[name] * factor).astype(out[name].dtype)
    return out
```

```python
import concourse.bass as bass
from concourse import mybir
from contextlib import ExitStack

N = 3125
E = 100000
D = 128
DH = 64
LAYERS = 4
P = 125
T = N // P
CE = 128
NG = -(-E // (CE * 128))
CH = -(-E // CE)
CP = NG * 128
W = 5
WT = P // W
NW = N // W
WC = T * W
WG = NW // P
RING = 4
PT = 4
PIECES = [(4 * j, min(4, T - 4 * j)) for j in range(-(-T // 4))]
MASKED = -1.0e30
ROUND = 12582912.0


def chain(eng, sem):
    count = [0]

    def link(ins):
        count[0] += 1
        ins.then_inc(sem, 1)
        eng.wait_ge(sem, count[0])

    return link


def gnn_program(nc, A, out, taps):
    fp32, bf16, i32 = mybir.dt.float32, mybir.dt.bfloat16, mybir.dt.int32
    ALU, ACT, AX = mybir.AluOpType, mybir.ActivationFunctionType, mybir.AxisListType
    ds = bass.ds

    count_d, weight_d, logmask_d = taps["count"], taps["weight"], taps["logmask"]

    outer = ExitStack()

    def act_sets(act):
        nc.scalar.preload_act_table_set("natural_log_exp_and_others")

    with outer:
        def osb(name, shape, dt):
            return outer.enter_context(nc.sbuf_tensor(name, shape, dt))

        def sem(name):
            return outer.enter_context(nc.semaphore(name))

        s_passed = sem("s_passed")

        def alone(eng):
            eng.sem_inc(s_passed, 1)

        ident = osb("ident", [128, 128], fp32)

        edges_st = ExitStack()

        def esb(name, shape, dt):
            return edges_st.enter_context(nc.sbuf_tensor(name, shape, dt))

        iota_col = esb("iota_col", [128, WC], bf16)
        window_base = esb("window_base", [128, NW], fp32)
        field = esb("field", [128, 5, CP], fp32)
        ranges = esb("ranges", [1, 2, NW], i32)

        prep = ExitStack()

        def psb(name, shape, dt):
            return prep.enter_context(nc.sbuf_tensor(name, shape, dt))

        src_i = psb("src_i", [128, NG, CE], i32)
        dst_i = psb("dst_i", [128, NG, CE], i32)
        w_f = psb("w_f", [128, NG, CE], fp32)
        srcf = psb("srcf", [128, NG, CE], fp32)
        dstf = psb("dstf", [128, NG, CE], fp32)
        tile_f = psb("tile_f", [128, NG, CE], fp32)
        win_f = psb("win_f", [128, NG, CE], fp32)
        tmp_f = psb("tmp_f", [128, NG, CE], fp32)
        part_bf = psb("part_bf", [128, NG, CE], bf16)
        edge_f = psb("edge_f", [128, 5, NG, CE], fp32)
        win_min = psb("win_min", [128, NG], fp32)
        win_max = psb("win_max", [128, NG], fp32)
        bc_max = psb("bc_max", [128, CP], fp32)
        bc_min = psb("bc_min", [128, CP], fp32)
        win_of = psb("win_of", [128, WG], fp32)
        chunk_no = psb("chunk_no", [128, CH], fp32)
        chunk_no1 = psb("chunk_no1", [128, CH], fp32)
        scr = psb("scr", [128, CH], fp32)
        lohi = psb("lohi", [128, 2, WG], fp32)
        psP = prep.enter_context(nc.psum_tensor("psP", [128, 4, 512], fp32))
        ranges_f = psb("ranges_f", [1, 2, NW], fp32)

        s_pad = sem("s_pad")
        s_edges = sem("s_edges")
        s_const = sem("s_const")
        s_fields = sem("s_fields")
        s_ftr = sem("s_ftr")
        s_fev = sem("s_fev")
        s_lohi = sem("s_lohi")
        s_row = sem("s_row")
        s_ranges = sem("s_ranges")
        s_pl = sem("s_pl")
        s_dl = sem("s_dl")
        FULL = (NG - 1) * 128 * CE
        REST = (E - FULL) // CE
        LAST = E - FULL - REST * CE

        with nc.Block() as block:
            @block.sync
            def _(sp):
                sp.wait_ge(s_pad, 1)
                for tile, a in ((src_i, A["src"]), (dst_i, A["dst"]), (w_f, A["edge_weight"])):
                    sp.dma_start(tile[:, 0:NG - 1, :], a[0:FULL].rearrange("(g p e) -> p g e", g=NG - 1, p=128)).then_inc(s_edges, 16)
                    sp.dma_start(tile[0:REST, NG - 1, :], a[FULL:FULL + REST * CE].rearrange("(p e) -> p e", p=REST)).then_inc(s_edges, 16)
                    sp.dma_start(tile[REST:REST + 1, NG - 1, 0:LAST], a[FULL + REST * CE:E].rearrange("(p e) -> p e", p=1)).then_inc(s_edges, 16)

            @block.gpsimd
            def _(pool):
                link = chain(pool, s_pl)
                nc.gpsimd.iota(iota_col[:], [[1, WC]], base=0, channel_multiplier=0, allow_small_or_imprecise_dtypes=True)
                nc.gpsimd.iota(window_base[:], [[-WC, NW]], base=0, channel_multiplier=0, allow_small_or_imprecise_dtypes=True)
                nc.gpsimd.iota(win_of[:], [[P, WG]], base=0, channel_multiplier=1, allow_small_or_imprecise_dtypes=True)
                nc.gpsimd.iota(chunk_no[:], [[1, CH]], base=0, channel_multiplier=0, allow_small_or_imprecise_dtypes=True)
                nc.gpsimd.iota(chunk_no1[:], [[1, CH]], base=1, channel_multiplier=0, allow_small_or_imprecise_dtypes=True)
                link(nc.gpsimd.memset(ident[:], 0.0))
                nc.gpsimd.affine_select(out=ident[:], in_=ident[:], compare_op=ALU.not_equal, fill=1.0, base=0,
                                        pattern=[[-1, 128]], channel_multiplier=1).then_inc(s_const, 1)

            @block.vector
            def _(dve):
                link = chain(dve, s_dl)
                v = nc.vector
                v.memset(src_i[:, NG - 1, :], N)
                v.memset(dst_i[:, NG - 1, :], N - 1)
                v.memset(w_f[:, NG - 1, :], 0.0).then_inc(s_pad, 1)
                dve.wait_ge(s_edges, 9 * 16)
                v.tensor_copy(srcf[:], src_i[:])
                link(v.tensor_copy(dstf[:], dst_i[:]))
                v.tensor_scalar(tile_f[:], srcf[:], (P - 1) / 2, 1.0 / P, ALU.subtract, ALU.mult)
                link(v.tensor_scalar(win_f[:], dstf[:], (W - 1) / 2, 1.0 / W, ALU.subtract, ALU.mult))
                v.tensor_scalar(tile_f[:], tile_f[:], ROUND, ROUND, ALU.add, ALU.subtract)
                link(v.tensor_scalar(win_f[:], win_f[:], ROUND, ROUND, ALU.add, ALU.subtract))
                v.scalar_tensor_tensor(edge_f[:, 0], tile_f[:], -float(P), srcf[:], ALU.mult, ALU.add)
                link(v.scalar_tensor_tensor(tmp_f[:], tile_f[:], float(W), dstf[:], ALU.mult, ALU.add))
                v.scalar_tensor_tensor(edge_f[:, 1], win_f[:], float(WC - W), tmp_f[:], ALU.mult, ALU.add)
                v.tensor_reduce(win_min[:], win_f[:], AX.X, ALU.min)
                v.tensor_reduce(win_max[:], win_f[:], AX.X, ALU.max)
                link(v.tensor_copy(part_bf[:], w_f[:]))
                v.tensor_copy(edge_f[:, 2], part_bf[:])
                link(v.tensor_tensor(tmp_f[:], w_f[:], part_bf[:], ALU.subtract))
                link(v.tensor_copy(part_bf[:], tmp_f[:]))
                v.tensor_copy(edge_f[:, 3], part_bf[:])
                link(v.tensor_tensor(tmp_f[:], tmp_f[:], part_bf[:], ALU.subtract))
                v.tensor_copy(edge_f[:, 4], tmp_f[:]).then_inc(s_fields, 1)
                n = 0
                for f in range(5):
                    for h, (g0, gn) in enumerate(((0, 4), (4, NG - 4))):
                        n += 1
                        dve.wait_ge(s_ftr, n)
                        v.tensor_copy(field[:, f, g0 * 128:(g0 + gn) * 128], psP[:, h, 0:gn * 128]).then_inc(s_fev, 1)
                for t in (bc_min, bc_max):
                    for h, (g0, gn) in enumerate(((0, 4), (4, NG - 4))):
                        n += 1
                        dve.wait_ge(s_ftr, n)
                        last = v.tensor_copy(t[:, g0 * 128:(g0 + gn) * 128], psP[:, h, 0:gn * 128]).then_inc(s_fev, 1)
                dve.wait_ge(s_fev, n)
                dve.wait_ge(s_const, 1)
                for g in range(WG):
                    link(v.tensor_scalar(scr[:], bc_max[:, 0:CH], win_of[:, g:g + 1], float(1 << 20), ALU.is_lt, ALU.mult))
                    link(v.tensor_tensor(scr[:], scr[:], chunk_no[:], ALU.add))
                    link(v.tensor_reduce(lohi[:, 0, g:g + 1], scr[:], AX.X, ALU.min))
                    link(v.scalar_tensor_tensor(scr[:], bc_min[:, 0:CH], win_of[:, g:g + 1], chunk_no1[:], ALU.is_le, ALU.mult))
                    link(v.tensor_reduce(lohi[:, 1, g:g + 1], scr[:], AX.X, ALU.max))
                link(v.tensor_scalar(lohi[:, 0], lohi[:, 0], float(CH - 1), None, ALU.min))
                v.scalar_tensor_tensor(lohi[:, 1], lohi[:, 0], 2.0, lohi[:, 1], ALU.add, ALU.max).then_inc(s_lohi, 1)
                dve.wait_ge(s_row, 1)
                for b in range(2):
                    v.tensor_copy(ranges_f[:, b, 0:4 * P].rearrange("o (g p) -> o g p", g=4),
                                  psP[0:1, 2 * b, :].rearrange("o (g p) -> o g p", g=4)[:, :, 0:P])
                    last = v.tensor_copy(ranges_f[:, b, 4 * P:5 * P], psP[0:1, 2 * b + 1, 0:P])
                link(last)
                v.tensor_copy(ranges[:], ranges_f[:]).then_inc(s_ranges, 1)

            @block.tensor
            def _(pe):
                pe.wait_ge(s_const, 1)
                pe.wait_ge(s_fields, 1)
                n = 0
                for f in range(5):
                    for h, (g0, gn) in enumerate(((0, 4), (4, NG - 4))):
                        if n >= 2:
                            pe.wait_ge(s_fev, n - 1)
                        for g in range(gn):
                            last = nc.tensor.transpose(psP[:, h, g * 128:(g + 1) * 128], edge_f[:, f, g0 + g, :], ident[:])
                        last.then_inc(s_ftr, 1)
                        n += 1
                for t in (win_min, win_max):
                    for h, (g0, gn) in enumerate(((0, 4), (4, NG - 4))):
                        pe.wait_ge(s_fev, n - 1)
                        for g in range(gn):
                            last = nc.tensor.matmul(psP[:, h, g * 128:(g + 1) * 128],
                                                    t[:, g0 + g:g0 + g + 1].broadcast_to([128, 128]), ident[:],
                                                    start=True, stop=True)
                        last.then_inc(s_ftr, 1)
                        n += 1
                pe.wait_ge(s_lohi, 1)
                for b in range(2):
                    for g in range(WG):
                        last = nc.tensor.matmul(psP[0:1, 2 * b + g // 4, (g % 4) * 128:(g % 4) * 128 + P], lohi[0:P, b, g:g + 1],
                                                ident[0:P, 0:P], start=True, stop=True)
                last.then_inc(s_row, 1)

        prep.close()

        build = ExitStack()

        def bsb(name, shape, dt):
            return build.enter_context(nc.sbuf_tensor(name, shape, dt))

        onehot = bsb("onehot", [128, RING, 5, 128], bf16)
        stage = bsb("stage", [P, 2, 2, T, P], fp32)
        count_f = bsb("count_f", [P, T, P], fp32)
        count_bf = bsb("count_bf", [P, T, P], bf16)
        weight_f = bsb("weight_f", [P, T, P], fp32)
        weight_T = bsb("weight_T", [P, T, P], fp32)
        logm = bsb("logm", [P, N], fp32)
        log_f = bsb("log_f", [P, N], fp32)
        none_f = bsb("none_f", [P, N], fp32)
        psW = build.enter_context(nc.psum_tensor("psW", [128, 2, 512], fp32))
        psT = build.enter_context(nc.psum_tensor("psT", [128, 2, 512], fp32))

        s_slot_free = sem("s_slot_free")
        s_hot = sem("s_hot")
        s_window = sem("s_window")
        s_half_free = sem("s_half_free")
        s_stage_free = sem("s_stage_free")
        s_count_f = sem("s_count_f")
        s_count_bf = sem("s_count_bf")
        s_turned = sem("s_turned")
        s_turned_free = sem("s_turned_free")
        s_ln = sem("s_ln")
        s_logmask = sem("s_logmask")
        s_logmask_free = sem("s_logmask_free")
        s_cd = sem("s_cd")
        s_wd = sem("s_wd")
        s_ld = sem("s_ld")
        NP = len(PIECES)

        with nc.Block() as block:
            @block.vector
            def _(dve):
                v = nc.vector
                dve.sem_inc(s_turned_free, 2)
                visit = dve.alloc_register("visit_v")
                dve.reg_mov(visit, 0)
                with dve.Fori(0, T) as dt:
                    with dve.Fori(0, WT) as ws:
                        w = dve.snap(dt * WT + ws, min_val=0, max_val=NW - 1)
                        lo = dve.value_load(ranges[0:1, 0, ds(w, 1)], min_val=0, max_val=CH - 1)
                        hi = dve.value_load(ranges[0:1, 1, ds(w, 1)], min_val=2, max_val=CH + 1)
                        with dve.Fori(lo, hi) as c:
                            n = dve.snap(visit, min_val=0, max_val=NW * CP)
                            slot = dve.snap(n & (RING - 1), min_val=0, max_val=RING - 1)
                            dve.wait_ge(s_slot_free, n + 1)
                            v.tensor_scalar(onehot[:, ds(slot, 1), 0, 0:WC], iota_col[:], field[:, 1, ds(c, 1)],
                                            window_base[:, ds(w, 1)], ALU.subtract, ALU.is_equal)
                            v.tensor_scalar(onehot[:, ds(slot, 1), 1, 0:P], iota_col[:, 0:P], field[:, 0, ds(c, 1)], None,
                                            ALU.is_equal)
                            for k in range(3):
                                last = v.tensor_scalar(onehot[:, ds(slot, 1), 2 + k, 0:P], iota_col[:, 0:P],
                                                       field[:, 0, ds(c, 1)], field[:, 2 + k, ds(c, 1)],
                                                       ALU.is_equal, ALU.mult)
                            last.then_inc(s_hot, 1)
                            dve.reg_add(visit, visit, 1)
                    par = dve.snap(dt & 1, min_val=0, max_val=1)
                    dve.wait_ge(s_half_free, (dt + 1) * WT + 2)
                    v.tensor_copy(weight_f[:], stage[:, ds(par, 1), 1])
                    v.tensor_copy(count_f[:], stage[:, ds(par, 1), 0]).then_inc(s_count_f, 1)
                    dve.wait_ge(s_cd, (dt + 1) * 16)
                    v.tensor_scalar(count_bf[:], stage[:, ds(par, 1), 0].rearrange('p o a d -> p (o a) d'), 1.0, None, ALU.mult).then_inc(s_count_bf, 1)
                    dve.sem_inc(s_stage_free, 1)
                    dve.wait_ge(s_logmask, dt + 1)
                    for j, (a0, an) in enumerate(PIECES):
                        cols = slice(a0 * P, (a0 + an) * P)
                        dve.wait_ge(s_turned, dt * (2 * NP) + j + 1)
                        v.tensor_scalar(none_f[:, cols], psT[0:P, j % 2, 0:an * P], 0.0, MASKED, ALU.is_equal, ALU.mult)
                        v.tensor_scalar(log_f[:, cols], psT[0:P, j % 2, 0:an * P], 1.0, None, ALU.max).then_inc(s_turned_free, 1)
                    dve.wait_ge(s_wd, (dt + 1) * 16)
                    for j, (a0, an) in enumerate(PIECES):
                        dve.wait_ge(s_turned, dt * (2 * NP) + NP + j + 1)
                        v.tensor_copy(weight_T[:, a0:a0 + an].rearrange("p a d -> p (a d)"),
                                      psT[0:P, (NP + j) % 2, 0:an * P]).then_inc(s_turned_free, 1)

            @block.tensor
            def _(pe):
                t = nc.tensor
                pe.sem_inc(s_slot_free, RING)
                visit = pe.alloc_register("visit_t")
                pe.reg_mov(visit, 0)

                def products(w, half, first):
                    n = pe.snap(visit, min_val=0, max_val=NW * CP)
                    slot = pe.snap(n & (RING - 1), min_val=0, max_val=RING - 1)
                    pe.wait_ge(s_hot, n + 1)
                    cols = onehot[:, ds(slot, 1), 0, 0:WC]
                    t.matmul(psW[0:P, ds(half, 1), 0:WC], onehot[:, ds(slot, 1), 1, 0:P], cols,
                             start=first, stop=True, skip_group_check=True)
                    for k in range(3):
                        last = t.matmul(psW[0:P, ds(half, 1), 128:128 + WC], onehot[:, ds(slot, 1), 2 + k, 0:P], cols,
                                        start=False, stop=True, skip_group_check=True)
                    last.then_inc(s_slot_free, 1)
                    pe.reg_add(visit, visit, 1)

                with pe.Fori(0, T) as dt:
                    with pe.Fori(0, WT) as ws:
                        w = pe.snap(dt * WT + ws, min_val=0, max_val=NW - 1)
                        half = pe.snap(w & 1, min_val=0, max_val=1)
                        lo = pe.value_load(ranges[0:1, 0, ds(w, 1)], min_val=0, max_val=CH - 1)
                        hi = pe.value_load(ranges[0:1, 1, ds(w, 1)], min_val=2, max_val=CH + 1)
                        pe.wait_ge(s_half_free, w + 1)
                        products(w, half, True)
                        with pe.Fori(lo + 1, hi) as c:
                            products(w, half, False)
                        t.matmul(psW[0:P, ds(half, 1), 384:385], iota_col[:, 0:P], iota_col[:, 0:1],
                                 start=False, stop=True, skip_group_check=True).then_inc(s_window, 1)
                    pe.wait_ge(s_count_f, dt + 1)
                    for k, of in enumerate((count_f, weight_f)):
                        for j, (a0, an) in enumerate(PIECES):
                            pe.wait_ge(s_turned_free, dt * (2 * NP) + (k * NP + j + 1))
                            for a in range(an):
                                last = t.transpose(psT[0:P, (k * NP + j) % 2, a * P:(a + 1) * P], of[:, a0 + a, :], ident[0:P, 0:P])
                            last.then_inc(s_turned, 1)

            @block.scalar
            def _(act):
                act_sets(act)
                act.sem_inc(s_half_free, 2)
                act.sem_inc(s_stage_free, 1)
                with act.Fori(0, T) as dt:
                    par = act.snap(dt & 1, min_val=0, max_val=1)
                    act.wait_ge(s_stage_free, dt + 1)
                    with act.Fori(0, WT) as ws:
                        w = act.snap(dt * WT + ws, min_val=0, max_val=NW - 1)
                        half = act.snap(w & 1, min_val=0, max_val=1)
                        act.wait_ge(s_window, w + 1)
                        for k in range(2):
                            last = nc.scalar.copy(stage[:, ds(par, 1), k, :, ds(ws * W, W)],
                                                  psW[0:P, ds(half, 1), 128 * k:128 * k + WC].rearrange("p o (a d) -> p o a d", a=T))
                        last.then_inc(s_half_free, 1)
                    act.wait_ge(s_turned_free, dt * (2 * NP) + (NP + 2))
                    nc.scalar.activation(log_f[:], log_f[:], ACT.Ln).then_inc(s_ln, 1)

            @block.gpsimd
            def _(pool):
                pool.sem_inc(s_logmask, 1)
                with pool.Fori(0, T) as dt:
                    pool.wait_ge(s_ln, dt + 1)
                    pool.wait_ge(s_logmask_free, dt + 1)
                    nc.gpsimd.tensor_tensor(logm[:], log_f[:], none_f[:], ALU.add).then_inc(s_logmask, 1)

            @block.sync
            def _(sp):
                sp.sem_inc(s_stage_free, 1)
                sp.sem_inc(s_cd, 16)
                sp.sem_inc(s_wd, 16)
                sp.sem_inc(s_logmask_free, 1)
                with sp.Fori(0, T) as dt:
                    sp.wait_ge(s_count_bf, dt + 1)
                    sp.dma_start(count_d[ds(dt, 1)].rearrange("o p a d -> p (o a) d"), count_bf[:]).then_inc(s_cd, 16)
                    sp.wait_ge(s_logmask, dt + 2)
                    alone(sp)
                    sp.dma_start(logmask_d[ds(dt, 1)].rearrange("o p n -> (o p) n"), logm[:]).then_inc(s_ld, 16)
                    sp.wait_ge(s_turned_free, (dt + 1) * (2 * NP) + 2)
                    sp.dma_start(weight_d[ds(dt, 1)].rearrange("o p a d -> p (o a) d"), weight_T[:]).then_inc(s_wd, 16)
                    sp.wait_ge(s_ld, (dt + 1) * 16)
                    sp.sem_inc(s_logmask_free, 1)
                sp.wait_ge(s_cd, (T + 1) * 16)
                sp.wait_ge(s_wd, (T + 1) * 16)

        build.close()
        edges_st.close()

        x_all = osb("x_all", [P, T, D], fp32)
        inv_deg = osb("inv_deg", [P, T], fp32)
        norm = osb("norm", [P, T], fp32)
        w_sage = osb("w_sage", [128, 4, D], fp32)
        w_n = osb("w_n", [128, D], fp32)
        w_out = osb("w_out", [128, D], fp32)
        w_low = osb("w_low", [128, D], fp32)
        w_1 = osb("w_1", [128, DH], fp32)
        w_2 = osb("w_2", [DH, D], fp32)
        bias = osb("bias", [P, 6, D], fp32)
        bn_col = osb("bn_col", [128, 1], fp32)
        minus_half = osb("minus_half", [128, T], fp32)

        BL1, BL2, BN, BOUT, B1, B2 = range(6)

        def row(ap):
            return ap.rearrange("(o d) -> o d", o=1).broadcast_to([P, ap.shape[0]])

        def column(ap):
            return ap.rearrange("(d o) -> d o", o=1)

        def tiles(eng):
            with eng.Fori(0, T // 2) as k:
                yield eng.snap(2 * k, min_val=0, max_val=T - 3), 0
                yield eng.snap(2 * k + 1, min_val=1, max_val=T - 2), 1
            yield T - 1, 0

        class Chain:

            def __init__(self, eng, semaphore, per_tile):
                self.eng, self.sem, self.per_tile = eng, semaphore, per_tile

            def tile(self, i):
                self.base, self.n = i * self.per_tile, 0

            def link(self, ins):
                self.n += 1
                assert self.n <= self.per_tile
                ins.then_inc(self.sem, 1)
                self.eng.wait_ge(self.sem, self.base + self.n)

            def alone(self):
                self.eng.sem_inc(s_passed, 1)

            def end(self):
                assert self.n == self.per_tile, self.n

        def split_parts(v, chain_, parts, i, y, rest, width, scale=None):
            hi = parts[:, ds(i, 1), 0:width]
            mid = parts[:, ds(i, 1), width:2 * width]
            lo = parts[:, ds(i, 1), 2 * width:3 * width]
            if scale is not None:
                chain_.link(v.tensor_scalar(hi, y, scale, None, ALU.mult))
                chain_.link(v.scalar_tensor_tensor(rest, y, scale, hi.rearrange("p o d -> p (o d)"), ALU.mult, ALU.subtract))
            else:
                chain_.link(v.tensor_scalar(hi, y, 1.0, None, ALU.mult))
                chain_.link(v.tensor_tensor(rest, y, hi.rearrange("p o d -> p (o d)"), ALU.subtract))
            chain_.link(v.tensor_scalar(mid, rest, 1.0, None, ALU.mult))
            return v.tensor_tensor(lo, rest, mid.rearrange("p o d -> p (o d)"), ALU.subtract)

        def normalise(v, chain_, x, stats, moments, centered, s_var):
            chain_.link(v.bn_stats(stats, x))
            chain_.alone()
            chain_.link(v.bn_aggr(moments[:, 0:2], stats))
            v.tensor_scalar(moments[:, 2:3], moments[:, 1:2], 1e-5, None, ALU.add).then_inc(s_var, 1)
            return v.tensor_scalar(centered, x, moments[:, 0:1], None, ALU.subtract)

        def rsqrt(pool, moments, s_var, s_rstd, i, u):
            pool.wait_ge(s_var, i + 1)
            nc.gpsimd.tensor_tensor(moments[:, u, 3:4], moments[:, u, 2:3], minus_half[0:P, 0:1], ALU.pow).then_inc(s_rstd, 1)

        PARTS = 3 * D + 1

        h_att = osb("h_att", [P, T, D], fp32)
        hT = osb("hT", [128, T, P], fp32)

        sage = ExitStack()

        def ssb(name, shape, dt):
            return sage.enter_context(nc.sbuf_tensor(name, shape, dt))

        parts_a = ssb("parts_a", [P, T, PARTS], bf16)
        parts_b = ssb("parts_b", [P, T, PARTS], bf16)
        self_a = ssb("self_a", [P, T, D], fp32)
        self_b = ssb("self_b", [P, T, D], fp32)
        w_raw = ssb("w_raw", [128, 4, D], fp32)
        w_nodes = ssb("w_nodes", [P, 2, D], fp32)
        w_turned = ssb("w_turned", [128, 2, P], fp32)
        agg = ssb("agg", [P, 2, D], fp32)
        rest = ssb("rest", [P, 2, D], fp32)
        stats = ssb("stats", [P, 2, 6], fp32)
        moments = ssb("moments", [P, 2, 4], fp32)
        centered = ssb("centered", [P, 2, D], fp32)
        x_new = ssb("x_new", [P, 2, D], fp32)
        deg1 = ssb("deg1", [P, 2, 2], fp32)
        mat = ssb("mat", [P, 2, T, P], bf16)
        psA = sage.enter_context(nc.psum_tensor("psA", [128, 2, 512], fp32))
        psY = sage.enter_context(nc.psum_tensor("psY", [128, 2, 512], fp32))
        psX = sage.enter_context(nc.psum_tensor("psX", [128, 2, 512], fp32))

        s_load = sem("s_load")
        s_half = sem("s_half")
        s_wt = sem("s_wt")
        s_wts = sem("s_wts")
        s3_mom = sem("s3_mom")
        s3_var = sem("s3_var")
        s3_rstd = sem("s3_rstd")
        s3_h = sem("s3_h")
        s3_turn = sem("s3_turn")
        s3_turned = sem("s3_turned")
        s3_y = sem("s3_y")
        s3_split = sem("s3_split")
        s3_chain = sem("s3_chain")
        loads = [(x_all[:], A["x"].rearrange("(t p) d -> p t d", p=P)),
                 (w_raw[:, 0], A["L0_gnn_Wl1"]), (w_raw[:, 1], A["L0_gnn_Wr1"]),
                 (w_raw[:, 2], A["L0_gnn_Wl2"]), (w_raw[:, 3], A["L0_gnn_Wr2"]),
                 (w_n[:], A["L1_gnn_Wn"]), (w_out[:], A["L1_gnn_Wout"]), (w_low[:], A["L2_gnn_weight_low"]),
                 (w_1[:], A["L3_gnn_W1"]), (w_2[:], A["L3_gnn_W2"]),
                 (bias[:, BL1], row(A["L0_gnn_bl1"])), (bias[:, BL2], row(A["L0_gnn_bl2"])),
                 (bias[:, BN], row(A["L1_gnn_bn"])), (bias[:, BOUT], row(A["L1_gnn_bout"])),
                 (bias[:, B1, 0:DH], row(A["L3_gnn_b1"])), (bias[:, B2], row(A["L3_gnn_b2"])),
                 (bn_col[:], column(A["L1_gnn_bn"]))]

        with nc.Block() as block:
            @block.sync
            def _(sp):
                for to, a in loads:
                    sp.dma_start(to, a).then_inc(s_load, 16)

            @block.gpsimd
            def _(pool):
                nc.gpsimd.memset(parts_a[:, :, 3 * D:PARTS], 1.0)
                nc.gpsimd.memset(parts_b[:, :, 3 * D:PARTS], 1.0)
                nc.gpsimd.memset(minus_half[:], -0.5).then_inc(s_half, 1)
                pool.wait_ge(s_half, 1)
                for i, u in tiles(pool):
                    rsqrt(pool, moments, s3_var, s3_rstd, i, u)

            @block.vector
            def _(dve):
                v = nc.vector
                dve.wait_ge(s_load, 16 * len(loads))
                dve.wait_ge(s_wt, 1)
                v.tensor_copy(w_sage[:], psA[:, 0, :].rearrange("p (k d) -> p k d", k=4)).then_inc(s_wts, 1)
                chain_ = Chain(dve, s3_chain, 5)

                def moments_of(i, u):
                    chain_.tile(i)
                    xi = x_all[:, ds(i, 1)].rearrange("p o d -> p (o d)")
                    normalise(v, chain_, xi, stats[:, u], moments[:, u], centered[:, u], s3_var).then_inc(s3_mom, 1)

                def outputs_of(i, u):
                    dve.wait_ge(s3_y, i + 1)
                    v.tensor_tensor(self_a[:, ds(i, 1)].rearrange("p o d -> p (o d)"), psY[0:P, u, D:2 * D], bias[:, BL1], ALU.add)
                    split_parts(v, chain_, parts_a, i, psY[0:P, u, 0:D], rest[:, u], D).then_inc(s3_split, 1)
                    chain_.end()

                for i, u in tiles(dve):
                    moments_of(i, u)
                    outputs_of(i, u)

            @block.scalar
            def _(act):
                act_sets(act)
                for i, u in tiles(act):
                    act.wait_ge(s3_mom, i + 1)
                    act.wait_ge(s3_rstd, i + 1)
                    nc.scalar.activation(w_nodes[:, u], centered[:, u], ACT.Relu, scale=moments[:, u, 3:4]).then_inc(s3_h, 1)
                    act.wait_ge(s3_turn, i + 1)
                    nc.scalar.copy(w_turned[:, u], psX[:, u, 0:P]).then_inc(s3_turned, 1)

            @block.tensor
            def _(pe):
                t = nc.tensor
                pe.wait_ge(s_load, 16 * len(loads))
                for k in range(4):
                    last = t.transpose(psA[:, 0, k * D:(k + 1) * D], w_raw[:, k], ident[:])
                last.then_inc(s_wt, 1)
                pe.wait_ge(s_wts, 1)
                for i, u in tiles(pe):
                    pe.wait_ge(s3_h, i + 1)
                    t.transpose(psX[:, u, 0:P], w_nodes[:, u], ident[0:P, 0:P]).then_inc(s3_turn, 1)
                    pe.wait_ge(s3_turned, i + 1)
                    t.matmul(psY[0:P, u, 0:2 * D], w_turned[:, u], w_sage[:, 0:2].rearrange("p k d -> p (k d)"),
                             start=True, stop=True).then_inc(s3_y, 1)

        def pipelined(eng, one, two):
            one(0, 0, 1)
            with eng.Fori(0, T // 2) as k:
                for u in (1, 0):
                    j = eng.snap(2 * k + (2 - u), min_val=1, max_val=T - 1)
                    i = eng.snap(2 * k + (1 - u), min_val=0, max_val=T - 2)
                    one(j, u, eng.snap(k + (2 - u), min_val=1, max_val=T // 2 + 1))
                    two(i, 1 - u)
            two(T - 1, 0)

        def flat(ap):
            return ap.rearrange("p o d -> p (o d)")

        def counts_of(i):
            return count_d[ds(i, 1)].rearrange("o p a d -> p (o a) d")

        def weights_of(i):
            return weight_d[:, :, ds(i, 1)].rearrange("a p o d -> p a (o d)")

        def convolution(name, source, tile, rhs, width, tails, dve_work, act_work, pool_work, psum):
            s_loaded = [sem(f"{name}_loaded_{u}") for u in range(2)]
            s_sum = sem(f"{name}_sum")
            s_sum_free = sem(f"{name}_sum_free")

            with nc.Block() as block:
                @block.sync
                def _(sp):
                    sp.sem_inc(s_sum, 2)
                    for i, u in tiles(sp):
                        sp.wait_ge(s_sum, i + 1)
                        alone(sp)
                        sp.dma_start(tile[:, u], source(i)).then_inc(s_loaded[u], 16)

                @block.tensor
                def _(pe):
                    def products(i, u, n):
                        pe.wait_ge(s_loaded[u], n * 16)
                        pe.wait_ge(s_sum_free, i + 1)
                        for a in range(T):
                            if a == T // 2 and not isinstance(i, int):
                                tails[0](pe, pe.snap(i - 1, min_val=0, max_val=T - 2), 1 - u)
                            last = nc.tensor.matmul(psum[0:P, u, 0:width], tile[:, u, a, :], rhs[:, a, 0:width],
                                                    start=a == 0, stop=a == T - 1)
                        last.then_inc(s_sum, 1)

                    def rest_of(i, u):
                        if isinstance(i, int):
                            tails[0](pe, i, u)
                        tails[1](pe, i, u)

                    pipelined(pe, products, rest_of)

                @block.vector
                def _(dve):
                    dve.sem_inc(s_sum_free, 2)
                    dve_work(dve, s_sum, s_sum_free)

                @block.scalar
                def _(act):
                    act_sets(act)
                    for i, u in tiles(act):
                        act_work(act, i, u, s_sum)

                @block.gpsimd
                def _(pool):
                    pool_work(pool)

        for layer in (1, 2):
            name = f"sage{layer}"
            parts, self_in = ((parts_a, self_a), (parts_b, self_b))[layer - 1]
            s_hi = sem(name + "_hi")
            s_var = sem(name + "_var")
            s_rstd = sem(name + "_rstd")
            s_mom = sem(name + "_mom")
            s_new = sem(name + "_new")
            s_turn = sem(name + "_turn")
            s_turned = sem(name + "_turned")
            s_y = sem(name + "_y")
            s_kept = sem(name + "_kept")
            s_fin = sem(name + "_fin")
            s_out = sem(name + "_out")

            def dve_work(dve, s_sum, s_sum_free, layer=layer, self_in=self_in, s_hi=s_hi, s_mom=s_mom, s_var=s_var, s_new=s_new, s_y=s_y,
                         s_kept=s_kept, s_fin=s_fin, s_out=s_out):
                v = nc.vector
                fin, outs = Chain(dve, s_fin, 6), Chain(dve, s_out, 3)

                def finish(i, u, n):
                    fin.tile(i)
                    dve.wait_ge(s_sum, i + 3)
                    dve.wait_ge(s_hi, i + 1)
                    if layer == 1:
                        fin.link(v.tensor_scalar(deg1[:, u, 0:1], psA[0:P, u, 3 * D:PARTS], 1.0, None, ALU.max))
                        fin.link(v.reciprocal(deg1[:, u, 1:2], deg1[:, u, 0:1]))
                        fin.link(v.tensor_scalar(inv_deg[:, ds(i, 1)], deg1[:, u, 1:2], 1.0, None, ALU.mult))
                        v.tensor_scalar(norm[:, ds(i, 1)], psA[0:P, u, 3 * D:PARTS], 1.0, None, ALU.add)
                    fin.link(v.tensor_tensor(agg[:, u], psA[0:P, u, D:2 * D], agg[:, u], ALU.add))
                    fin.link(v.tensor_tensor(agg[:, u], psA[0:P, u, 2 * D:3 * D], agg[:, u], ALU.add))
                    fin.link(v.scalar_tensor_tensor(agg[:, u], agg[:, u], inv_deg[:, ds(i, 1)], flat(self_in[:, ds(i, 1)]),
                                                    ALU.mult, ALU.add))
                    if layer == 1:
                        v.tensor_scalar(w_nodes[:, u], agg[:, u], 0.0, None, ALU.max).then_inc(s_new, 1)
                    else:
                        dve.wait_ge(s_kept, i + 1)
                        alone(dve)
                        fin.link(v.scalar_tensor_tensor(x_new[:, u], agg[:, u], 0.0, flat(x_all[:, ds(i, 1)]), ALU.max, ALU.add))
                        normalise(v, fin, x_new[:, u], stats[:, u], moments[:, u], centered[:, u], s_var).then_inc(s_mom, 1)
                    dve.sem_inc(s_sum_free, 1)
                    fin.end()

                def outputs(i, u):
                    outs.tile(i)
                    dve.wait_ge(s_y, i + 1)
                    if layer == 1:
                        v.tensor_tensor(flat(self_b[:, ds(i, 1)]), psY[0:P, u, D:2 * D], bias[:, BL2], ALU.add)
                        split_parts(v, outs, parts_b, i, psY[0:P, u, 0:D], rest[:, u], D)
                        outs.end()
                    else:
                        v.tensor_tensor(flat(h_att[:, ds(i, 1)]), psY[0:P, u, 0:D], bias[:, BN], ALU.add)
                        v.tensor_scalar(hT[:, ds(i, 1)].rearrange("p o d -> p (o d)"), psY[:, u, D:D + P], bn_col[:, 0:1], None, ALU.add)

                pipelined(dve, finish, outputs)

            def act_work(act, i, u, s_sum, layer=layer, s_hi=s_hi, s_mom=s_mom, s_rstd=s_rstd, s_new=s_new, s_turn=s_turn, s_turned=s_turned):
                act.wait_ge(s_sum, i + 3)
                nc.scalar.copy(agg[:, u], psA[0:P, u, 0:D]).then_inc(s_hi, 1)
                if layer == 2:
                    act.wait_ge(s_mom, i + 1)
                    act.wait_ge(s_rstd, i + 1)
                    nc.scalar.activation(w_nodes[:, u], centered[:, u], ACT.Relu, scale=moments[:, u, 3:4]).then_inc(s_new, 1)
                act.wait_ge(s_turn, i + 1)
                nc.scalar.copy(w_turned[:, u], psX[:, u, 0:P]).then_inc(s_turned, 1)

            def pool_work(pool, layer=layer, s_kept=s_kept, s_var=s_var, s_mom=s_mom, s_rstd=s_rstd):
                if layer == 2:
                    pool.sem_inc(s_kept, 2)
                    nc.gpsimd.tensor_tensor(norm[:], norm[:], minus_half[0:P, :], ALU.pow)
                    for i, u in tiles(pool):
                        rsqrt(pool, moments, s_var, s_rstd, i, u)
                        pool.wait_ge(s_mom, i + 1)
                        alone(pool)
                        nc.gpsimd.tensor_copy(flat(x_all[:, ds(i, 1)]), x_new[:, u]).then_inc(s_kept, 1)

            def tail_1(pe, i, u, s_new=s_new, s_turn=s_turn):
                pe.wait_ge(s_new, i + 1)
                nc.tensor.transpose(psX[:, u, 0:P], w_nodes[:, u], ident[0:P, 0:P]).then_inc(s_turn, 1)

            def tail_2(pe, i, u, layer=layer, s_turned=s_turned, s_y=s_y):
                pe.wait_ge(s_turned, i + 1)
                if layer == 1:
                    nc.tensor.matmul(psY[0:P, u, 0:2 * D], w_turned[:, u], w_sage[:, 2:4].rearrange("p k d -> p (k d)"),
                                     start=True, stop=True).then_inc(s_y, 1)
                else:
                    nc.tensor.matmul(psY[0:P, u, 0:D], w_turned[:, u], w_n[:], start=True, stop=True)
                    nc.tensor.matmul(psY[:, u, D:D + P], w_n[:], w_turned[:, u], start=True, stop=True,
                                     skip_group_check=True).then_inc(s_y, 1)

            convolution(name, counts_of, mat, parts, PARTS, (tail_1, tail_2), dve_work, act_work, pool_work, psA)
        sage.close()

        att = ExitStack()

        def asb(name, shape, dt=fp32):
            return att.enter_context(nc.sbuf_tensor(name, shape, dt))

        SCALE = float(D) ** -0.5
        NPC = len(PIECES)
        EVEN = [j for j in range(NPC) if j % 2 == 0]
        ODD = [j for j in range(NPC) if j % 2 == 1]
        EXP = [(0, 3), (3, 5), (5, NPC)]

        wl = asb("wl", [128, 4, D])
        rows_l = asb("rows_l", [P, 3, D])
        cols_l = asb("cols_l", [128, 3])
        bq_scaled = asb("bq_scaled", [128, 1])
        kT = asb("kT", [128, T, P])
        vT = asb("vT", [128, T, P])
        vo = asb("vo", [P, T, D])
        qT = asb("qT", [128, 2, P])
        probs = asb("probs", [P, 2, N])
        logm_in = asb("logm_in", [P, 2, N])
        probs_T = asb("probs_T", [P, 3, 4 * P])
        piece_max = asb("piece_max", [P, 2, NPC])
        neg_max = asb("neg_max", [P, 2, 2])
        row_sum = asb("row_sum", [P, 2, 4])
        inv_sum = asb("inv_sum", [P, 2, 2])
        y_att = asb("y_att", [P, 2, D])
        c_att = asb("c_att", [P, 2, D])
        h_new = asb("h_new", [P, 2, D])
        st_att = asb("st_att", [P, 2, 6])
        mo_att = asb("mo_att", [P, 2, 4])
        psS = att.enter_context(nc.psum_tensor("psS", [128, 3, 512], fp32))
        psR = att.enter_context(nc.psum_tensor("psR", [128, 2, 512], fp32))
        psO = att.enter_context(nc.psum_tensor("psO", [128, 512], fp32))
        psQ = att.enter_context(nc.psum_tensor("psQ", [128, 512], fp32))
        psH = att.enter_context(nc.psum_tensor("psH", [128, 512], fp32))

        a_w = sem("a_w")
        a_bq = sem("a_bq")
        a_kv = sem("a_kv")
        a_kv_out = sem("a_kv_out")
        a_vo = sem("a_vo")
        a_vo_out = sem("a_vo_out")
        a_q = sem("a_q")
        a_q_out = sem("a_q_out")
        a_logm = [sem(f"a_logm_{u}") for u in range(2)]
        a_logm_free = sem("a_logm_free")
        a_s = sem("a_s")
        a_s_out = sem("a_s_out")
        a_max = sem("a_max")
        a_exp = sem("a_exp")
        a_t = sem("a_t")
        a_t_dve = sem("a_t_dve")
        a_t_act = sem("a_t_act")
        a_pv = sem("a_pv")
        a_o = sem("a_o")
        a_var = sem("a_var")
        a_cen = sem("a_cen")
        a_h = sem("a_h")
        a_h_kept = sem("a_h_kept")
        a_hT = sem("a_hT")
        a_hT_out = sem("a_hT_out")
        a_mx_chain = sem("a_mx_chain")
        a_dve_chain = sem("a_dve_chain")
        a_pool_chain = sem("a_pool_chain")
        NLOADS = 10
        AHEAD = {"pe": (a_pv,), "dve": (a_s_out, a_t_dve, a_o), "act": (a_q_out, a_t_act, a_hT_out), "pool": (a_h_kept,)}

        def ahead(eng, name):
            for s in AHEAD[name]:
                eng.sem_inc(s, 1)

        def flat_t(ap):
            return ap.rearrange("p a d -> p (a d)")

        def steps(eng, l):
            def one(s):
                return s, eng.snap(l * T + s, min_val=s, max_val=(LAYERS - 1) * T + s), s % 2
            for s in (0, 1, 2):
                yield one(s)
            with eng.Fori(0, (T - 5) // 2) as k:
                for d in (3, 4):
                    s = eng.snap(2 * k + d, min_val=3, max_val=T - 3)
                    yield s, eng.snap(l * T + s, min_val=3, max_val=(LAYERS - 1) * T + T - 3), d % 2
            for s in range(T - 2, T + 3):
                yield one(s)

        def has(s, back):
            return True if not isinstance(s, int) else 0 <= s - back < T

        with nc.Block() as block:
            @block.sync
            def _(sp):
                with sp.Fori(0, LAYERS) as l:
                    sp.wait_ge(a_h_kept, l * T + 1)
                    alone(sp)
                    one = ds(l, 1)
                    for k, w in enumerate(("WQ", "WK", "WV", "WO")):
                        sp.dma_start(wl[:, k], A["L1_gnn_" + w][one].rearrange("o i j -> (o i) j")).then_inc(a_w, 16)
                    for k, w in enumerate(("bO", "ln_g", "ln_b")):
                        sp.dma_start(rows_l[:, k], A["L1_gnn_" + w][one].broadcast_to([P, D])).then_inc(a_w, 16)
                    for k, w in enumerate(("bQ", "bK", "bV")):
                        sp.dma_start(cols_l[:, k:k + 1], A["L1_gnn_" + w][one].rearrange("o d -> d o")).then_inc(a_w, 16)
                    for s, g, u in steps(sp, l):
                        if not has(s, 0):
                            continue
                        sp.wait_ge(a_logm_free, g + 2 if isinstance(s, int) and s == 0 else g + 1 if not isinstance(s, int) or s > 1 else g)
                        sp.dma_start(logm_in[:, u], logmask_d[ds(s, 1)].rearrange("o p n -> (o p) n")).then_inc(a_logm[u], 16)

            @block.tensor
            def _(pe):
                t = nc.tensor
                ahead(pe, "pe")

                def queries(s1, g1):
                    pe.wait_ge(a_q_out, g1 + 1)
                    alone(pe)
                    t.matmul(psQ[:, 0:P], wl[:, 0], flat(hT[:, ds(s1, 1)]), start=True, stop=True).then_inc(a_q, 1)

                def values(g, u, j):
                    a0, an = PIECES[j]
                    if j == 0:
                        pe.wait_ge(a_o, g + 1)
                    if j % 2 == 0:
                        pe.wait_ge(a_t_dve, g * len(EVEN) + j // 2 + 2)
                    else:
                        pe.wait_ge(a_t_act, g * len(ODD) + j // 2 + 2)
                    for a in range(an):
                        last = t.matmul(psO[0:P, 0:D], probs_T[:, j % 3, a * P:(a + 1) * P], vo[:, a0 + a],
                                        start=a0 + a == 0, stop=a0 + a == T - 1)
                    last.then_inc(a_pv, 1)

                with pe.Fori(0, LAYERS) as l:
                    pe.wait_ge(a_w, (l + 1) * (NLOADS * 16))
                    pe.wait_ge(a_hT_out, l * T + 1)
                    pe.wait_ge(a_s_out, l * (T * NPC) + 1)
                    n = 0
                    for j, (a0, an) in enumerate(PIECES):
                        for k in (1, 2):
                            if n >= 3:
                                pe.wait_ge(a_kv_out, l * (2 * NPC) + n - 2)
                            t.matmul(psS[:, n % 3, 0:an * P], wl[:, k], flat_t(hT[:, a0:a0 + an]),
                                     start=True, stop=True).then_inc(a_kv, 1)
                            n += 1
                    for j, (a0, an) in enumerate(PIECES):
                        pe.wait_ge(a_kv_out, l * (2 * NPC) + 2 * j + 2)
                        if j >= 2:
                            pe.wait_ge(a_vo_out, l * NPC + j - 1)
                        for a in range(an):
                            last = t.matmul(psR[0:P, j % 2, a * D:(a + 1) * D], vT[:, a0 + a], wl[:, 3],
                                            start=True, stop=True)
                        last.then_inc(a_vo, 1)
                    pe.wait_ge(a_kv_out, (l + 1) * (2 * NPC))
                    pe.wait_ge(a_vo_out, (l + 1) * NPC)
                    queries(0, l * T)
                    for s, g, u in steps(pe, l):
                        if has(s, -1):
                            queries(s + 1, g + 1)
                        gi = pe.snap(g - 2, min_val=0, max_val=LAYERS * T) if has(s, 2) else None
                        for j, (a0, an) in enumerate(PIECES):
                            if has(s, 0):
                                if j == 0:
                                    pe.wait_ge(a_q_out, g + 2)
                                if j >= 3:
                                    pe.wait_ge(a_s_out, g * NPC + j - 1)
                                elif not (isinstance(s, int) and s == 0):
                                    pe.wait_ge(a_s_out, g * NPC - (0, 2, 1)[j] + 1)
                                t.matmul(psS[0:P, j % 3, 0:an * P], qT[:, u], flat_t(kT[:, a0:a0 + an]),
                                         start=True, stop=True).then_inc(a_s, 1)
                            if has(s, 2):
                                if j == 0:
                                    pe.wait_ge(a_exp, gi + 1)
                                if j % 2 == 0:
                                    pe.wait_ge(a_t_dve, gi * len(EVEN) + j // 2 + 1)
                                else:
                                    pe.wait_ge(a_t_act, gi * len(ODD) + j // 2 + 1)
                                for a in range(an):
                                    last = t.transpose(psR[0:P, j % 2, a * P:(a + 1) * P],
                                                       probs[:, u, (a0 + a) * P:(a0 + a + 1) * P], ident[0:P, 0:P])
                                last.then_inc(a_t, 1)
                                if j >= 1:
                                    values(gi, u, j - 1)
                            if j == 3 and has(s, 3):
                                pe.wait_ge(a_h, g - 2)
                                pe.wait_ge(a_hT_out, g - 2)
                                t.transpose(psH[:, 0:P], h_new[:, 1 - u], ident[0:P, 0:P]).then_inc(a_hT, 1)
                        if has(s, 2):
                            values(gi, u, NPC - 1)

            @block.vector
            def _(dve):
                v = nc.vector
                mx, fin = Chain(dve, a_mx_chain, 1), Chain(dve, a_dve_chain, 6)
                dve.sem_inc(a_logm_free, 2)
                ahead(dve, "dve")
                with dve.Fori(0, LAYERS) as l:
                    dve.wait_ge(a_w, (l + 1) * (NLOADS * 16))
                    dve.wait_ge(a_q_out, l * T + 1)
                    v.tensor_scalar(bq_scaled[:], cols_l[:, 0:1], SCALE, None, ALU.mult).then_inc(a_bq, 1)
                    dve.wait_ge(a_h_kept, l * T + 1)
                    for j, (a0, an) in enumerate(PIECES):
                        dve.wait_ge(a_vo, l * NPC + j + 1)
                        v.tensor_copy(vo[:, a0:a0 + an].rearrange("p a d -> p (a d)"), psR[0:P, j % 2, 0:an * D]).then_inc(a_vo_out, 1)
                    for s, g, u in steps(dve, l):
                        if has(s, 0):
                            n = l * (T // 2 + 1 - u) + (s // 2 + 1)
                            dve.wait_ge(a_logm[u], n * 16)
                            alone(dve)
                        gi = dve.snap(g - 2, min_val=0, max_val=LAYERS * T) if has(s, 2) else None
                        for j, (a0, an) in enumerate(PIECES):
                            cols = slice(a0 * P, (a0 + an) * P)
                            if has(s, 0):
                                if has(s, 2):
                                    dve.wait_ge(a_t, gi * NPC + j + 1)
                                    alone(dve)
                                dve.wait_ge(a_s, g * NPC + j + 1)
                                alone(dve)
                                v.tensor_tensor_reduce(out=probs[:, u, cols], in0=psS[0:P, j % 3, 0:an * P], in1=logm_in[:, u, cols],
                                                       scale=1.0, scalar=-3.0e38, op0=ALU.add, op1=ALU.max,
                                                       accum_out=piece_max[:, u, j:j + 1]).then_inc(a_s_out, 1)
                            if has(s, 2) and j in EVEN:
                                dve.wait_ge(a_t, gi * NPC + j + 1)
                                dve.wait_ge(a_pv, gi * NPC + (j - 2 if j >= 3 else 0) + 1)
                                v.tensor_copy(probs_T[:, j % 3, 0:an * P], psR[0:P, j % 2, 0:an * P]).then_inc(a_t_dve, 1)
                        if has(s, 0):
                            mx.tile(g)
                            dve.wait_ge(a_s_out, g * NPC + NPC + 1)
                            mx.link(v.tensor_reduce(neg_max[:, u, 0:1], piece_max[:, u], AX.X, ALU.max, negate=True))
                            v.tensor_scalar(neg_max[:, u, 1:2], neg_max[:, u, 0:1], -MASKED / 10, None, ALU.min).then_inc(a_max, 1)
                            dve.sem_inc(a_logm_free, 1)
                        if has(s, 2):
                            i = s - 2
                            fin.tile(gi)
                            dve.wait_ge(a_exp, gi + 1)
                            fin.link(v.tensor_reduce(inv_sum[:, u, 0:1], row_sum[:, u, 0:len(EXP)], AX.X, ALU.add))
                            fin.link(v.tensor_scalar(inv_sum[:, u, 0:1], inv_sum[:, u, 0:1], 1e-30, None, ALU.max))
                            fin.link(v.reciprocal(inv_sum[:, u, 1:2], inv_sum[:, u, 0:1]))
                            dve.wait_ge(a_pv, gi * NPC + NPC + 1)
                            v.scalar_tensor_tensor(y_att[:, u], psO[0:P, 0:D], inv_sum[:, u, 1:2], flat(h_att[:, ds(i, 1)]),
                                                   ALU.mult, ALU.add).then_inc(a_o, 1)
                            dve.wait_ge(a_o, gi + 2)
                            fin.link(v.tensor_tensor(y_att[:, u], y_att[:, u], rows_l[:, 0], ALU.add))
                            normalise(v, fin, y_att[:, u], st_att[:, u], mo_att[:, u], c_att[:, u], a_var).then_inc(a_cen, 1)
                            fin.end()

            @block.scalar
            def _(act):
                act_sets(act)
                sc = nc.scalar
                ahead(act, "act")

                def queries_out(g1, u1):
                    act.wait_ge(a_q, g1 + 1)
                    sc.activation(qT[:, u1], psQ[:, 0:P], ACT.Identity, bias=bq_scaled[:], scale=SCALE).then_inc(a_q_out, 1)

                with act.Fori(0, LAYERS) as l:
                    act.wait_ge(a_bq, l + 1)
                    for j, (a0, an) in enumerate(PIECES):
                        for k, to in ((1, kT), (2, vT)):
                            act.wait_ge(a_kv, l * (2 * NPC) + 2 * j + k)
                            sc.activation(flat_t(to[:, a0:a0 + an]), psS[:, (2 * j + k - 1) % 3, 0:an * P], ACT.Identity,
                                          bias=cols_l[:, k:k + 1]).then_inc(a_kv_out, 1)
                    queries_out(l * T, 0)
                    for s, g, u in steps(act, l):
                        if has(s, -1):
                            if has(s, 1):
                                act.wait_ge(a_s, g * NPC)
                            queries_out(g + 1, 1 - u)
                        gi = act.snap(g - 2, min_val=0, max_val=LAYERS * T) if has(s, 2) else None

                        def exponentials(part):
                            p0, p1 = EXP[part]
                            cols = slice(PIECES[p0][0] * P, (PIECES[p1 - 1][0] + PIECES[p1 - 1][1]) * P)
                            ins = sc.activation(probs[:, 1 - u, cols], probs[:, 1 - u, cols], ACT.Exp,
                                                bias=neg_max[:, 1 - u, 1:2], accum_out=row_sum[:, 1 - u, part:part + 1])
                            if part == len(EXP) - 1:
                                ins.then_inc(a_exp, 1)

                        if has(s, 1):
                            if has(s, 3):
                                act.wait_ge(a_o, g - 1)
                            act.wait_ge(a_max, g)
                        for part in range(len(EXP)):
                            if has(s, 1):
                                exponentials(part)
                            j = 2 * part + 1
                            if has(s, 2):
                                act.wait_ge(a_t, gi * NPC + j + 1)
                                act.wait_ge(a_pv, gi * NPC + (j - 2 if j >= 3 else 0) + 1)
                                a0, an = PIECES[j]
                                sc.copy(probs_T[:, j % 3, 0:an * P], psR[0:P, j % 2, 0:an * P]).then_inc(a_t_act, 1)
                            if part == 1 and has(s, 3):
                                act.wait_ge(a_hT, g - 2)
                                alone(act)
                                sc.copy(flat(hT[:, ds(s - 3, 1)]), psH[:, 0:P]).then_inc(a_hT_out, 1)

            @block.gpsimd
            def _(pool):
                p = nc.gpsimd
                ahead(pool, "pool")
                link = Chain(pool, a_pool_chain, 3)
                with pool.Fori(0, LAYERS) as l:
                    for i, u in tiles(pool):
                        g = pool.snap(l * T + i, min_val=0, max_val=LAYERS * T)
                        link.tile(g)
                        pool.wait_ge(a_var, g + 1)
                        link.link(p.tensor_tensor(mo_att[:, u, 3:4], mo_att[:, u, 2:3], minus_half[0:P, 0:1], ALU.pow))
                        pool.wait_ge(a_cen, g + 1)
                        link.link(p.tensor_tensor(c_att[:, u], c_att[:, u], mo_att[:, u, 3:4].broadcast_to([P, D]), ALU.mult))
                        link.link(p.tensor_tensor(c_att[:, u], c_att[:, u], rows_l[:, 1], ALU.mult))
                        p.tensor_tensor(h_new[:, u], c_att[:, u], rows_l[:, 2], ALU.add).then_inc(a_h, 1)
                        pool.wait_ge(a_h, g + 1)
                        alone(pool)
                        p.tensor_copy(flat(h_att[:, ds(i, 1)]), h_new[:, u]).then_inc(a_h_kept, 1)
        att.close()

        late = ExitStack()

        def lsb(name, shape, dt=fp32):
            return late.enter_context(nc.sbuf_tensor(name, shape, dt))

        support = lsb("support", [P, T, D])
        parts_c = lsb("parts_c", [P, T, 3 * DH], bf16)
        parts_d = lsb("parts_d", [P, T, 3 * DH], bf16)
        self_c = lsb("self_c", [P, T, DH])
        self_d = lsb("self_d", [P, T, DH])
        l_nodes = lsb("l_nodes", [P, 2, D])
        l_turned = lsb("l_turned", [128, 2, P])
        l_turned2 = lsb("l_turned2", [128, 2, P])
        l_agg = lsb("l_agg", [P, 2, D])
        l_rest = lsb("l_rest", [P, 2, D])
        l_stats = lsb("l_stats", [P, 2, 6])
        l_moments = lsb("l_moments", [P, 2, 4])
        l_centered = lsb("l_centered", [P, 2, D])
        l_x = lsb("l_x", [P, 2, D])
        l_mat = lsb("l_mat", [P, 2, T, P])
        l_mat_bf = lsb("l_mat_bf", [P, 2, T, P], bf16)
        psE = late.enter_context(nc.psum_tensor("psE", [128, 2, 512], fp32))
        psF = late.enter_context(nc.psum_tensor("psF", [128, 2, 512], fp32))
        psG = late.enter_context(nc.psum_tensor("psG", [128, 2, 512], fp32))

        def keep_and_scale(pool, s_var, s_rstd, s_mom, s_kept):
            pool.sem_inc(s_kept, 2)
            for i, u in tiles(pool):
                rsqrt(pool, l_moments, s_var, s_rstd, i, u)
                pool.wait_ge(s_mom, i + 1)
                alone(pool)
                nc.gpsimd.tensor_copy(flat(x_all[:, ds(i, 1)]), l_x[:, u]).then_inc(s_kept, 1)

        o_copy = sem("o_copy")
        o_y = sem("o_y")
        o_var = sem("o_var")
        o_rstd = sem("o_rstd")
        o_mom = sem("o_mom")
        o_kept = sem("o_kept")
        o_new = sem("o_new")
        o_turn = sem("o_turn")
        o_turned = sem("o_turned")
        o_sup = sem("o_sup")
        o_chain = sem("o_chain")
        o_done = sem("o_done")

        with nc.Block() as block:
            @block.tensor
            def _(pe):
                def first(i, u, n):
                    pe.wait_ge(o_copy, i + 1)
                    nc.tensor.matmul(psE[0:P, u, 0:D], l_turned[:, u], w_out[:], start=True, stop=True).then_inc(o_y, 1)

                def second(i, u):
                    pe.wait_ge(o_new, i + 1)
                    nc.tensor.transpose(psF[:, u, 0:P], l_nodes[:, u], ident[0:P, 0:P]).then_inc(o_turn, 1)
                    pe.wait_ge(o_turned, i + 1)
                    nc.tensor.matmul(psG[0:P, u, 0:D], l_turned2[:, u], w_low[:], start=True, stop=True).then_inc(o_sup, 1)

                pipelined(pe, first, second)

            @block.vector
            def _(dve):
                v = nc.vector
                chain_ = Chain(dve, o_chain, 4)

                def first(i, u, n):
                    chain_.tile(i)
                    dve.wait_ge(o_kept, i + 1)
                    dve.wait_ge(o_y, i + 1)
                    chain_.link(v.tensor_tensor(l_x[:, u], psE[0:P, u, 0:D], bias[:, BOUT], ALU.add))
                    chain_.link(v.tensor_tensor(l_x[:, u], l_x[:, u], flat(x_all[:, ds(i, 1)]), ALU.add))
                    normalise(v, chain_, l_x[:, u], l_stats[:, u], l_moments[:, u], l_centered[:, u], o_var).then_inc(o_mom, 1)
                    chain_.end()

                def second(i, u):
                    dve.wait_ge(o_sup, i + 1)
                    alone(dve)
                    v.tensor_copy(flat(support[:, ds(i, 1)]), psG[0:P, u, 0:D]).then_inc(o_done, 1)

                pipelined(dve, first, second)

            @block.scalar
            def _(act):
                act_sets(act)

                def first(i, u, n):
                    nc.scalar.copy(l_turned[:, u], flat(hT[:, ds(i, 1)])).then_inc(o_copy, 1)

                def second(i, u):
                    act.wait_ge(o_rstd, i + 1)
                    act.wait_ge(o_mom, i + 1)
                    nc.scalar.activation(l_nodes[:, u], l_centered[:, u], ACT.Relu, scale=l_moments[:, u, 3:4]).then_inc(o_new, 1)
                    act.wait_ge(o_turn, i + 1)
                    nc.scalar.copy(l_turned2[:, u], psF[:, u, 0:P]).then_inc(o_turned, 1)

                pipelined(act, first, second)

            @block.gpsimd
            def _(pool):
                keep_and_scale(pool, o_var, o_rstd, o_mom, o_kept)

        def low_pass():
            s_var, s_rstd, s_mom, s_new = sem("low_var"), sem("low_rstd"), sem("low_mom"), sem("low_new")
            s_turn, s_turned, s_y = sem("low_turn"), sem("low_turned"), sem("low_y")
            s_fin, s_out, s_kept = sem("low_fin"), sem("low_out"), sem("low_kept")

            def dve_work(dve, s_sum, s_sum_free):
                v = nc.vector
                fin, outs = Chain(dve, s_fin, 3), Chain(dve, s_out, 4)

                def finish(i, u, n):
                    fin.tile(i)
                    dve.wait_ge(s_kept, i + 1)
                    dve.wait_ge(s_sum, i + 3)
                    fin.link(v.tensor_tensor(l_x[:, u], psE[0:P, u, 0:D], flat(x_all[:, ds(i, 1)]), ALU.add))
                    normalise(v, fin, l_x[:, u], l_stats[:, u], l_moments[:, u], l_centered[:, u], s_var).then_inc(s_mom, 1)
                    dve.sem_inc(s_sum_free, 1)
                    fin.end()

                def outputs(i, u):
                    outs.tile(i)
                    dve.wait_ge(s_y, i + 1)
                    scale = norm[:, ds(i, 1)]
                    outs.link(v.tensor_scalar(l_agg[:, u, 0:DH], psG[0:P, u, 0:DH], scale, scale, ALU.mult, ALU.mult))
                    v.tensor_tensor(flat(self_c[:, ds(i, 1)]), l_agg[:, u, 0:DH], bias[:, B1, 0:DH], ALU.add)
                    split_parts(v, outs, parts_c, i, psG[0:P, u, 0:DH], l_rest[:, u, 0:DH], DH, scale)
                    outs.end()

                pipelined(dve, finish, outputs)

            def act_work(act, i, u, s_sum):
                act.wait_ge(s_mom, i + 1)
                act.wait_ge(s_rstd, i + 1)
                nc.scalar.activation(l_nodes[:, u], l_centered[:, u], ACT.Relu, scale=l_moments[:, u, 3:4]).then_inc(s_new, 1)
                act.wait_ge(s_turn, i + 1)
                nc.scalar.copy(l_turned[:, u], psF[:, u, 0:P]).then_inc(s_turned, 1)

            def pool_work(pool):
                keep_and_scale(pool, s_var, s_rstd, s_mom, s_kept)

            def tail_1(pe, i, u):
                pe.wait_ge(s_new, i + 1)
                nc.tensor.transpose(psF[:, u, 0:P], l_nodes[:, u], ident[0:P, 0:P]).then_inc(s_turn, 1)

            def tail_2(pe, i, u):
                pe.wait_ge(s_turned, i + 1)
                nc.tensor.matmul(psG[0:P, u, 0:DH], l_turned[:, u], w_1[:], start=True, stop=True).then_inc(s_y, 1)

            convolution("low", weights_of, l_mat, support, D, (tail_1, tail_2), dve_work, act_work, pool_work, psE)

        low_pass()

        def sum_parts(v, chain_, i, u, own):
            chain_.link(v.tensor_tensor(l_agg[:, u, 0:DH], psE[0:P, u, DH:2 * DH], l_agg[:, u, 0:DH], ALU.add))
            chain_.link(v.tensor_tensor(l_agg[:, u, 0:DH], psE[0:P, u, 2 * DH:3 * DH], l_agg[:, u, 0:DH], ALU.add))
            return v.scalar_tensor_tensor(l_nodes[:, u, 0:DH], l_agg[:, u, 0:DH], norm[:, ds(i, 1)], flat(own[:, ds(i, 1)]),
                                          ALU.mult, ALU.add)

        def gcn_first():
            s_hi, s_fin = sem("gcn1_hi"), sem("gcn1_fin")

            def dve_work(dve, s_sum, s_sum_free):
                v = nc.vector
                fin = Chain(dve, s_fin, 7)
                for i, u in tiles(dve):
                    fin.tile(i)
                    dve.wait_ge(s_sum, i + 3)
                    dve.wait_ge(s_hi, i + 1)
                    fin.link(sum_parts(v, fin, i, u, self_c))
                    dve.sem_inc(s_sum_free, 1)
                    fin.link(v.tensor_scalar(l_x[:, u, 0:DH], l_nodes[:, u, 0:DH], 0.0, norm[:, ds(i, 1)], ALU.max, ALU.mult))
                    v.tensor_scalar(flat(self_d[:, ds(i, 1)]), l_x[:, u, 0:DH], norm[:, ds(i, 1)], None, ALU.mult)
                    split_parts(v, fin, parts_d, i, l_x[:, u, 0:DH], l_rest[:, u, 0:DH], DH)
                    fin.end()

            def act_work(act, i, u, s_sum):
                act.wait_ge(s_sum, i + 3)
                nc.scalar.copy(l_agg[:, u, 0:DH], psE[0:P, u, 0:DH]).then_inc(s_hi, 1)

            nothing = lambda pe, i, u: None
            convolution("gcn1", counts_of, l_mat_bf, parts_c, 3 * DH, (nothing, nothing), dve_work, act_work, lambda pool: None, psE)

        def gcn_second():
            s_hi, s_fin, s_new, s_turn = sem("gcn2_hi"), sem("gcn2_fin"), sem("gcn2_new"), sem("gcn2_turn")
            s_turned, s_y, s_out = sem("gcn2_turned"), sem("gcn2_y"), sem("gcn2_out")

            def dve_work(dve, s_sum, s_sum_free):
                v = nc.vector
                fin, outs = Chain(dve, s_fin, 2), Chain(dve, s_out, 1)

                def finish(i, u, n):
                    fin.tile(i)
                    dve.wait_ge(s_sum, i + 3)
                    dve.wait_ge(s_hi, i + 1)
                    sum_parts(v, fin, i, u, self_d).then_inc(s_new, 1)
                    dve.sem_inc(s_sum_free, 1)
                    fin.end()

                def outputs(i, u):
                    outs.tile(i)
                    dve.wait_ge(s_y, i + 1)
                    xi = flat(x_all[:, ds(i, 1)])
                    outs.link(v.tensor_tensor(l_x[:, u], psG[0:P, u, 0:D], bias[:, B2], ALU.add))
                    v.tensor_tensor(xi, l_x[:, u], xi, ALU.add)

                pipelined(dve, finish, outputs)

            def act_work(act, i, u, s_sum):
                act.wait_ge(s_sum, i + 3)
                nc.scalar.copy(l_agg[:, u, 0:DH], psE[0:P, u, 0:DH]).then_inc(s_hi, 1)
                act.wait_ge(s_turn, i + 1)
                nc.scalar.copy(l_turned[0:DH, u], psF[0:DH, u, 0:P]).then_inc(s_turned, 1)

            def tail_1(pe, i, u):
                pe.wait_ge(s_new, i + 1)
                alone(pe)
                nc.tensor.transpose(psF[0:DH, u, 0:P], l_nodes[:, u, 0:DH], ident[0:P, 0:P]).then_inc(s_turn, 1)

            def tail_2(pe, i, u):
                pe.wait_ge(s_turned, i + 1)
                nc.tensor.matmul(psG[0:P, u, 0:D], l_turned[0:DH, u], w_2[:], start=True, stop=True).then_inc(s_y, 1)

            convolution("gcn2", counts_of, l_mat_bf, parts_d, 3 * DH, (tail_1, tail_2), dve_work, act_work, lambda pool: None, psE)

        gcn_first()
        gcn_second()

        s_stored = sem("s_stored")
        with nc.Block() as block:
            @block.sync
            def _(sp):
                sp.dma_start(out.rearrange("(t p) d -> p t d", p=P), x_all[:]).then_inc(s_stored, 16)
                sp.wait_ge(s_stored, 16)

        late.close()


_INS = ["x", "src", "dst", "edge_weight", "L0_gnn_Wl1", "L0_gnn_bl1", "L0_gnn_Wr1", "L0_gnn_Wl2", "L0_gnn_bl2", "L0_gnn_Wr2",
        "L1_gnn_Wn", "L1_gnn_bn", "L1_gnn_WQ", "L1_gnn_bQ", "L1_gnn_WK", "L1_gnn_bK", "L1_gnn_WV", "L1_gnn_bV",
        "L1_gnn_WO", "L1_gnn_bO", "L1_gnn_ln_g", "L1_gnn_ln_b", "L1_gnn_Wout", "L1_gnn_bout", "L2_gnn_weight_low",
        "L3_gnn_W1", "L3_gnn_b1", "L3_gnn_W2", "L3_gnn_b2"]


def kernel(**inputs):
    import numpy as np
    import concourse.bacc as bacc
    from concourse.bass_utils import run_bass_kernel_spmd

    nc = bacc.Bacc("TRN2", target_bir_lowering=False, num_devices=1)
    arrays, A = {}, {}
    for name in _INS:
        a = np.ascontiguousarray(inputs[name])
        arrays[f"in_{name}"] = a
        A[name] = nc.dram_tensor(f"in_{name}", a.shape, mybir.dt.from_np(a.dtype), kind="ExternalInput").ap()
    scratch = {
        "count": nc.dram_tensor("count", (T, P, T, P), mybir.dt.bfloat16).ap(),
        "weight": nc.dram_tensor("weight", (T, P, T, P), mybir.dt.float32).ap(),
        "logmask": nc.dram_tensor("logmask", (T, P, N), mybir.dt.float32).ap(),
    }
    out = nc.dram_tensor("out", (N, D), mybir.dt.float32, kind="ExternalOutput").ap()
    gnn_program(nc, A, out, scratch)
    r = run_bass_kernel_spmd(nc, [arrays], core_ids=[0])
    return r.results[0]["out"]
```

```python
import concourse.bass as bass
from concourse import mybir
from contextlib import ExitStack

N = 3125
E = 100000
D = 128
DH = 64
LAYERS = 4
P = 125
T = N // P
CE = 128
NG = -(-E // (CE * 128))
CH = -(-E // CE)
CP = NG * 128
W = 5
WT = P // W
NW = N // W
WC = T * W
WG = NW // P
BLOCK = 32
NB = E // BLOCK
PB = 125
GB = NB // PB
SLOTS = 2
SPAN = SLOTS * 128 // BLOCK
EXTRA = SPAN * BLOCK
KEY = 128
BW = 5
BT = WT // BW
AHEAD = 2
RING = 4
PT = 4
PIECES = [(4 * j, min(4, T - 4 * j)) for j in range(-(-T // 4))]
MASKED = -1.0e30
ROUND = 12582912.0


def chain(eng, sem):
    count = [0]

    def link(ins):
        count[0] += 1
        ins.then_inc(sem, 1)
        eng.wait_ge(sem, count[0])

    return link


def gnn_program(nc, A, out, taps):
    fp32, bf16, i32 = mybir.dt.float32, mybir.dt.bfloat16, mybir.dt.int32
    ALU, ACT, AX = mybir.AluOpType, mybir.ActivationFunctionType, mybir.AxisListType
    ds = bass.ds

    count_d, weight_d, logmask_d = taps["count"], taps["weight"], taps["logmask"]

    outer = ExitStack()

    def act_sets(act):
        nc.scalar.preload_act_table_set("natural_log_exp_and_others")

    with outer:
        def osb(name, shape, dt):
            return outer.enter_context(nc.sbuf_tensor(name, shape, dt))

        stage_sems = []

        def sem(name):
            handle = nc.alloc_semaphore(name=name)
            stage_sems.append(handle)
            return handle

        def done_with_semaphores():
            nc.clear_and_free_semaphores(list(stage_sems))
            stage_sems.clear()
            nc.all_engine_barrier()

        s_passed = outer.enter_context(nc.semaphore("s_passed"))

        def alone(eng):
            eng.sem_inc(s_passed, 1)

        ident = osb("ident", [128, 128], fp32)


        is_fast = osb("is_fast", [1, 1], i32)

        def path(eng, fast):
            flag = eng.value_load(is_fast[0:1, 0:1], min_val=0, max_val=1)
            return eng.If(flag == fast)

        fast_st = ExitStack()

        def fsb(name, shape, dt=fp32):
            return fast_st.enter_context(nc.sbuf_tensor(name, shape, dt))

        iota_p = fsb("iota_p", [128, P], bf16)
        slot_f = fsb("slot_f", [128, 3, SLOTS * (NW + AHEAD * BW)])
        F_SRC, F_KEY, F_W = range(3)

        blocks_st = ExitStack()

        def ksb(name, shape, dt=fp32):
            return blocks_st.enter_context(nc.sbuf_tensor(name, shape, dt))

        ROW = GB * BLOCK
        LONG = ROW + EXTRA
        k_src = ksb("k_src", [PB, LONG], i32)
        k_dst = ksb("k_dst", [PB, LONG], i32)
        k_w = ksb("k_w", [PB, LONG])
        k_srcf = ksb("k_srcf", [PB, LONG])
        k_dstf = ksb("k_dstf", [PB, LONG])
        k_tile = ksb("k_tile", [PB, LONG])
        k_win = ksb("k_win", [PB, LONG])
        k_eight = ksb("k_eight", [PB, LONG])
        k_rest = ksb("k_rest", [PB, LONG])
        pieces = ksb("pieces", [PB, 7, LONG], bf16)
        PARTS_OF = {F_SRC: (0,), F_KEY: (1, 2, 3), F_W: (4, 5, 6)}
        win_lo = ksb("win_lo", [PB, GB + SPAN])
        win_hi = ksb("win_hi", [PB, GB])
        block_no = ksb("block_no", [128, GB])
        iota_w = ksb("iota_w", [128, NW])
        key_base = ksb("key_base", [128, NW])
        picks = ksb("picks", [PB, GB, NW], bf16)
        ones_k = ksb("ones_k", [PB, 128], bf16)
        ones_f = ksb("ones_f", [PB, 1])
        first_block = ksb("first_block", [PB, NW])
        bad = ksb("bad", [PB, 2, GB])
        bad_sum = ksb("bad_sum", [PB, 1])
        psK = blocks_st.enter_context(nc.psum_tensor("psK", [128, 2, 2, 512], fp32))
        psB = blocks_st.enter_context(nc.psum_tensor("psB", [128, 3, 512], fp32))

        k_pad = sem("k_pad")
        k_edges = sem("k_edges")
        k_const = sem("k_const")
        k_cmp = sem("k_cmp")
        k_count = sem("k_count")
        k_flag = sem("k_flag")
        k_bad = sem("k_bad")
        k_pieces = sem("k_pieces")
        k_picks = sem("k_picks")
        k_out = sem("k_out")
        k_taken = sem("k_taken")
        k_dve = sem("k_dve")
        HALVES = ((0, 325), (325, NW - 325))
        FIELDS = [(f, s) for s in range(SLOTS) for f in (F_SRC, F_KEY, F_W)]

        with nc.Block() as block:
            @block.sync
            def _(sp):
                sp.wait_ge(k_pad, 1)
                for tile, a in ((k_dst, A["dst"]), (k_src, A["src"]), (k_w, A["edge_weight"])):
                    sp.dma_start(tile[:, 0:ROW], a.rearrange("(p r) -> p r", p=PB)).then_inc(k_edges, 16)
                    sp.dma_start(tile[0:PB - 1, ROW:LONG], a[ROW:E].rearrange("(p r) -> p r", p=PB - 1)[:, 0:EXTRA]).then_inc(k_edges, 16)

            @block.gpsimd
            def _(pool):
                g = nc.gpsimd
                g.iota(iota_w[:], [[1, NW]], base=0, channel_multiplier=0, allow_small_or_imprecise_dtypes=True)
                g.iota(key_base[:], [[KEY, NW]], base=0, channel_multiplier=0, allow_small_or_imprecise_dtypes=True)
                g.iota(block_no[:], [[1, GB]], base=0, channel_multiplier=GB, allow_small_or_imprecise_dtypes=True)
                g.iota(iota_p[:], [[1, P]], base=0, channel_multiplier=0, allow_small_or_imprecise_dtypes=True)
                g.memset(ones_f[:], 1.0)
                g.memset(ones_k[:], 1.0)
                g.memset(ident[:], 0.0).then_inc(k_const, 1)
                pool.wait_ge(k_const, 1)
                g.affine_select(out=ident[:], in_=ident[:], compare_op=ALU.not_equal, fill=1.0, base=0,
                                pattern=[[-1, 128]], channel_multiplier=1).then_inc(k_const, 1)

            @block.vector
            def _(dve):
                link = chain(dve, k_dve)
                v = nc.vector
                v.memset(slot_f[:, :, SLOTS * NW:], -1.0)
                v.memset(k_dst[:, ROW:LONG], N)
                v.memset(k_src[:, ROW:LONG], 0)
                v.memset(k_w[:, ROW:LONG], 0.0).then_inc(k_pad, 1)
                dve.wait_ge(k_edges, 6 * 16)
                v.tensor_copy(k_srcf[:], k_src[:])
                link(v.tensor_copy(k_dstf[:], k_dst[:]))
                v.tensor_scalar(k_tile[:], k_srcf[:], (P - 1) / 2, 1.0 / P, ALU.subtract, ALU.mult)
                link(v.tensor_scalar(k_win[:], k_dstf[:], (W - 1) / 2, 1.0 / W, ALU.subtract, ALU.mult))
                v.tensor_scalar(k_tile[:], k_tile[:], ROUND, ROUND, ALU.add, ALU.subtract)
                link(v.tensor_scalar(k_win[:], k_win[:], ROUND, ROUND, ALU.add, ALU.subtract))
                v.tensor_reduce(win_lo[:], k_win[:].rearrange("p (g e) -> p g e", e=BLOCK), AX.X, ALU.min)
                link(v.tensor_reduce(win_hi[:], k_win[:, 0:ROW].rearrange("p (g e) -> p g e", e=BLOCK), AX.X, ALU.max))
                v.tensor_tensor(bad[:, 0], win_lo[:, 1:GB + 1], win_hi[:], ALU.is_lt)
                link(v.tensor_tensor(bad[:, 1], win_lo[:, SPAN:SPAN + GB], win_hi[:], ALU.is_le))
                v.tensor_reduce(bad_sum[:], bad[:].rearrange("p b g -> p (b g)"), AX.X, ALU.max).then_inc(k_bad, 1)
                dve.wait_ge(k_const, 2)
                for g in range(GB):
                    v.tensor_scalar(picks[:, g], iota_w[0:PB], win_hi[:, g:g + 1], None, ALU.is_gt).then_inc(k_cmp, 1)
                v.scalar_tensor_tensor(pieces[:, 0], k_tile[:], -float(P), k_srcf[:], ALU.mult, ALU.add)
                v.tensor_scalar(k_eight[:], k_win[:], 3.5, 0.125, ALU.subtract, ALU.mult)
                link(v.scalar_tensor_tensor(k_rest[:], k_tile[:], float(W), k_dstf[:], ALU.mult, ALU.add))
                v.scalar_tensor_tensor(pieces[:, 1], k_win[:], -float(W), k_rest[:], ALU.mult, ALU.add)
                link(v.tensor_scalar(k_eight[:], k_eight[:], ROUND, ROUND, ALU.add, ALU.subtract))
                v.tensor_scalar(pieces[:, 2], k_eight[:], 8.0 * KEY, None, ALU.mult)
                link(v.scalar_tensor_tensor(k_eight[:], k_eight[:], -8.0, k_win[:], ALU.mult, ALU.add))
                v.tensor_scalar(pieces[:, 3], k_eight[:], float(KEY), None, ALU.mult)
                link(v.tensor_copy(pieces[:, 4], k_w[:]))
                link(v.tensor_tensor(k_rest[:], k_w[:], pieces[:, 4], ALU.subtract))
                link(v.tensor_copy(pieces[:, 5], k_rest[:]))
                v.tensor_tensor(pieces[:, 6], k_rest[:], pieces[:, 5], ALU.subtract).then_inc(k_pieces, 1)
                dve.wait_ge(k_flag, 1)
                v.tensor_scalar(is_fast[:], psB[0:1, 2, 0:1], 0.0, None, ALU.is_equal)
                dve.wait_ge(k_count, 1)
                for h, (w0, wn) in enumerate(HALVES):
                    last = v.tensor_copy(first_block[:, w0:w0 + wn], psB[0:PB, h, 0:wn])
                link(last)
                for g in range(GB):
                    v.tensor_scalar(picks[:, g], first_block[:], block_no[0:PB, g:g + 1], None, ALU.is_equal).then_inc(k_picks, 1)
                for n, (f, s) in enumerate(FIELDS):
                    dve.wait_ge(k_out, n + 1)
                    for h, (w0, wn) in enumerate(HALVES):
                        to = slot_f[:, f, 0:SLOTS * NW].rearrange("p (w s) -> p w s", s=SLOTS)[:, w0:w0 + wn, s]
                        if f == F_KEY:
                            last = v.tensor_tensor(to, psK[:, n % 2, h, 0:wn], key_base[:, w0:w0 + wn], ALU.subtract)
                        else:
                            last = v.tensor_copy(to, psK[:, n % 2, h, 0:wn])
                    last.then_inc(k_taken, 1)

            @block.tensor
            def _(pe):
                t = nc.tensor
                pe.wait_ge(k_const, 2)
                pe.wait_ge(k_bad, 1)
                t.matmul(psB[0:1, 2, 0:1], bad_sum[:], ones_f[:], start=True, stop=True).then_inc(k_flag, 1)
                for g in range(GB):
                    pe.wait_ge(k_cmp, g + 1)
                    for h, (w0, wn) in enumerate(HALVES):
                        last = t.matmul(psB[:, h, 0:wn], ones_k[:], picks[:, g, w0:w0 + wn], start=g == 0, stop=g == GB - 1)
                last.then_inc(k_count, 1)
                pe.wait_ge(k_pieces, 1)
                for n, (f, s) in enumerate(FIELDS):
                    if n >= 2:
                        pe.wait_ge(k_taken, n - 1)
                    for g in range(GB):
                        pe.wait_ge(k_picks, g + 1)
                        for k in PARTS_OF[f]:
                            e0 = g * BLOCK + s * 128
                            for h, (w0, wn) in enumerate(HALVES):
                                last = t.matmul(psK[:, n % 2, h, 0:wn], pieces[:, k, e0:e0 + 128], picks[:, g, w0:w0 + wn],
                                                start=g == 0 and k == PARTS_OF[f][0], stop=g == GB - 1 and k == PARTS_OF[f][-1])
                    last.then_inc(k_out, 1)

        blocks_st.close()

        dense = ExitStack()

        def dsb(name, shape, dt=fp32):
            return dense.enter_context(nc.sbuf_tensor(name, shape, dt))

        SB = BW * SLOTS
        src_hot = dsb("src_hot", [128, BT, SB, P], bf16)
        src_w = dsb("src_w", [128, BT, SB, P])
        col_hot = dsb("col_hot", [128, BT, SB, P], bf16)
        col_f = dsb("col_f", [128, BT, SB, P])
        sums = dsb("sums", [P, 2, 2, T, P])
        f_count = dsb("f_count", [P, T, P], bf16)
        f_weight = dsb("f_weight", [P, T, P])
        f_log = dsb("f_log", [P, N])
        f_none = dsb("f_none", [P, N])
        f_logm = dsb("f_logm", [P, N])
        tiny = dsb("tiny", [P, 1])
        psN = dense.enter_context(nc.psum_tensor("psN", [128, 2, 3, 512], fp32))
        psV = dense.enter_context(nc.psum_tensor("psV", [128, 2, 512], fp32))

        f_hot = sem("f_hot")
        f_srcw = sem("f_srcw")
        f_colf = sem("f_colf")
        f_used = sem("f_used")
        f_sums = sem("f_sums")
        f_piece = sem("f_piece")
        f_mask = sem("f_mask")
        f_piece_out = sem("f_piece_out")
        f_cast = sem("f_cast")
        f_masked = sem("f_masked")
        f_tiny = sem("f_tiny")
        f_stored = [sem(f"f_stored_{k}") for k in range(3)]
        NPC2 = 2 * len(PIECES)
        PER = -(-NPC2 // BT)

        def dense_tiles(eng):
            yield 0, 0, True, False
            with eng.Fori(0, T // 2) as k:
                yield eng.snap(2 * k + 1, min_val=1, max_val=T - 2), 1, True, True
                yield eng.snap(2 * k + 2, min_val=2, max_val=T - 1), 0, True, True
            yield T, T % 2, False, True

        with nc.Block() as block:
            @block.vector
            def _(dve):
                v = nc.vector
                with path(dve, 1):
                    v.memset(tiny[:], 1e-18).then_inc(f_tiny, 1)
                    dve.sem_inc(f_cast, 1)

                    def hot(b, r, to, f):
                        return v.tensor_tensor(
                            to[:, r], iota_p[:].rearrange("p (o c) -> p o c", o=1).broadcast_to([128, SB, P]),
                            slot_f[:, f, ds(b * SB, SB)].rearrange("p (k o) -> p k o", o=1).broadcast_to([128, SB, P]), ALU.is_equal)

                    for b in range(AHEAD):
                        hot(b, b, src_hot, F_SRC)
                        hot(b, b, col_hot, F_KEY).then_inc(f_hot, 1)
                    for i, u, now, before in dense_tiles(dve):
                        for j in range(BT):
                            def mask(n):
                                q = PER * j + n
                                if before and q < len(PIECES):
                                    a0, an = PIECES[q]
                                    dve.wait_ge(f_piece, (i - 1) * NPC2 + q + 1)
                                    v.tensor_scalar(f_none[:, a0 * P:(a0 + an) * P], psV[0:P, q % 2, 0:an * P], 0.0, MASKED,
                                                    ALU.is_equal, ALU.mult).then_inc(f_mask, 1)

                            if before and j == 0:
                                dve.wait_ge(f_masked, i)
                                alone(dve)
                            mask(0)
                            if now:
                                b = i * BT + (j + AHEAD)
                                dve.wait_ge(f_used, b + 1)
                                alone(dve)
                                hot(b, (j + AHEAD) % BT, src_hot, F_SRC)
                            mask(1)
                            if now:
                                hot(b, (j + AHEAD) % BT, col_hot, F_KEY).then_inc(f_hot, 1)
                            mask(2)
                            if before and j == BT - 2:
                                dve.wait_ge(f_stored[0], i * 16)
                                alone(dve)
                                v.tensor_copy(f_count[:], sums[:, 1 - u, 0]).then_inc(f_cast, 1)

            @block.gpsimd
            def _(pool):
                g = nc.gpsimd
                with path(pool, 1):
                    pool.sem_inc(f_masked, 1)

                    def weighted(b, r):
                        pool.wait_ge(f_hot, b + 1)
                        alone(pool)
                        g.tensor_tensor(src_w[:, r], src_hot[:, r],
                                        slot_f[:, F_W, ds(b * SB, SB)].rearrange("p (k o) -> p k o", o=1).broadcast_to([128, SB, P]),
                                        ALU.mult).then_inc(f_srcw, 1)

                    for b in range(AHEAD):
                        weighted(b, b)
                    for i, u, now, before in dense_tiles(pool):
                        for j in range(BT):
                            if now:
                                weighted(i * BT + (j + AHEAD), (j + AHEAD) % BT)
                            if before and j == (len(PIECES) - 1) // PER + 1:
                                pool.wait_ge(f_piece_out, (i - 1) * NPC2 + (len(PIECES) + 2))
                                alone(pool)
                                pool.wait_ge(f_stored[1], i * 16)
                                alone(pool)
                                g.tensor_tensor(f_logm[:], f_log[:], f_none[:], ALU.add).then_inc(f_masked, 1)

            @block.scalar
            def _(act):
                s = nc.scalar
                act_sets(act)
                with path(act, 1):
                    act.sem_inc(f_sums, 2)
                    act.sem_inc(f_piece_out, 2)
                    act.wait_ge(f_tiny, 1)

                    def columns(b, r):
                        act.wait_ge(f_hot, b + 1)
                        s.copy(col_f[:, r], col_hot[:, r]).then_inc(f_colf, 1)

                    def take_sums(i, u, j, k):
                        h = (BT * u + j) % 2
                        d0 = j * BW * W
                        if k == 0:
                            act.wait_ge(f_used, i * BT + (j + 1 + BT))
                        if k < 2:
                            s.copy(sums[:, u, k, :, d0:d0 + 4 * W].rearrange("p a (w d) -> p w a d", w=4),
                                   psN[0:P, h, k, 0:4 * WC].rearrange("p (w a d) -> p w a d", w=4, a=T))
                        else:
                            s.copy(sums[:, u, :, :, d0 + 4 * W:d0 + 5 * W],
                                   psN[0:P, h, 2, 0:2 * WC].rearrange("p (k a d) -> p k a d", k=2, a=T)).then_inc(f_sums, 1)

                    for b in range(AHEAD):
                        columns(b, b)
                    for i, u, now, before in dense_tiles(act):
                        for j in range(BT):
                            def piece(n):
                                q = PER * j + n
                                if before and q < NPC2:
                                    a0, an = PIECES[q % len(PIECES)]
                                    if q < len(PIECES):
                                        act.wait_ge(f_mask, (i - 1) * len(PIECES) + q + 1)
                                        ins = s.activation(f_log[:, a0 * P:(a0 + an) * P], psV[0:P, q % 2, 0:an * P], ACT.Ln, bias=tiny[:])
                                    else:
                                        if q == len(PIECES):
                                            act.wait_ge(f_stored[2], i * 16)
                                            alone(act)
                                        act.wait_ge(f_piece, (i - 1) * NPC2 + q + 1)
                                        ins = s.copy(f_weight[:, a0:a0 + an].rearrange("p a d -> p (a d)"), psV[0:P, q % 2, 0:an * P])
                                    ins.then_inc(f_piece_out, 1)

                            if j == 0 and before:
                                for k in range(3):
                                    take_sums(i - 1, 1 - u, BT - 1, k)
                                act.wait_ge(f_masked, i)
                                alone(act)
                                act.wait_ge(f_cast, i)
                                alone(act)
                            piece(0)
                            if now:
                                columns(i * BT + (j + AHEAD), (j + AHEAD) % BT)
                            piece(1)
                            if now and j >= 1:
                                for k in range(3):
                                    take_sums(i, u, j - 1, k)
                            piece(2)

            @block.tensor
            def _(pe):
                t_ = nc.tensor
                with path(pe, 1):
                    pe.sem_inc(f_used, BT)
                    for i, u, now, before in dense_tiles(pe):
                        for j in range(BT):
                            h = (BT * u + j) % 2

                            def piece(n):
                                q = PER * j + n
                                if before and q < NPC2:
                                    a0, an = PIECES[q % len(PIECES)]
                                    if q == 0:
                                        pe.wait_ge(f_sums, i * BT + 2)
                                        alone(pe)
                                    pe.wait_ge(f_piece_out, (i - 1) * NPC2 + q + 1)
                                    for a in range(an):
                                        last = t_.transpose(psV[0:P, q % 2, a * P:(a + 1) * P],
                                                            sums[:, 1 - u, q // len(PIECES), a0 + a], ident[0:P, 0:P])
                                    last.then_inc(f_piece, 1)

                            def products(w, k, rows, cols):
                                to = psN[0:P, h, k, w * WC:(w + 1) * WC] if w < 4 else psN[0:P, h, 2, k * WC:(k + 1) * WC]
                                for s in range(SLOTS):
                                    x = w * SLOTS + s
                                    last = t_.matmul(to, rows[:, j, x], cols[:, j, x], start=s == 0, stop=s == SLOTS - 1)
                                return last

                            if now:
                                pe.wait_ge(f_sums, i * BT + j + 1)
                                pe.wait_ge(f_colf, i * BT + j + 1)
                                for w in range(BW):
                                    products(w, 0, src_hot, col_hot)
                                pe.wait_ge(f_srcw, i * BT + j + 1)
                                products(0, 1, src_w, col_f)
                            piece(0)
                            if now:
                                for w in (1, 2):
                                    products(w, 1, src_w, col_f)
                            piece(1)
                            if now:
                                for w in (3, 4):
                                    last = products(w, 1, src_w, col_f)
                                last.then_inc(f_used, 1)
                            piece(2)

            @block.sync
            def _(sp):
                with path(sp, 1):
                    for s in f_stored:
                        sp.sem_inc(s, 16)
                    with sp.Fori(0, T) as t:
                        to = [x[ds(t, 1)].rearrange("o p a d -> (o p) (a d)") for x in (count_d, weight_d)]
                        sp.wait_ge(f_cast, t + 2)
                        alone(sp)
                        sp.dma_start(to[0], f_count[:].rearrange("p a d -> p (a d)")).then_inc(f_stored[0], 16)
                        sp.wait_ge(f_masked, t + 2)
                        alone(sp)
                        sp.dma_start(logmask_d[ds(t, 1)].rearrange("o p n -> (o p) n"), f_logm[:]).then_inc(f_stored[1], 16)
                        sp.wait_ge(f_piece_out, t * NPC2 + (NPC2 + 2))
                        alone(sp)
                        sp.dma_start(to[1], f_weight[:].rearrange("p a d -> p (a d)")).then_inc(f_stored[2], 16)
                    for s in f_stored:
                        sp.wait_ge(s, (T + 1) * 16)

        dense.close()
        fast_st.close()
        edges_st = ExitStack()

        def esb(name, shape, dt):
            return edges_st.enter_context(nc.sbuf_tensor(name, shape, dt))

        iota_col = esb("iota_col", [128, WC], bf16)
        window_base = esb("window_base", [128, NW], fp32)
        field = esb("field", [128, 5, CP], fp32)
        ranges = esb("ranges", [1, 2, NW], i32)

        prep = ExitStack()

        def psb(name, shape, dt):
            return prep.enter_context(nc.sbuf_tensor(name, shape, dt))

        src_i = psb("src_i", [128, NG, CE], i32)
        dst_i = psb("dst_i", [128, NG, CE], i32)
        w_f = psb("w_f", [128, NG, CE], fp32)
        srcf = psb("srcf", [128, NG, CE], fp32)
        dstf = psb("dstf", [128, NG, CE], fp32)
        tile_f = psb("tile_f", [128, NG, CE], fp32)
        win_f = psb("win_f", [128, NG, CE], fp32)
        tmp_f = psb("tmp_f", [128, NG, CE], fp32)
        part_bf = psb("part_bf", [128, NG, CE], bf16)
        edge_f = psb("edge_f", [128, 5, NG, CE], fp32)
        win_min = psb("win_min", [128, NG], fp32)
        win_max = psb("win_max", [128, NG], fp32)
        bc_max = psb("bc_max", [128, CP], fp32)
        bc_min = psb("bc_min", [128, CP], fp32)
        win_of = psb("win_of", [128, WG], fp32)
        chunk_no = psb("chunk_no", [128, CH], fp32)
        chunk_no1 = psb("chunk_no1", [128, CH], fp32)
        scr = psb("scr", [128, CH], fp32)
        lohi = psb("lohi", [128, 2, WG], fp32)
        psP = prep.enter_context(nc.psum_tensor("psP", [128, 4, 512], fp32))
        ranges_f = psb("ranges_f", [1, 2, NW], fp32)

        s_pad = sem("s_pad")
        s_edges = sem("s_edges")
        s_const = sem("s_const")
        s_fields = sem("s_fields")
        s_ftr = sem("s_ftr")
        s_fev = sem("s_fev")
        s_lohi = sem("s_lohi")
        s_row = sem("s_row")
        s_ranges = sem("s_ranges")
        s_dl = sem("s_dl")
        FULL = (NG - 1) * 128 * CE
        REST = (E - FULL) // CE
        LAST = E - FULL - REST * CE

        with nc.Block() as block:
            @block.sync
            def _(sp):
                with path(sp, 0):
                    sp.wait_ge(s_pad, 1)
                    for tile, a in ((src_i, A["src"]), (dst_i, A["dst"]), (w_f, A["edge_weight"])):
                        sp.dma_start(tile[:, 0:NG - 1, :], a[0:FULL].rearrange("(g p e) -> p g e", g=NG - 1, p=128)).then_inc(s_edges, 16)
                        sp.dma_start(tile[0:REST, NG - 1, :], a[FULL:FULL + REST * CE].rearrange("(p e) -> p e", p=REST)).then_inc(s_edges, 16)
                        sp.dma_start(tile[REST:REST + 1, NG - 1, 0:LAST], a[FULL + REST * CE:E].rearrange("(p e) -> p e", p=1)).then_inc(s_edges, 16)

            @block.gpsimd
            def _(pool):
                with path(pool, 0):
                    nc.gpsimd.iota(iota_col[:], [[1, WC]], base=0, channel_multiplier=0, allow_small_or_imprecise_dtypes=True)
                    nc.gpsimd.iota(window_base[:], [[-WC, NW]], base=0, channel_multiplier=0, allow_small_or_imprecise_dtypes=True)
                    nc.gpsimd.iota(win_of[:], [[P, WG]], base=0, channel_multiplier=1, allow_small_or_imprecise_dtypes=True)
                    nc.gpsimd.iota(chunk_no[:], [[1, CH]], base=0, channel_multiplier=0, allow_small_or_imprecise_dtypes=True)
                    nc.gpsimd.iota(chunk_no1[:], [[1, CH]], base=1, channel_multiplier=0, allow_small_or_imprecise_dtypes=True).then_inc(s_const, 1)

            @block.vector
            def _(dve):
                with path(dve, 0):
                    link = chain(dve, s_dl)
                    v = nc.vector
                    v.memset(src_i[:, NG - 1, :], N)
                    v.memset(dst_i[:, NG - 1, :], N - 1)
                    v.memset(w_f[:, NG - 1, :], 0.0).then_inc(s_pad, 1)
                    dve.wait_ge(s_edges, 9 * 16)
                    v.tensor_copy(srcf[:], src_i[:])
                    link(v.tensor_copy(dstf[:], dst_i[:]))
                    v.tensor_scalar(tile_f[:], srcf[:], (P - 1) / 2, 1.0 / P, ALU.subtract, ALU.mult)
                    link(v.tensor_scalar(win_f[:], dstf[:], (W - 1) / 2, 1.0 / W, ALU.subtract, ALU.mult))
                    v.tensor_scalar(tile_f[:], tile_f[:], ROUND, ROUND, ALU.add, ALU.subtract)
                    link(v.tensor_scalar(win_f[:], win_f[:], ROUND, ROUND, ALU.add, ALU.subtract))
                    v.scalar_tensor_tensor(edge_f[:, 0], tile_f[:], -float(P), srcf[:], ALU.mult, ALU.add)
                    link(v.scalar_tensor_tensor(tmp_f[:], tile_f[:], float(W), dstf[:], ALU.mult, ALU.add))
                    v.scalar_tensor_tensor(edge_f[:, 1], win_f[:], float(WC - W), tmp_f[:], ALU.mult, ALU.add)
                    v.tensor_reduce(win_min[:], win_f[:], AX.X, ALU.min)
                    v.tensor_reduce(win_max[:], win_f[:], AX.X, ALU.max)
                    link(v.tensor_copy(part_bf[:], w_f[:]))
                    v.tensor_copy(edge_f[:, 2], part_bf[:])
                    link(v.tensor_tensor(tmp_f[:], w_f[:], part_bf[:], ALU.subtract))
                    link(v.tensor_copy(part_bf[:], tmp_f[:]))
                    v.tensor_copy(edge_f[:, 3], part_bf[:])
                    link(v.tensor_tensor(tmp_f[:], tmp_f[:], part_bf[:], ALU.subtract))
                    v.tensor_copy(edge_f[:, 4], tmp_f[:]).then_inc(s_fields, 1)
                    n = 0
                    for f in range(5):
                        for h, (g0, gn) in enumerate(((0, 4), (4, NG - 4))):
                            n += 1
                            dve.wait_ge(s_ftr, n)
                            v.tensor_copy(field[:, f, g0 * 128:(g0 + gn) * 128], psP[:, h, 0:gn * 128]).then_inc(s_fev, 1)
                    for t in (bc_min, bc_max):
                        for h, (g0, gn) in enumerate(((0, 4), (4, NG - 4))):
                            n += 1
                            dve.wait_ge(s_ftr, n)
                            last = v.tensor_copy(t[:, g0 * 128:(g0 + gn) * 128], psP[:, h, 0:gn * 128]).then_inc(s_fev, 1)
                    dve.wait_ge(s_fev, n)
                    dve.wait_ge(s_const, 1)
                    for g in range(WG):
                        link(v.tensor_scalar(scr[:], bc_max[:, 0:CH], win_of[:, g:g + 1], float(1 << 20), ALU.is_lt, ALU.mult))
                        link(v.tensor_tensor(scr[:], scr[:], chunk_no[:], ALU.add))
                        link(v.tensor_reduce(lohi[:, 0, g:g + 1], scr[:], AX.X, ALU.min))
                        link(v.scalar_tensor_tensor(scr[:], bc_min[:, 0:CH], win_of[:, g:g + 1], chunk_no1[:], ALU.is_le, ALU.mult))
                        link(v.tensor_reduce(lohi[:, 1, g:g + 1], scr[:], AX.X, ALU.max))
                    link(v.tensor_scalar(lohi[:, 0], lohi[:, 0], float(CH - 1), None, ALU.min))
                    v.scalar_tensor_tensor(lohi[:, 1], lohi[:, 0], 2.0, lohi[:, 1], ALU.add, ALU.max).then_inc(s_lohi, 1)
                    dve.wait_ge(s_row, 1)
                    for b in range(2):
                        v.tensor_copy(ranges_f[:, b, 0:4 * P].rearrange("o (g p) -> o g p", g=4),
                                      psP[0:1, 2 * b, :].rearrange("o (g p) -> o g p", g=4)[:, :, 0:P])
                        last = v.tensor_copy(ranges_f[:, b, 4 * P:5 * P], psP[0:1, 2 * b + 1, 0:P])
                    link(last)
                    v.tensor_copy(ranges[:], ranges_f[:]).then_inc(s_ranges, 1)

            @block.tensor
            def _(pe):
                with path(pe, 0):
                    pe.wait_ge(s_const, 1)
                    pe.wait_ge(s_fields, 1)
                    n = 0
                    for f in range(5):
                        for h, (g0, gn) in enumerate(((0, 4), (4, NG - 4))):
                            if n >= 2:
                                pe.wait_ge(s_fev, n - 1)
                            for g in range(gn):
                                last = nc.tensor.transpose(psP[:, h, g * 128:(g + 1) * 128], edge_f[:, f, g0 + g, :], ident[:])
                            last.then_inc(s_ftr, 1)
                            n += 1
                    for t in (win_min, win_max):
                        for h, (g0, gn) in enumerate(((0, 4), (4, NG - 4))):
                            pe.wait_ge(s_fev, n - 1)
                            for g in range(gn):
                                last = nc.tensor.matmul(psP[:, h, g * 128:(g + 1) * 128],
                                                        t[:, g0 + g:g0 + g + 1].broadcast_to([128, 128]), ident[:],
                                                        start=True, stop=True)
                            last.then_inc(s_ftr, 1)
                            n += 1
                    pe.wait_ge(s_lohi, 1)
                    for b in range(2):
                        for g in range(WG):
                            last = nc.tensor.matmul(psP[0:1, 2 * b + g // 4, (g % 4) * 128:(g % 4) * 128 + P], lohi[0:P, b, g:g + 1],
                                                    ident[0:P, 0:P], start=True, stop=True)
                    last.then_inc(s_row, 1)

        prep.close()

        build = ExitStack()

        def bsb(name, shape, dt):
            return build.enter_context(nc.sbuf_tensor(name, shape, dt))

        onehot = bsb("onehot", [128, RING, 5, 128], bf16)
        stage = bsb("stage", [P, 2, 2, T, P], fp32)
        count_f = bsb("count_f", [P, T, P], fp32)
        count_bf = bsb("count_bf", [P, T, P], bf16)
        weight_f = bsb("weight_f", [P, T, P], fp32)
        weight_T = bsb("weight_T", [P, T, P], fp32)
        logm = bsb("logm", [P, N], fp32)
        log_f = bsb("log_f", [P, N], fp32)
        none_f = bsb("none_f", [P, N], fp32)
        psW = build.enter_context(nc.psum_tensor("psW", [128, 2, 512], fp32))
        psT = build.enter_context(nc.psum_tensor("psT", [128, 2, 512], fp32))

        s_slot_free = sem("s_slot_free")
        s_hot = sem("s_hot")
        s_window = sem("s_window")
        s_half_free = sem("s_half_free")
        s_stage_free = sem("s_stage_free")
        s_count_f = sem("s_count_f")
        s_count_bf = sem("s_count_bf")
        s_turned = sem("s_turned")
        s_turned_free = sem("s_turned_free")
        s_ln = sem("s_ln")
        s_logmask = sem("s_logmask")
        s_logmask_free = sem("s_logmask_free")
        s_cd = sem("s_cd")
        s_wd = sem("s_wd")
        s_ld = sem("s_ld")
        NP = len(PIECES)

        with nc.Block() as block:
            @block.vector
            def _(dve):
                with path(dve, 0):
                    v = nc.vector
                    dve.sem_inc(s_turned_free, 2)
                    visit = dve.alloc_register("visit_v")
                    dve.reg_mov(visit, 0)
                    with dve.Fori(0, T) as dt:
                        with dve.Fori(0, WT) as ws:
                            w = dve.snap(dt * WT + ws, min_val=0, max_val=NW - 1)
                            lo = dve.value_load(ranges[0:1, 0, ds(w, 1)], min_val=0, max_val=CH - 1)
                            hi = dve.value_load(ranges[0:1, 1, ds(w, 1)], min_val=2, max_val=CH + 1)
                            with dve.Fori(lo, hi) as c:
                                n = dve.snap(visit, min_val=0, max_val=NW * CP)
                                slot = dve.snap(n & (RING - 1), min_val=0, max_val=RING - 1)
                                dve.wait_ge(s_slot_free, n + 1)
                                v.tensor_scalar(onehot[:, ds(slot, 1), 0, 0:WC], iota_col[:], field[:, 1, ds(c, 1)],
                                                window_base[:, ds(w, 1)], ALU.subtract, ALU.is_equal)
                                v.tensor_scalar(onehot[:, ds(slot, 1), 1, 0:P], iota_col[:, 0:P], field[:, 0, ds(c, 1)], None,
                                                ALU.is_equal)
                                for k in range(3):
                                    last = v.tensor_scalar(onehot[:, ds(slot, 1), 2 + k, 0:P], iota_col[:, 0:P],
                                                           field[:, 0, ds(c, 1)], field[:, 2 + k, ds(c, 1)],
                                                           ALU.is_equal, ALU.mult)
                                last.then_inc(s_hot, 1)
                                dve.reg_add(visit, visit, 1)
                        par = dve.snap(dt & 1, min_val=0, max_val=1)
                        dve.wait_ge(s_half_free, (dt + 1) * WT + 2)
                        v.tensor_copy(weight_f[:], stage[:, ds(par, 1), 1])
                        v.tensor_copy(count_f[:], stage[:, ds(par, 1), 0]).then_inc(s_count_f, 1)
                        dve.wait_ge(s_cd, (dt + 1) * 16)
                        v.tensor_scalar(count_bf[:], stage[:, ds(par, 1), 0].rearrange('p o a d -> p (o a) d'), 1.0, None, ALU.mult).then_inc(s_count_bf, 1)
                        dve.sem_inc(s_stage_free, 1)
                        dve.wait_ge(s_logmask, dt + 1)
                        for j, (a0, an) in enumerate(PIECES):
                            cols = slice(a0 * P, (a0 + an) * P)
                            dve.wait_ge(s_turned, dt * (2 * NP) + j + 1)
                            v.tensor_scalar(none_f[:, cols], psT[0:P, j % 2, 0:an * P], 0.0, MASKED, ALU.is_equal, ALU.mult)
                            v.tensor_scalar(log_f[:, cols], psT[0:P, j % 2, 0:an * P], 1.0, None, ALU.max).then_inc(s_turned_free, 1)
                        dve.wait_ge(s_wd, (dt + 1) * 16)
                        for j, (a0, an) in enumerate(PIECES):
                            dve.wait_ge(s_turned, dt * (2 * NP) + NP + j + 1)
                            v.tensor_copy(weight_T[:, a0:a0 + an].rearrange("p a d -> p (a d)"),
                                          psT[0:P, (NP + j) % 2, 0:an * P]).then_inc(s_turned_free, 1)

            @block.tensor
            def _(pe):
                with path(pe, 0):
                    t = nc.tensor
                    pe.sem_inc(s_slot_free, RING)
                    visit = pe.alloc_register("visit_t")
                    pe.reg_mov(visit, 0)

                    def products(w, half, first):
                        n = pe.snap(visit, min_val=0, max_val=NW * CP)
                        slot = pe.snap(n & (RING - 1), min_val=0, max_val=RING - 1)
                        pe.wait_ge(s_hot, n + 1)
                        cols = onehot[:, ds(slot, 1), 0, 0:WC]
                        t.matmul(psW[0:P, ds(half, 1), 0:WC], onehot[:, ds(slot, 1), 1, 0:P], cols,
                                 start=first, stop=True, skip_group_check=True)
                        for k in range(3):
                            last = t.matmul(psW[0:P, ds(half, 1), 128:128 + WC], onehot[:, ds(slot, 1), 2 + k, 0:P], cols,
                                            start=False, stop=True, skip_group_check=True)
                        last.then_inc(s_slot_free, 1)
                        pe.reg_add(visit, visit, 1)

                    with pe.Fori(0, T) as dt:
                        with pe.Fori(0, WT) as ws:
                            w = pe.snap(dt * WT + ws, min_val=0, max_val=NW - 1)
                            half = pe.snap(w & 1, min_val=0, max_val=1)
                            lo = pe.value_load(ranges[0:1, 0, ds(w, 1)], min_val=0, max_val=CH - 1)
                            hi = pe.value_load(ranges[0:1, 1, ds(w, 1)], min_val=2, max_val=CH + 1)
                            pe.wait_ge(s_half_free, w + 1)
                            products(w, half, True)
                            with pe.Fori(lo + 1, hi) as c:
                                products(w, half, False)
                            t.matmul(psW[0:P, ds(half, 1), 384:385], iota_col[:, 0:P], iota_col[:, 0:1],
                                     start=False, stop=True, skip_group_check=True).then_inc(s_window, 1)
                        pe.wait_ge(s_count_f, dt + 1)
                        for k, of in enumerate((count_f, weight_f)):
                            for j, (a0, an) in enumerate(PIECES):
                                pe.wait_ge(s_turned_free, dt * (2 * NP) + (k * NP + j + 1))
                                for a in range(an):
                                    last = t.transpose(psT[0:P, (k * NP + j) % 2, a * P:(a + 1) * P], of[:, a0 + a, :], ident[0:P, 0:P])
                                last.then_inc(s_turned, 1)

            @block.scalar
            def _(act):
                with path(act, 0):
                    act_sets(act)
                    act.sem_inc(s_half_free, 2)
                    act.sem_inc(s_stage_free, 1)
                    with act.Fori(0, T) as dt:
                        par = act.snap(dt & 1, min_val=0, max_val=1)
                        act.wait_ge(s_stage_free, dt + 1)
                        with act.Fori(0, WT) as ws:
                            w = act.snap(dt * WT + ws, min_val=0, max_val=NW - 1)
                            half = act.snap(w & 1, min_val=0, max_val=1)
                            act.wait_ge(s_window, w + 1)
                            for k in range(2):
                                last = nc.scalar.copy(stage[:, ds(par, 1), k, :, ds(ws * W, W)],
                                                      psW[0:P, ds(half, 1), 128 * k:128 * k + WC].rearrange("p o (a d) -> p o a d", a=T))
                            last.then_inc(s_half_free, 1)
                        act.wait_ge(s_turned_free, dt * (2 * NP) + (NP + 2))
                        nc.scalar.activation(log_f[:], log_f[:], ACT.Ln).then_inc(s_ln, 1)

            @block.gpsimd
            def _(pool):
                with path(pool, 0):
                    pool.sem_inc(s_logmask, 1)
                    with pool.Fori(0, T) as dt:
                        pool.wait_ge(s_ln, dt + 1)
                        pool.wait_ge(s_logmask_free, dt + 1)
                        nc.gpsimd.tensor_tensor(logm[:], log_f[:], none_f[:], ALU.add).then_inc(s_logmask, 1)

            @block.sync
            def _(sp):
                with path(sp, 0):
                    sp.sem_inc(s_stage_free, 1)
                    sp.sem_inc(s_cd, 16)
                    sp.sem_inc(s_wd, 16)
                    sp.sem_inc(s_logmask_free, 1)
                    with sp.Fori(0, T) as dt:
                        sp.wait_ge(s_count_bf, dt + 1)
                        sp.dma_start(count_d[ds(dt, 1)].rearrange("o p a d -> p (o a) d"), count_bf[:]).then_inc(s_cd, 16)
                        sp.wait_ge(s_logmask, dt + 2)
                        alone(sp)
                        sp.dma_start(logmask_d[ds(dt, 1)].rearrange("o p n -> (o p) n"), logm[:]).then_inc(s_ld, 16)
                        sp.wait_ge(s_turned_free, (dt + 1) * (2 * NP) + 2)
                        sp.dma_start(weight_d[ds(dt, 1)].rearrange("o p a d -> p (o a) d"), weight_T[:]).then_inc(s_wd, 16)
                        sp.wait_ge(s_ld, (dt + 1) * 16)
                        sp.sem_inc(s_logmask_free, 1)
                    sp.wait_ge(s_cd, (T + 1) * 16)
                    sp.wait_ge(s_wd, (T + 1) * 16)

        build.close()
        edges_st.close()
        done_with_semaphores()

        x_all = osb("x_all", [P, T, D], fp32)
        inv_deg = osb("inv_deg", [P, T], fp32)
        norm = osb("norm", [P, T], fp32)
        w_sage = osb("w_sage", [128, 4, D], fp32)
        w_n = osb("w_n", [128, D], fp32)
        w_out = osb("w_out", [128, D], fp32)
        w_low = osb("w_low", [128, D], fp32)
        w_1 = osb("w_1", [128, DH], fp32)
        w_2 = osb("w_2", [DH, D], fp32)
        bias = osb("bias", [P, 6, D], fp32)
        bn_col = osb("bn_col", [128, 1], fp32)
        minus_half = osb("minus_half", [128, T], fp32)

        BL1, BL2, BN, BOUT, B1, B2 = range(6)

        def row(ap):
            return ap.rearrange("(o d) -> o d", o=1).broadcast_to([P, ap.shape[0]])

        def column(ap):
            return ap.rearrange("(d o) -> d o", o=1)

        def tiles(eng):
            with eng.Fori(0, T // 2) as k:
                yield eng.snap(2 * k, min_val=0, max_val=T - 3), 0
                yield eng.snap(2 * k + 1, min_val=1, max_val=T - 2), 1
            yield T - 1, 0

        class Chain:

            def __init__(self, eng, semaphore, per_tile):
                self.eng, self.sem, self.per_tile = eng, semaphore, per_tile

            def tile(self, i):
                self.base, self.n = i * self.per_tile, 0

            def link(self, ins):
                self.n += 1
                assert self.n <= self.per_tile
                ins.then_inc(self.sem, 1)
                self.eng.wait_ge(self.sem, self.base + self.n)

            def alone(self):
                self.eng.sem_inc(s_passed, 1)

            def end(self):
                assert self.n == self.per_tile, self.n

        def split_parts(v, chain_, parts, i, y, rest, width, scale=None):
            hi = parts[:, ds(i, 1), 0:width]
            mid = parts[:, ds(i, 1), width:2 * width]
            lo = parts[:, ds(i, 1), 2 * width:3 * width]
            if scale is not None:
                chain_.link(v.tensor_scalar(hi, y, scale, None, ALU.mult))
                chain_.link(v.scalar_tensor_tensor(rest, y, scale, hi.rearrange("p o d -> p (o d)"), ALU.mult, ALU.subtract))
            else:
                chain_.link(v.tensor_scalar(hi, y, 1.0, None, ALU.mult))
                chain_.link(v.tensor_tensor(rest, y, hi.rearrange("p o d -> p (o d)"), ALU.subtract))
            chain_.link(v.tensor_scalar(mid, rest, 1.0, None, ALU.mult))
            return v.tensor_tensor(lo, rest, mid.rearrange("p o d -> p (o d)"), ALU.subtract)

        def normalise(v, chain_, x, stats, moments, centered, s_var):
            chain_.link(v.bn_stats(stats, x))
            chain_.alone()
            chain_.link(v.bn_aggr(moments[:, 0:2], stats))
            v.tensor_scalar(moments[:, 2:3], moments[:, 1:2], 1e-5, None, ALU.add).then_inc(s_var, 1)
            return v.tensor_scalar(centered, x, moments[:, 0:1], None, ALU.subtract)

        def rsqrt(pool, moments, s_var, s_rstd, i, u):
            pool.wait_ge(s_var, i + 1)
            nc.gpsimd.tensor_tensor(moments[:, u, 3:4], moments[:, u, 2:3], minus_half[0:P, 0:1], ALU.pow).then_inc(s_rstd, 1)

        PARTS = 3 * D + 1

        h_att = osb("h_att", [P, T, D], fp32)
        hT = osb("hT", [128, T, P], fp32)

        sage = ExitStack()

        def ssb(name, shape, dt):
            return sage.enter_context(nc.sbuf_tensor(name, shape, dt))

        parts_a = ssb("parts_a", [P, T, PARTS], bf16)
        parts_b = ssb("parts_b", [P, T, PARTS], bf16)
        self_a = ssb("self_a", [P, T, D], fp32)
        self_b = ssb("self_b", [P, T, D], fp32)
        w_raw = ssb("w_raw", [128, 4, D], fp32)
        w_nodes = ssb("w_nodes", [P, 2, D], fp32)
        w_turned = ssb("w_turned", [128, 2, P], fp32)
        agg = ssb("agg", [P, 2, D], fp32)
        rest = ssb("rest", [P, 2, D], fp32)
        stats = ssb("stats", [P, 2, 6], fp32)
        moments = ssb("moments", [P, 2, 4], fp32)
        centered = ssb("centered", [P, 2, D], fp32)
        x_new = ssb("x_new", [P, 2, D], fp32)
        deg1 = ssb("deg1", [P, 2, 2], fp32)
        mat = ssb("mat", [P, 2, T, P], bf16)
        psA = sage.enter_context(nc.psum_tensor("psA", [128, 2, 512], fp32))
        psY = sage.enter_context(nc.psum_tensor("psY", [128, 2, 512], fp32))
        psX = sage.enter_context(nc.psum_tensor("psX", [128, 2, 512], fp32))

        s_load = sem("s_load")
        s_half = sem("s_half")
        s_wt = sem("s_wt")
        s_wts = sem("s_wts")
        s3_mom = sem("s3_mom")
        s3_var = sem("s3_var")
        s3_rstd = sem("s3_rstd")
        s3_h = sem("s3_h")
        s3_turn = sem("s3_turn")
        s3_turned = sem("s3_turned")
        s3_y = sem("s3_y")
        s3_split = sem("s3_split")
        s3_chain = sem("s3_chain")
        loads = [(x_all[:], A["x"].rearrange("(t p) d -> p t d", p=P)),
                 (w_raw[:, 0], A["L0_gnn_Wl1"]), (w_raw[:, 1], A["L0_gnn_Wr1"]),
                 (w_raw[:, 2], A["L0_gnn_Wl2"]), (w_raw[:, 3], A["L0_gnn_Wr2"]),
                 (w_n[:], A["L1_gnn_Wn"]), (w_out[:], A["L1_gnn_Wout"]), (w_low[:], A["L2_gnn_weight_low"]),
                 (w_1[:], A["L3_gnn_W1"]), (w_2[:], A["L3_gnn_W2"]),
                 (bias[:, BL1], row(A["L0_gnn_bl1"])), (bias[:, BL2], row(A["L0_gnn_bl2"])),
                 (bias[:, BN], row(A["L1_gnn_bn"])), (bias[:, BOUT], row(A["L1_gnn_bout"])),
                 (bias[:, B1, 0:DH], row(A["L3_gnn_b1"])), (bias[:, B2], row(A["L3_gnn_b2"])),
                 (bn_col[:], column(A["L1_gnn_bn"]))]

        with nc.Block() as block:
            @block.sync
            def _(sp):
                for to, a in loads:
                    sp.dma_start(to, a).then_inc(s_load, 16)

            @block.gpsimd
            def _(pool):
                nc.gpsimd.memset(parts_a[:, :, 3 * D:PARTS], 1.0)
                nc.gpsimd.memset(parts_b[:, :, 3 * D:PARTS], 1.0)
                nc.gpsimd.memset(minus_half[:], -0.5).then_inc(s_half, 1)
                pool.wait_ge(s_half, 1)
                for i, u in tiles(pool):
                    rsqrt(pool, moments, s3_var, s3_rstd, i, u)

            @block.vector
            def _(dve):
                v = nc.vector
                dve.wait_ge(s_load, 16 * len(loads))
                dve.wait_ge(s_wt, 1)
                v.tensor_copy(w_sage[:], psA[:, 0, :].rearrange("p (k d) -> p k d", k=4)).then_inc(s_wts, 1)
                chain_ = Chain(dve, s3_chain, 5)

                def moments_of(i, u):
                    chain_.tile(i)
                    xi = x_all[:, ds(i, 1)].rearrange("p o d -> p (o d)")
                    normalise(v, chain_, xi, stats[:, u], moments[:, u], centered[:, u], s3_var).then_inc(s3_mom, 1)

                def outputs_of(i, u):
                    dve.wait_ge(s3_y, i + 1)
                    v.tensor_tensor(self_a[:, ds(i, 1)].rearrange("p o d -> p (o d)"), psY[0:P, u, D:2 * D], bias[:, BL1], ALU.add)
                    split_parts(v, chain_, parts_a, i, psY[0:P, u, 0:D], rest[:, u], D).then_inc(s3_split, 1)
                    chain_.end()

                for i, u in tiles(dve):
                    moments_of(i, u)
                    outputs_of(i, u)

            @block.scalar
            def _(act):
                act_sets(act)
                for i, u in tiles(act):
                    act.wait_ge(s3_mom, i + 1)
                    act.wait_ge(s3_rstd, i + 1)
                    nc.scalar.activation(w_nodes[:, u], centered[:, u], ACT.Relu, scale=moments[:, u, 3:4]).then_inc(s3_h, 1)
                    act.wait_ge(s3_turn, i + 1)
                    nc.scalar.copy(w_turned[:, u], psX[:, u, 0:P]).then_inc(s3_turned, 1)

            @block.tensor
            def _(pe):
                t = nc.tensor
                pe.wait_ge(s_load, 16 * len(loads))
                for k in range(4):
                    last = t.transpose(psA[:, 0, k * D:(k + 1) * D], w_raw[:, k], ident[:])
                last.then_inc(s_wt, 1)
                pe.wait_ge(s_wts, 1)
                for i, u in tiles(pe):
                    pe.wait_ge(s3_h, i + 1)
                    t.transpose(psX[:, u, 0:P], w_nodes[:, u], ident[0:P, 0:P]).then_inc(s3_turn, 1)
                    pe.wait_ge(s3_turned, i + 1)
                    t.matmul(psY[0:P, u, 0:2 * D], w_turned[:, u], w_sage[:, 0:2].rearrange("p k d -> p (k d)"),
                             start=True, stop=True).then_inc(s3_y, 1)

        def pipelined(eng, one, two):
            one(0, 0, 1)
            with eng.Fori(0, T // 2) as k:
                for u in (1, 0):
                    j = eng.snap(2 * k + (2 - u), min_val=1, max_val=T - 1)
                    i = eng.snap(2 * k + (1 - u), min_val=0, max_val=T - 2)
                    one(j, u, eng.snap(k + (2 - u), min_val=1, max_val=T // 2 + 1))
                    two(i, 1 - u)
            two(T - 1, 0)

        def flat(ap):
            return ap.rearrange("p o d -> p (o d)")

        def counts_of(i):
            return count_d[ds(i, 1)].rearrange("o p a d -> p (o a) d")

        def weights_of(i):
            return weight_d[:, :, ds(i, 1)].rearrange("a p o d -> p a (o d)")

        def convolution(name, source, tile, rhs, width, tails, dve_work, act_work, pool_work, psum):
            s_loaded = [sem(f"{name}_loaded_{u}") for u in range(2)]
            s_sum = sem(f"{name}_sum")
            s_sum_free = sem(f"{name}_sum_free")

            with nc.Block() as block:
                @block.sync
                def _(sp):
                    sp.sem_inc(s_sum, 2)
                    for i, u in tiles(sp):
                        sp.wait_ge(s_sum, i + 1)
                        alone(sp)
                        sp.dma_start(tile[:, u], source(i)).then_inc(s_loaded[u], 16)

                @block.tensor
                def _(pe):
                    def products(i, u, n):
                        pe.wait_ge(s_loaded[u], n * 16)
                        pe.wait_ge(s_sum_free, i + 1)
                        for a in range(T):
                            if a == T // 2 and not isinstance(i, int):
                                tails[0](pe, pe.snap(i - 1, min_val=0, max_val=T - 2), 1 - u)
                            last = nc.tensor.matmul(psum[0:P, u, 0:width], tile[:, u, a, :], rhs[:, a, 0:width],
                                                    start=a == 0, stop=a == T - 1)
                        last.then_inc(s_sum, 1)

                    def rest_of(i, u):
                        if isinstance(i, int):
                            tails[0](pe, i, u)
                        tails[1](pe, i, u)

                    pipelined(pe, products, rest_of)

                @block.vector
                def _(dve):
                    dve.sem_inc(s_sum_free, 2)
                    dve_work(dve, s_sum, s_sum_free)

                @block.scalar
                def _(act):
                    act_sets(act)
                    for i, u in tiles(act):
                        act_work(act, i, u, s_sum)

                @block.gpsimd
                def _(pool):
                    pool_work(pool)

        for layer in (1, 2):
            name = f"sage{layer}"
            parts, self_in = ((parts_a, self_a), (parts_b, self_b))[layer - 1]
            s_hi = sem(name + "_hi")
            s_var = sem(name + "_var")
            s_rstd = sem(name + "_rstd")
            s_mom = sem(name + "_mom")
            s_new = sem(name + "_new")
            s_turn = sem(name + "_turn")
            s_turned = sem(name + "_turned")
            s_y = sem(name + "_y")
            s_kept = sem(name + "_kept")
            s_fin = sem(name + "_fin")
            s_out = sem(name + "_out")

            def dve_work(dve, s_sum, s_sum_free, layer=layer, self_in=self_in, s_hi=s_hi, s_mom=s_mom, s_var=s_var, s_new=s_new, s_y=s_y,
                         s_kept=s_kept, s_fin=s_fin, s_out=s_out):
                v = nc.vector
                fin, outs = Chain(dve, s_fin, 6), Chain(dve, s_out, 3)

                def finish(i, u, n):
                    fin.tile(i)
                    dve.wait_ge(s_sum, i + 3)
                    dve.wait_ge(s_hi, i + 1)
                    if layer == 1:
                        fin.link(v.tensor_scalar(deg1[:, u, 0:1], psA[0:P, u, 3 * D:PARTS], 1.0, None, ALU.max))
                        fin.link(v.reciprocal(deg1[:, u, 1:2], deg1[:, u, 0:1]))
                        fin.link(v.tensor_scalar(inv_deg[:, ds(i, 1)], deg1[:, u, 1:2], 1.0, None, ALU.mult))
                        v.tensor_scalar(norm[:, ds(i, 1)], psA[0:P, u, 3 * D:PARTS], 1.0, None, ALU.add)
                    fin.link(v.tensor_tensor(agg[:, u], psA[0:P, u, D:2 * D], agg[:, u], ALU.add))
                    fin.link(v.tensor_tensor(agg[:, u], psA[0:P, u, 2 * D:3 * D], agg[:, u], ALU.add))
                    fin.link(v.scalar_tensor_tensor(agg[:, u], agg[:, u], inv_deg[:, ds(i, 1)], flat(self_in[:, ds(i, 1)]),
                                                    ALU.mult, ALU.add))
                    if layer == 1:
                        v.tensor_scalar(w_nodes[:, u], agg[:, u], 0.0, None, ALU.max).then_inc(s_new, 1)
                    else:
                        dve.wait_ge(s_kept, i + 1)
                        alone(dve)
                        fin.link(v.scalar_tensor_tensor(x_new[:, u], agg[:, u], 0.0, flat(x_all[:, ds(i, 1)]), ALU.max, ALU.add))
                        normalise(v, fin, x_new[:, u], stats[:, u], moments[:, u], centered[:, u], s_var).then_inc(s_mom, 1)
                    dve.sem_inc(s_sum_free, 1)
                    fin.end()

                def outputs(i, u):
                    outs.tile(i)
                    dve.wait_ge(s_y, i + 1)
                    if layer == 1:
                        v.tensor_tensor(flat(self_b[:, ds(i, 1)]), psY[0:P, u, D:2 * D], bias[:, BL2], ALU.add)
                        split_parts(v, outs, parts_b, i, psY[0:P, u, 0:D], rest[:, u], D)
                        outs.end()
                    else:
                        v.tensor_tensor(flat(h_att[:, ds(i, 1)]), psY[0:P, u, 0:D], bias[:, BN], ALU.add)
                        v.tensor_scalar(hT[:, ds(i, 1)].rearrange("p o d -> p (o d)"), psY[:, u, D:D + P], bn_col[:, 0:1], None, ALU.add)

                pipelined(dve, finish, outputs)

            def act_work(act, i, u, s_sum, layer=layer, s_hi=s_hi, s_mom=s_mom, s_rstd=s_rstd, s_new=s_new, s_turn=s_turn, s_turned=s_turned):
                act.wait_ge(s_sum, i + 3)
                nc.scalar.copy(agg[:, u], psA[0:P, u, 0:D]).then_inc(s_hi, 1)
                if layer == 2:
                    act.wait_ge(s_mom, i + 1)
                    act.wait_ge(s_rstd, i + 1)
                    nc.scalar.activation(w_nodes[:, u], centered[:, u], ACT.Relu, scale=moments[:, u, 3:4]).then_inc(s_new, 1)
                act.wait_ge(s_turn, i + 1)
                nc.scalar.copy(w_turned[:, u], psX[:, u, 0:P]).then_inc(s_turned, 1)

            def pool_work(pool, layer=layer, s_kept=s_kept, s_var=s_var, s_mom=s_mom, s_rstd=s_rstd):
                if layer == 2:
                    pool.sem_inc(s_kept, 2)
                    nc.gpsimd.tensor_tensor(norm[:], norm[:], minus_half[0:P, :], ALU.pow)
                    for i, u in tiles(pool):
                        rsqrt(pool, moments, s_var, s_rstd, i, u)
                        pool.wait_ge(s_mom, i + 1)
                        alone(pool)
                        nc.gpsimd.tensor_copy(flat(x_all[:, ds(i, 1)]), x_new[:, u]).then_inc(s_kept, 1)

            def tail_1(pe, i, u, s_new=s_new, s_turn=s_turn):
                pe.wait_ge(s_new, i + 1)
                nc.tensor.transpose(psX[:, u, 0:P], w_nodes[:, u], ident[0:P, 0:P]).then_inc(s_turn, 1)

            def tail_2(pe, i, u, layer=layer, s_turned=s_turned, s_y=s_y):
                pe.wait_ge(s_turned, i + 1)
                if layer == 1:
                    nc.tensor.matmul(psY[0:P, u, 0:2 * D], w_turned[:, u], w_sage[:, 2:4].rearrange("p k d -> p (k d)"),
                                     start=True, stop=True).then_inc(s_y, 1)
                else:
                    nc.tensor.matmul(psY[0:P, u, 0:D], w_turned[:, u], w_n[:], start=True, stop=True)
                    nc.tensor.matmul(psY[:, u, D:D + P], w_n[:], w_turned[:, u], start=True, stop=True,
                                     skip_group_check=True).then_inc(s_y, 1)

            convolution(name, counts_of, mat, parts, PARTS, (tail_1, tail_2), dve_work, act_work, pool_work, psA)
        sage.close()

        att = ExitStack()

        def asb(name, shape, dt=fp32):
            return att.enter_context(nc.sbuf_tensor(name, shape, dt))

        SCALE = float(D) ** -0.5
        NPC = len(PIECES)
        EVEN = [j for j in range(NPC) if j % 2 == 0]
        ODD = [j for j in range(NPC) if j % 2 == 1]
        EXP = [(0, 3), (3, 5), (5, NPC)]

        wl = asb("wl", [128, 4, D])
        rows_l = asb("rows_l", [P, 3, D])
        cols_l = asb("cols_l", [128, 3])
        bq_scaled = asb("bq_scaled", [128, 1])
        kT = asb("kT", [128, T, P])
        vT = asb("vT", [128, T, P])
        vo = asb("vo", [P, T, D])
        qT = asb("qT", [128, 2, P])
        probs = asb("probs", [P, 2, N])
        logm_in = asb("logm_in", [P, 2, N])
        probs_T = asb("probs_T", [P, 3, 4 * P])
        piece_max = asb("piece_max", [P, 2, NPC])
        neg_max = asb("neg_max", [P, 2, 2])
        row_sum = asb("row_sum", [P, 2, 4])
        inv_sum = asb("inv_sum", [P, 2, 2])
        y_att = asb("y_att", [P, 2, D])
        c_att = asb("c_att", [P, 2, D])
        h_new = asb("h_new", [P, 2, D])
        st_att = asb("st_att", [P, 2, 6])
        mo_att = asb("mo_att", [P, 2, 4])
        psS = att.enter_context(nc.psum_tensor("psS", [128, 3, 512], fp32))
        psR = att.enter_context(nc.psum_tensor("psR", [128, 2, 512], fp32))
        psO = att.enter_context(nc.psum_tensor("psO", [128, 512], fp32))
        psQ = att.enter_context(nc.psum_tensor("psQ", [128, 512], fp32))
        psH = att.enter_context(nc.psum_tensor("psH", [128, 512], fp32))

        a_w = sem("a_w")
        a_bq = sem("a_bq")
        a_kv = sem("a_kv")
        a_kv_out = sem("a_kv_out")
        a_vo = sem("a_vo")
        a_vo_out = sem("a_vo_out")
        a_q = sem("a_q")
        a_q_out = sem("a_q_out")
        a_logm = [sem(f"a_logm_{u}") for u in range(2)]
        a_logm_free = sem("a_logm_free")
        a_s = sem("a_s")
        a_s_out = sem("a_s_out")
        a_max = sem("a_max")
        a_exp = sem("a_exp")
        a_t = sem("a_t")
        a_t_dve = sem("a_t_dve")
        a_t_act = sem("a_t_act")
        a_pv = sem("a_pv")
        a_o = sem("a_o")
        a_var = sem("a_var")
        a_cen = sem("a_cen")
        a_h = sem("a_h")
        a_h_kept = sem("a_h_kept")
        a_hT = sem("a_hT")
        a_hT_out = sem("a_hT_out")
        a_mx_chain = sem("a_mx_chain")
        a_dve_chain = sem("a_dve_chain")
        a_pool_chain = sem("a_pool_chain")
        NLOADS = 10
        ONE_AHEAD = {"pe": (a_pv,), "dve": (a_s_out, a_t_dve, a_o), "act": (a_q_out, a_t_act, a_hT_out), "pool": (a_h_kept,)}

        def ahead(eng, name):
            for s in ONE_AHEAD[name]:
                eng.sem_inc(s, 1)

        def flat_t(ap):
            return ap.rearrange("p a d -> p (a d)")

        def steps(eng, l):
            def one(s):
                return s, eng.snap(l * T + s, min_val=s, max_val=(LAYERS - 1) * T + s), s % 2
            for s in (0, 1, 2):
                yield one(s)
            with eng.Fori(0, (T - 5) // 2) as k:
                for d in (3, 4):
                    s = eng.snap(2 * k + d, min_val=3, max_val=T - 3)
                    yield s, eng.snap(l * T + s, min_val=3, max_val=(LAYERS - 1) * T + T - 3), d % 2
            for s in range(T - 2, T + 3):
                yield one(s)

        def has(s, back):
            return True if not isinstance(s, int) else 0 <= s - back < T

        with nc.Block() as block:
            @block.sync
            def _(sp):
                with sp.Fori(0, LAYERS) as l:
                    sp.wait_ge(a_h_kept, l * T + 1)
                    alone(sp)
                    one = ds(l, 1)
                    for k, w in enumerate(("WQ", "WK", "WV", "WO")):
                        sp.dma_start(wl[:, k], A["L1_gnn_" + w][one].rearrange("o i j -> (o i) j")).then_inc(a_w, 16)
                    for k, w in enumerate(("bO", "ln_g", "ln_b")):
                        sp.dma_start(rows_l[:, k], A["L1_gnn_" + w][one].broadcast_to([P, D])).then_inc(a_w, 16)
                    for k, w in enumerate(("bQ", "bK", "bV")):
                        sp.dma_start(cols_l[:, k:k + 1], A["L1_gnn_" + w][one].rearrange("o d -> d o")).then_inc(a_w, 16)
                    for s, g, u in steps(sp, l):
                        if not has(s, 0):
                            continue
                        sp.wait_ge(a_logm_free, g + 2 if isinstance(s, int) and s == 0 else g + 1 if not isinstance(s, int) or s > 1 else g)
                        sp.dma_start(logm_in[:, u], logmask_d[ds(s, 1)].rearrange("o p n -> (o p) n")).then_inc(a_logm[u], 16)

            @block.tensor
            def _(pe):
                t = nc.tensor
                ahead(pe, "pe")

                def queries(s1, g1):
                    pe.wait_ge(a_q_out, g1 + 1)
                    alone(pe)
                    t.matmul(psQ[:, 0:P], wl[:, 0], flat(hT[:, ds(s1, 1)]), start=True, stop=True).then_inc(a_q, 1)

                def values(g, u, j):
                    a0, an = PIECES[j]
                    if j == 0:
                        pe.wait_ge(a_o, g + 1)
                    if j % 2 == 0:
                        pe.wait_ge(a_t_dve, g * len(EVEN) + j // 2 + 2)
                    else:
                        pe.wait_ge(a_t_act, g * len(ODD) + j // 2 + 2)
                    for a in range(an):
                        last = t.matmul(psO[0:P, 0:D], probs_T[:, j % 3, a * P:(a + 1) * P], vo[:, a0 + a],
                                        start=a0 + a == 0, stop=a0 + a == T - 1)
                    last.then_inc(a_pv, 1)

                with pe.Fori(0, LAYERS) as l:
                    pe.wait_ge(a_w, (l + 1) * (NLOADS * 16))
                    pe.wait_ge(a_hT_out, l * T + 1)
                    pe.wait_ge(a_s_out, l * (T * NPC) + 1)
                    n = 0
                    for j, (a0, an) in enumerate(PIECES):
                        for k in (1, 2):
                            if n >= 3:
                                pe.wait_ge(a_kv_out, l * (2 * NPC) + n - 2)
                            t.matmul(psS[:, n % 3, 0:an * P], wl[:, k], flat_t(hT[:, a0:a0 + an]),
                                     start=True, stop=True).then_inc(a_kv, 1)
                            n += 1
                    for j, (a0, an) in enumerate(PIECES):
                        pe.wait_ge(a_kv_out, l * (2 * NPC) + 2 * j + 2)
                        if j >= 2:
                            pe.wait_ge(a_vo_out, l * NPC + j - 1)
                        for a in range(an):
                            last = t.matmul(psR[0:P, j % 2, a * D:(a + 1) * D], vT[:, a0 + a], wl[:, 3],
                                            start=True, stop=True)
                        last.then_inc(a_vo, 1)
                    pe.wait_ge(a_kv_out, (l + 1) * (2 * NPC))
                    pe.wait_ge(a_vo_out, (l + 1) * NPC)
                    queries(0, l * T)
                    for s, g, u in steps(pe, l):
                        if has(s, -1):
                            queries(s + 1, g + 1)
                        gi = pe.snap(g - 2, min_val=0, max_val=LAYERS * T) if has(s, 2) else None
                        for j, (a0, an) in enumerate(PIECES):
                            if has(s, 0):
                                if j == 0:
                                    pe.wait_ge(a_q_out, g + 2)
                                if j >= 3:
                                    pe.wait_ge(a_s_out, g * NPC + j - 1)
                                elif not (isinstance(s, int) and s == 0):
                                    pe.wait_ge(a_s_out, g * NPC - (0, 2, 1)[j] + 1)
                                t.matmul(psS[0:P, j % 3, 0:an * P], qT[:, u], flat_t(kT[:, a0:a0 + an]),
                                         start=True, stop=True).then_inc(a_s, 1)
                            if has(s, 2):
                                if j == 0:
                                    pe.wait_ge(a_exp, gi + 1)
                                if j % 2 == 0:
                                    pe.wait_ge(a_t_dve, gi * len(EVEN) + j // 2 + 1)
                                else:
                                    pe.wait_ge(a_t_act, gi * len(ODD) + j // 2 + 1)
                                for a in range(an):
                                    last = t.transpose(psR[0:P, j % 2, a * P:(a + 1) * P],
                                                       probs[:, u, (a0 + a) * P:(a0 + a + 1) * P], ident[0:P, 0:P])
                                last.then_inc(a_t, 1)
                                if j >= 1:
                                    values(gi, u, j - 1)
                            if j == 3 and has(s, 3):
                                pe.wait_ge(a_h, g - 2)
                                pe.wait_ge(a_hT_out, g - 2)
                                t.transpose(psH[:, 0:P], h_new[:, 1 - u], ident[0:P, 0:P]).then_inc(a_hT, 1)
                        if has(s, 2):
                            values(gi, u, NPC - 1)

            @block.vector
            def _(dve):
                v = nc.vector
                mx, fin = Chain(dve, a_mx_chain, 1), Chain(dve, a_dve_chain, 6)
                dve.sem_inc(a_logm_free, 2)
                ahead(dve, "dve")
                with dve.Fori(0, LAYERS) as l:
                    dve.wait_ge(a_w, (l + 1) * (NLOADS * 16))
                    dve.wait_ge(a_q_out, l * T + 1)
                    v.tensor_scalar(bq_scaled[:], cols_l[:, 0:1], SCALE, None, ALU.mult).then_inc(a_bq, 1)
                    dve.wait_ge(a_h_kept, l * T + 1)
                    for j, (a0, an) in enumerate(PIECES):
                        dve.wait_ge(a_vo, l * NPC + j + 1)
                        v.tensor_copy(vo[:, a0:a0 + an].rearrange("p a d -> p (a d)"), psR[0:P, j % 2, 0:an * D]).then_inc(a_vo_out, 1)
                    for s, g, u in steps(dve, l):
                        if has(s, 0):
                            n = l * (T // 2 + 1 - u) + (s // 2 + 1)
                            dve.wait_ge(a_logm[u], n * 16)
                            alone(dve)
                        gi = dve.snap(g - 2, min_val=0, max_val=LAYERS * T) if has(s, 2) else None
                        for j, (a0, an) in enumerate(PIECES):
                            cols = slice(a0 * P, (a0 + an) * P)
                            if has(s, 0):
                                if has(s, 2):
                                    dve.wait_ge(a_t, gi * NPC + j + 1)
                                    alone(dve)
                                dve.wait_ge(a_s, g * NPC + j + 1)
                                alone(dve)
                                v.tensor_tensor_reduce(out=probs[:, u, cols], in0=psS[0:P, j % 3, 0:an * P], in1=logm_in[:, u, cols],
                                                       scale=1.0, scalar=-3.0e38, op0=ALU.add, op1=ALU.max,
                                                       accum_out=piece_max[:, u, j:j + 1]).then_inc(a_s_out, 1)
                            if has(s, 2) and j in EVEN:
                                dve.wait_ge(a_t, gi * NPC + j + 1)
                                dve.wait_ge(a_pv, gi * NPC + (j - 2 if j >= 3 else 0) + 1)
                                v.tensor_copy(probs_T[:, j % 3, 0:an * P], psR[0:P, j % 2, 0:an * P]).then_inc(a_t_dve, 1)
                        if has(s, 0):
                            mx.tile(g)
                            dve.wait_ge(a_s_out, g * NPC + NPC + 1)
                            mx.link(v.tensor_reduce(neg_max[:, u, 0:1], piece_max[:, u], AX.X, ALU.max, negate=True))
                            v.tensor_scalar(neg_max[:, u, 1:2], neg_max[:, u, 0:1], -MASKED / 10, None, ALU.min).then_inc(a_max, 1)
                            dve.sem_inc(a_logm_free, 1)
                        if has(s, 2):
                            i = s - 2
                            fin.tile(gi)
                            dve.wait_ge(a_exp, gi + 1)
                            fin.link(v.tensor_reduce(inv_sum[:, u, 0:1], row_sum[:, u, 0:len(EXP)], AX.X, ALU.add))
                            fin.link(v.tensor_scalar(inv_sum[:, u, 0:1], inv_sum[:, u, 0:1], 1e-30, None, ALU.max))
                            fin.link(v.reciprocal(inv_sum[:, u, 1:2], inv_sum[:, u, 0:1]))
                            dve.wait_ge(a_pv, gi * NPC + NPC + 1)
                            v.scalar_tensor_tensor(y_att[:, u], psO[0:P, 0:D], inv_sum[:, u, 1:2], flat(h_att[:, ds(i, 1)]),
                                                   ALU.mult, ALU.add).then_inc(a_o, 1)
                            dve.wait_ge(a_o, gi + 2)
                            fin.link(v.tensor_tensor(y_att[:, u], y_att[:, u], rows_l[:, 0], ALU.add))
                            normalise(v, fin, y_att[:, u], st_att[:, u], mo_att[:, u], c_att[:, u], a_var).then_inc(a_cen, 1)
                            fin.end()

            @block.scalar
            def _(act):
                act_sets(act)
                sc = nc.scalar
                ahead(act, "act")

                def queries_out(g1, u1):
                    act.wait_ge(a_q, g1 + 1)
                    sc.activation(qT[:, u1], psQ[:, 0:P], ACT.Identity, bias=bq_scaled[:], scale=SCALE).then_inc(a_q_out, 1)

                with act.Fori(0, LAYERS) as l:
                    act.wait_ge(a_bq, l + 1)
                    for j, (a0, an) in enumerate(PIECES):
                        for k, to in ((1, kT), (2, vT)):
                            act.wait_ge(a_kv, l * (2 * NPC) + 2 * j + k)
                            sc.activation(flat_t(to[:, a0:a0 + an]), psS[:, (2 * j + k - 1) % 3, 0:an * P], ACT.Identity,
                                          bias=cols_l[:, k:k + 1]).then_inc(a_kv_out, 1)
                    queries_out(l * T, 0)
                    for s, g, u in steps(act, l):
                        if has(s, -1):
                            if has(s, 1):
                                act.wait_ge(a_s, g * NPC)
                            queries_out(g + 1, 1 - u)
                        gi = act.snap(g - 2, min_val=0, max_val=LAYERS * T) if has(s, 2) else None

                        def exponentials(part):
                            p0, p1 = EXP[part]
                            cols = slice(PIECES[p0][0] * P, (PIECES[p1 - 1][0] + PIECES[p1 - 1][1]) * P)
                            ins = sc.activation(probs[:, 1 - u, cols], probs[:, 1 - u, cols], ACT.Exp,
                                                bias=neg_max[:, 1 - u, 1:2], accum_out=row_sum[:, 1 - u, part:part + 1])
                            if part == len(EXP) - 1:
                                ins.then_inc(a_exp, 1)

                        if has(s, 1):
                            if has(s, 3):
                                act.wait_ge(a_o, g - 1)
                            act.wait_ge(a_max, g)
                        for part in range(len(EXP)):
                            if has(s, 1):
                                exponentials(part)
                            j = 2 * part + 1
                            if has(s, 2):
                                act.wait_ge(a_t, gi * NPC + j + 1)
                                act.wait_ge(a_pv, gi * NPC + (j - 2 if j >= 3 else 0) + 1)
                                a0, an = PIECES[j]
                                sc.copy(probs_T[:, j % 3, 0:an * P], psR[0:P, j % 2, 0:an * P]).then_inc(a_t_act, 1)
                            if part == 1 and has(s, 3):
                                act.wait_ge(a_hT, g - 2)
                                alone(act)
                                sc.copy(flat(hT[:, ds(s - 3, 1)]), psH[:, 0:P]).then_inc(a_hT_out, 1)

            @block.gpsimd
            def _(pool):
                p = nc.gpsimd
                ahead(pool, "pool")
                link = Chain(pool, a_pool_chain, 3)
                with pool.Fori(0, LAYERS) as l:
                    for i, u in tiles(pool):
                        g = pool.snap(l * T + i, min_val=0, max_val=LAYERS * T)
                        link.tile(g)
                        pool.wait_ge(a_var, g + 1)
                        link.link(p.tensor_tensor(mo_att[:, u, 3:4], mo_att[:, u, 2:3], minus_half[0:P, 0:1], ALU.pow))
                        pool.wait_ge(a_cen, g + 1)
                        link.link(p.tensor_tensor(c_att[:, u], c_att[:, u], mo_att[:, u, 3:4].broadcast_to([P, D]), ALU.mult))
                        link.link(p.tensor_tensor(c_att[:, u], c_att[:, u], rows_l[:, 1], ALU.mult))
                        p.tensor_tensor(h_new[:, u], c_att[:, u], rows_l[:, 2], ALU.add).then_inc(a_h, 1)
                        pool.wait_ge(a_h, g + 1)
                        alone(pool)
                        p.tensor_copy(flat(h_att[:, ds(i, 1)]), h_new[:, u]).then_inc(a_h_kept, 1)
        att.close()

        late = ExitStack()

        def lsb(name, shape, dt=fp32):
            return late.enter_context(nc.sbuf_tensor(name, shape, dt))

        support = lsb("support", [P, T, D])
        parts_c = lsb("parts_c", [P, T, 3 * DH], bf16)
        parts_d = lsb("parts_d", [P, T, 3 * DH], bf16)
        self_c = lsb("self_c", [P, T, DH])
        self_d = lsb("self_d", [P, T, DH])
        l_nodes = lsb("l_nodes", [P, 2, D])
        l_turned = lsb("l_turned", [128, 2, P])
        l_turned2 = lsb("l_turned2", [128, 2, P])
        l_agg = lsb("l_agg", [P, 2, D])
        l_rest = lsb("l_rest", [P, 2, D])
        l_stats = lsb("l_stats", [P, 2, 6])
        l_moments = lsb("l_moments", [P, 2, 4])
        l_centered = lsb("l_centered", [P, 2, D])
        l_x = lsb("l_x", [P, 2, D])
        l_mat = lsb("l_mat", [P, 2, T, P])
        l_mat_bf = lsb("l_mat_bf", [P, 2, T, P], bf16)
        psE = late.enter_context(nc.psum_tensor("psE", [128, 2, 512], fp32))
        psF = late.enter_context(nc.psum_tensor("psF", [128, 2, 512], fp32))
        psG = late.enter_context(nc.psum_tensor("psG", [128, 2, 512], fp32))

        def keep_and_scale(pool, s_var, s_rstd, s_mom, s_kept):
            pool.sem_inc(s_kept, 2)
            for i, u in tiles(pool):
                rsqrt(pool, l_moments, s_var, s_rstd, i, u)
                pool.wait_ge(s_mom, i + 1)
                alone(pool)
                nc.gpsimd.tensor_copy(flat(x_all[:, ds(i, 1)]), l_x[:, u]).then_inc(s_kept, 1)

        o_copy = sem("o_copy")
        o_y = sem("o_y")
        o_var = sem("o_var")
        o_rstd = sem("o_rstd")
        o_mom = sem("o_mom")
        o_kept = sem("o_kept")
        o_new = sem("o_new")
        o_turn = sem("o_turn")
        o_turned = sem("o_turned")
        o_sup = sem("o_sup")
        o_chain = sem("o_chain")
        o_done = sem("o_done")

        with nc.Block() as block:
            @block.tensor
            def _(pe):
                def first(i, u, n):
                    pe.wait_ge(o_copy, i + 1)
                    nc.tensor.matmul(psE[0:P, u, 0:D], l_turned[:, u], w_out[:], start=True, stop=True).then_inc(o_y, 1)

                def second(i, u):
                    pe.wait_ge(o_new, i + 1)
                    nc.tensor.transpose(psF[:, u, 0:P], l_nodes[:, u], ident[0:P, 0:P]).then_inc(o_turn, 1)
                    pe.wait_ge(o_turned, i + 1)
                    nc.tensor.matmul(psG[0:P, u, 0:D], l_turned2[:, u], w_low[:], start=True, stop=True).then_inc(o_sup, 1)

                pipelined(pe, first, second)

            @block.vector
            def _(dve):
                v = nc.vector
                chain_ = Chain(dve, o_chain, 4)

                def first(i, u, n):
                    chain_.tile(i)
                    dve.wait_ge(o_kept, i + 1)
                    dve.wait_ge(o_y, i + 1)
                    chain_.link(v.tensor_tensor(l_x[:, u], psE[0:P, u, 0:D], bias[:, BOUT], ALU.add))
                    chain_.link(v.tensor_tensor(l_x[:, u], l_x[:, u], flat(x_all[:, ds(i, 1)]), ALU.add))
                    normalise(v, chain_, l_x[:, u], l_stats[:, u], l_moments[:, u], l_centered[:, u], o_var).then_inc(o_mom, 1)
                    chain_.end()

                def second(i, u):
                    dve.wait_ge(o_sup, i + 1)
                    alone(dve)
                    v.tensor_copy(flat(support[:, ds(i, 1)]), psG[0:P, u, 0:D]).then_inc(o_done, 1)

                pipelined(dve, first, second)

            @block.scalar
            def _(act):
                act_sets(act)

                def first(i, u, n):
                    nc.scalar.copy(l_turned[:, u], flat(hT[:, ds(i, 1)])).then_inc(o_copy, 1)

                def second(i, u):
                    act.wait_ge(o_rstd, i + 1)
                    act.wait_ge(o_mom, i + 1)
                    nc.scalar.activation(l_nodes[:, u], l_centered[:, u], ACT.Relu, scale=l_moments[:, u, 3:4]).then_inc(o_new, 1)
                    act.wait_ge(o_turn, i + 1)
                    nc.scalar.copy(l_turned2[:, u], psF[:, u, 0:P]).then_inc(o_turned, 1)

                pipelined(act, first, second)

            @block.gpsimd
            def _(pool):
                keep_and_scale(pool, o_var, o_rstd, o_mom, o_kept)

        def low_pass():
            s_var, s_rstd, s_mom, s_new = sem("low_var"), sem("low_rstd"), sem("low_mom"), sem("low_new")
            s_turn, s_turned, s_y = sem("low_turn"), sem("low_turned"), sem("low_y")
            s_fin, s_out, s_kept = sem("low_fin"), sem("low_out"), sem("low_kept")

            def dve_work(dve, s_sum, s_sum_free):
                v = nc.vector
                fin, outs = Chain(dve, s_fin, 3), Chain(dve, s_out, 4)

                def finish(i, u, n):
                    fin.tile(i)
                    dve.wait_ge(s_kept, i + 1)
                    dve.wait_ge(s_sum, i + 3)
                    fin.link(v.tensor_tensor(l_x[:, u], psE[0:P, u, 0:D], flat(x_all[:, ds(i, 1)]), ALU.add))
                    normalise(v, fin, l_x[:, u], l_stats[:, u], l_moments[:, u], l_centered[:, u], s_var).then_inc(s_mom, 1)
                    dve.sem_inc(s_sum_free, 1)
                    fin.end()

                def outputs(i, u):
                    outs.tile(i)
                    dve.wait_ge(s_y, i + 1)
                    scale = norm[:, ds(i, 1)]
                    outs.link(v.tensor_scalar(l_agg[:, u, 0:DH], psG[0:P, u, 0:DH], scale, scale, ALU.mult, ALU.mult))
                    v.tensor_tensor(flat(self_c[:, ds(i, 1)]), l_agg[:, u, 0:DH], bias[:, B1, 0:DH], ALU.add)
                    split_parts(v, outs, parts_c, i, psG[0:P, u, 0:DH], l_rest[:, u, 0:DH], DH, scale)
                    outs.end()

                pipelined(dve, finish, outputs)

            def act_work(act, i, u, s_sum):
                act.wait_ge(s_mom, i + 1)
                act.wait_ge(s_rstd, i + 1)
                nc.scalar.activation(l_nodes[:, u], l_centered[:, u], ACT.Relu, scale=l_moments[:, u, 3:4]).then_inc(s_new, 1)
                act.wait_ge(s_turn, i + 1)
                nc.scalar.copy(l_turned[:, u], psF[:, u, 0:P]).then_inc(s_turned, 1)

            def pool_work(pool):
                keep_and_scale(pool, s_var, s_rstd, s_mom, s_kept)

            def tail_1(pe, i, u):
                pe.wait_ge(s_new, i + 1)
                nc.tensor.transpose(psF[:, u, 0:P], l_nodes[:, u], ident[0:P, 0:P]).then_inc(s_turn, 1)

            def tail_2(pe, i, u):
                pe.wait_ge(s_turned, i + 1)
                nc.tensor.matmul(psG[0:P, u, 0:DH], l_turned[:, u], w_1[:], start=True, stop=True).then_inc(s_y, 1)

            convolution("low", weights_of, l_mat, support, D, (tail_1, tail_2), dve_work, act_work, pool_work, psE)

        low_pass()

        def sum_parts(v, chain_, i, u, own):
            chain_.link(v.tensor_tensor(l_agg[:, u, 0:DH], psE[0:P, u, DH:2 * DH], l_agg[:, u, 0:DH], ALU.add))
            chain_.link(v.tensor_tensor(l_agg[:, u, 0:DH], psE[0:P, u, 2 * DH:3 * DH], l_agg[:, u, 0:DH], ALU.add))
            return v.scalar_tensor_tensor(l_nodes[:, u, 0:DH], l_agg[:, u, 0:DH], norm[:, ds(i, 1)], flat(own[:, ds(i, 1)]),
                                          ALU.mult, ALU.add)

        def gcn_first():
            s_hi, s_fin = sem("gcn1_hi"), sem("gcn1_fin")

            def dve_work(dve, s_sum, s_sum_free):
                v = nc.vector
                fin = Chain(dve, s_fin, 7)
                for i, u in tiles(dve):
                    fin.tile(i)
                    dve.wait_ge(s_sum, i + 3)
                    dve.wait_ge(s_hi, i + 1)
                    fin.link(sum_parts(v, fin, i, u, self_c))
                    dve.sem_inc(s_sum_free, 1)
                    fin.link(v.tensor_scalar(l_x[:, u, 0:DH], l_nodes[:, u, 0:DH], 0.0, norm[:, ds(i, 1)], ALU.max, ALU.mult))
                    v.tensor_scalar(flat(self_d[:, ds(i, 1)]), l_x[:, u, 0:DH], norm[:, ds(i, 1)], None, ALU.mult)
                    split_parts(v, fin, parts_d, i, l_x[:, u, 0:DH], l_rest[:, u, 0:DH], DH)
                    fin.end()

            def act_work(act, i, u, s_sum):
                act.wait_ge(s_sum, i + 3)
                nc.scalar.copy(l_agg[:, u, 0:DH], psE[0:P, u, 0:DH]).then_inc(s_hi, 1)

            nothing = lambda pe, i, u: None
            convolution("gcn1", counts_of, l_mat_bf, parts_c, 3 * DH, (nothing, nothing), dve_work, act_work, lambda pool: None, psE)

        def gcn_second():
            s_hi, s_fin, s_new, s_turn = sem("gcn2_hi"), sem("gcn2_fin"), sem("gcn2_new"), sem("gcn2_turn")
            s_turned, s_y, s_out = sem("gcn2_turned"), sem("gcn2_y"), sem("gcn2_out")

            def dve_work(dve, s_sum, s_sum_free):
                v = nc.vector
                fin, outs = Chain(dve, s_fin, 2), Chain(dve, s_out, 1)

                def finish(i, u, n):
                    fin.tile(i)
                    dve.wait_ge(s_sum, i + 3)
                    dve.wait_ge(s_hi, i + 1)
                    sum_parts(v, fin, i, u, self_d).then_inc(s_new, 1)
                    dve.sem_inc(s_sum_free, 1)
                    fin.end()

                def outputs(i, u):
                    outs.tile(i)
                    dve.wait_ge(s_y, i + 1)
                    xi = flat(x_all[:, ds(i, 1)])
                    outs.link(v.tensor_tensor(l_x[:, u], psG[0:P, u, 0:D], bias[:, B2], ALU.add))
                    v.tensor_tensor(xi, l_x[:, u], xi, ALU.add)

                pipelined(dve, finish, outputs)

            def act_work(act, i, u, s_sum):
                act.wait_ge(s_sum, i + 3)
                nc.scalar.copy(l_agg[:, u, 0:DH], psE[0:P, u, 0:DH]).then_inc(s_hi, 1)
                act.wait_ge(s_turn, i + 1)
                nc.scalar.copy(l_turned[0:DH, u], psF[0:DH, u, 0:P]).then_inc(s_turned, 1)

            def tail_1(pe, i, u):
                pe.wait_ge(s_new, i + 1)
                alone(pe)
                nc.tensor.transpose(psF[0:DH, u, 0:P], l_nodes[:, u, 0:DH], ident[0:P, 0:P]).then_inc(s_turn, 1)

            def tail_2(pe, i, u):
                pe.wait_ge(s_turned, i + 1)
                nc.tensor.matmul(psG[0:P, u, 0:D], l_turned[0:DH, u], w_2[:], start=True, stop=True).then_inc(s_y, 1)

            convolution("gcn2", counts_of, l_mat_bf, parts_d, 3 * DH, (tail_1, tail_2), dve_work, act_work, lambda pool: None, psE)

        gcn_first()
        gcn_second()

        s_stored = sem("s_stored")
        with nc.Block() as block:
            @block.sync
            def _(sp):
                sp.dma_start(out.rearrange("(t p) d -> p t d", p=P), x_all[:]).then_inc(s_stored, 16)
                sp.wait_ge(s_stored, 16)

        late.close()


_INS = ["x", "src", "dst", "edge_weight", "L0_gnn_Wl1", "L0_gnn_bl1", "L0_gnn_Wr1", "L0_gnn_Wl2", "L0_gnn_bl2", "L0_gnn_Wr2",
        "L1_gnn_Wn", "L1_gnn_bn", "L1_gnn_WQ", "L1_gnn_bQ", "L1_gnn_WK", "L1_gnn_bK", "L1_gnn_WV", "L1_gnn_bV",
        "L1_gnn_WO", "L1_gnn_bO", "L1_gnn_ln_g", "L1_gnn_ln_b", "L1_gnn_Wout", "L1_gnn_bout", "L2_gnn_weight_low",
        "L3_gnn_W1", "L3_gnn_b1", "L3_gnn_W2", "L3_gnn_b2"]


def kernel(**inputs):
    import numpy as np
    import concourse.bacc as bacc
    from concourse.bass_utils import run_bass_kernel_spmd

    nc = bacc.Bacc("TRN2", target_bir_lowering=False, num_devices=1)
    arrays, A = {}, {}
    for name in _INS:
        a = np.ascontiguousarray(inputs[name])
        arrays[f"in_{name}"] = a
        A[name] = nc.dram_tensor(f"in_{name}", a.shape, mybir.dt.from_np(a.dtype), kind="ExternalInput").ap()
    scratch = {
        "count": nc.dram_tensor("count", (T, P, T, P), mybir.dt.bfloat16).ap(),
        "weight": nc.dram_tensor("weight", (T, P, T, P), mybir.dt.float32).ap(),
        "logmask": nc.dram_tensor("logmask", (T, P, N), mybir.dt.float32).ap(),
    }
    out = nc.dram_tensor("out", (N, D), mybir.dt.float32, kind="ExternalOutput").ap()
    gnn_program(nc, A, out, scratch)
    r = run_bass_kernel_spmd(nc, [arrays], core_ids=[0])
    return r.results[0]["out"]
```

```python
import math

import concourse.bass as bass
from concourse import mybir
from contextlib import ExitStack

N = 3125
E = 100000
D = 128
DH = 64
LAYERS = 4
P = 125
T = N // P
CE = 128
NG = -(-E // (CE * 128))
CH = -(-E // CE)
CP = NG * 128
W = 5
WT = P // W
NW = N // W
WC = T * W
WG = NW // P
BLOCK = 32
NB = E // BLOCK
PB = 125
GB = NB // PB
SLOTS = 2
PAD = 128
SPAN = SLOTS * 128 // BLOCK
EXTRA = SPAN * BLOCK
KEY = 128
BW = 5
BT = WT // BW
AHEAD = 3
RING = 4
PT = 4
PIECES = [(4 * j, min(4, T - 4 * j)) for j in range(-(-T // 4))]
MASKED = -1.0e30
TINY = 1.0e-18
ROUND = 12582912.0


def chain(eng, sem):
    count = [0]

    def link(ins):
        count[0] += 1
        ins.then_inc(sem, 1)
        eng.wait_ge(sem, count[0])

    return link


def gnn_program(nc, A, out, scratch):
    fp32, bf16, i32 = mybir.dt.float32, mybir.dt.bfloat16, mybir.dt.int32
    ALU, ACT, AX = mybir.AluOpType, mybir.ActivationFunctionType, mybir.AxisListType
    ds = bass.ds

    count_d, count_rest_d, weight_d, logmask_d = (scratch[k] for k in ("count", "count_rest", "weight", "logmask"))

    outer = ExitStack()

    def act_sets(act):
        nc.scalar.preload_act_table_set("natural_log_exp_and_others")

    with outer:
        def osb(name, shape, dt):
            return outer.enter_context(nc.sbuf_tensor(name, shape, dt))

        stage_sems = []

        def sem(name):
            handle = nc.alloc_semaphore(name=name)
            stage_sems.append(handle)
            return handle

        def done_with_semaphores():
            nc.clear_and_free_semaphores(list(stage_sems))
            stage_sems.clear()
            nc.all_engine_barrier()

        s_passed = outer.enter_context(nc.semaphore("s_passed"))

        def alone(eng):
            eng.sem_inc(s_passed, 1)

        def tiles(eng):
            with eng.Fori(0, T // 2) as k:
                yield eng.snap(2 * k, min_val=0, max_val=T - 3), 0
                yield eng.snap(2 * k + 1, min_val=1, max_val=T - 2), 1
            yield T - 1, 0

        ident = osb("ident", [128, 128], fp32)


        is_fast = osb("is_fast", [1, 1], i32)

        def path(eng, fast):
            flag = eng.value_load(is_fast[0:1, 0:1], min_val=0, max_val=1)
            return eng.If(flag == fast)

        fast_st = ExitStack()

        def fsb(name, shape, dt=fp32):
            return fast_st.enter_context(nc.sbuf_tensor(name, shape, dt))

        iota_p = fsb("iota_p", [128, P], bf16)
        slot_f = fsb("slot_f", [128, 3, SLOTS * (NW + AHEAD * BW)])
        F_SRC, F_KEY, F_W = range(3)

        blocks_st = ExitStack()

        def ksb(name, shape, dt=fp32):
            return blocks_st.enter_context(nc.sbuf_tensor(name, shape, dt))

        ROW = GB * BLOCK
        LONG = ROW + EXTRA
        k_src = ksb("k_src", [PB, LONG], i32)
        k_dst = ksb("k_dst", [PB, LONG], i32)
        k_w = ksb("k_w", [PB, LONG])
        k_srcf = ksb("k_srcf", [PB, LONG])
        k_dstf = ksb("k_dstf", [PB, LONG])
        k_tile = ksb("k_tile", [PB, LONG])
        k_win = ksb("k_win", [PB, LONG])
        k_eight = ksb("k_eight", [PB, LONG])
        k_rest = ksb("k_rest", [PB, LONG])
        pieces = ksb("pieces", [PB, 7, LONG], bf16)
        PARTS_OF = {F_SRC: (0,), F_KEY: (1, 2, 3), F_W: (4, 5, 6)}
        win_lo = ksb("win_lo", [PB, GB + SPAN])
        win_hi = ksb("win_hi", [PB, GB])
        block_no = ksb("block_no", [128, GB])
        iota_w = ksb("iota_w", [128, NW])
        key_base = ksb("key_base", [128, NW])
        picks = ksb("picks", [PB, GB, NW], bf16)
        ones_k = ksb("ones_k", [PB, 128], bf16)
        ones_f = ksb("ones_f", [PB, 1])
        first_block = ksb("first_block", [PB, NW])
        bad = ksb("bad", [PB, 2, GB])
        bad_sum = ksb("bad_sum", [PB, 1])
        psK = blocks_st.enter_context(nc.psum_tensor("psK", [128, 2, 2, 512], fp32))
        psB = blocks_st.enter_context(nc.psum_tensor("psB", [128, 3, 512], fp32))

        k_pad = sem("k_pad")
        k_edges = sem("k_edges")
        k_const = sem("k_const")
        k_cmp = sem("k_cmp")
        k_count = sem("k_count")
        k_flag = sem("k_flag")
        k_bad = sem("k_bad")
        k_pieces = sem("k_pieces")
        k_picks = sem("k_picks")
        k_out = sem("k_out")
        k_taken = sem("k_taken")
        k_dve = sem("k_dve")
        HALVES = ((0, 325), (325, NW - 325))
        FIELDS = [(f, s) for s in range(SLOTS) for f in (F_SRC, F_KEY, F_W)]

        with nc.Block() as block:
            @block.sync
            def _(sp):
                sp.wait_ge(k_pad, 1)
                for tile, a in ((k_dst, A["dst"]), (k_src, A["src"]), (k_w, A["edge_weight"])):
                    sp.dma_start(tile[:, 0:ROW], a.rearrange("(p r) -> p r", p=PB)).then_inc(k_edges, 16)
                    sp.dma_start(tile[0:PB - 1, ROW:LONG], a[ROW:E].rearrange("(p r) -> p r", p=PB - 1)[:, 0:EXTRA]).then_inc(k_edges, 16)

            @block.gpsimd
            def _(pool):
                g = nc.gpsimd
                g.iota(iota_w[:], [[1, NW]], base=0, channel_multiplier=0, allow_small_or_imprecise_dtypes=True)
                g.iota(key_base[:], [[KEY, NW]], base=0, channel_multiplier=0, allow_small_or_imprecise_dtypes=True)
                g.iota(block_no[:], [[1, GB]], base=0, channel_multiplier=GB, allow_small_or_imprecise_dtypes=True)
                g.iota(iota_p[:], [[1, P]], base=0, channel_multiplier=0, allow_small_or_imprecise_dtypes=True)
                g.memset(ones_f[:], 1.0)
                g.memset(ones_k[:], 1.0)
                g.memset(ident[:], 0.0).then_inc(k_const, 1)
                pool.wait_ge(k_const, 1)
                g.affine_select(out=ident[:], in_=ident[:], compare_op=ALU.not_equal, fill=1.0, base=0,
                                pattern=[[-1, 128]], channel_multiplier=1).then_inc(k_const, 1)

            @block.vector
            def _(dve):
                link = chain(dve, k_dve)
                v = nc.vector
                v.memset(slot_f[:, :, SLOTS * NW:], -1.0)
                v.memset(k_dst[:, ROW:LONG], N)
                v.memset(k_src[:, ROW:LONG], 0)
                v.memset(k_w[:, ROW:LONG], 0.0).then_inc(k_pad, 1)
                dve.wait_ge(k_edges, 6 * 16)
                v.tensor_copy(k_srcf[:], k_src[:])
                link(v.tensor_copy(k_dstf[:], k_dst[:]))
                v.tensor_scalar(k_tile[:], k_srcf[:], (P - 1) / 2, 1.0 / P, ALU.subtract, ALU.mult)
                link(v.tensor_scalar(k_win[:], k_dstf[:], (W - 1) / 2, 1.0 / W, ALU.subtract, ALU.mult))
                v.tensor_scalar(k_tile[:], k_tile[:], ROUND, ROUND, ALU.add, ALU.subtract)
                link(v.tensor_scalar(k_win[:], k_win[:], ROUND, ROUND, ALU.add, ALU.subtract))
                v.tensor_reduce(win_lo[:], k_win[:].rearrange("p (g e) -> p g e", e=BLOCK), AX.X, ALU.min)
                link(v.tensor_reduce(win_hi[:], k_win[:, 0:ROW].rearrange("p (g e) -> p g e", e=BLOCK), AX.X, ALU.max))
                v.tensor_tensor(bad[:, 0], win_lo[:, 1:GB + 1], win_hi[:], ALU.is_lt)
                link(v.tensor_tensor(bad[:, 1], win_lo[:, SPAN:SPAN + GB], win_hi[:], ALU.is_le))
                v.tensor_reduce(bad_sum[:], bad[:].rearrange("p b g -> p (b g)"), AX.X, ALU.max).then_inc(k_bad, 1)
                dve.wait_ge(k_const, 2)
                for g in range(GB):
                    v.tensor_scalar(picks[:, g], iota_w[0:PB], win_hi[:, g:g + 1], None, ALU.is_gt).then_inc(k_cmp, 1)
                v.scalar_tensor_tensor(pieces[:, 0], k_tile[:], -float(P), k_srcf[:], ALU.mult, ALU.add)
                v.tensor_scalar(k_eight[:], k_win[:], 3.5, 0.125, ALU.subtract, ALU.mult)
                link(v.scalar_tensor_tensor(k_rest[:], k_tile[:], float(W), k_dstf[:], ALU.mult, ALU.add))
                v.scalar_tensor_tensor(pieces[:, 1], k_win[:], -float(W), k_rest[:], ALU.mult, ALU.add)
                link(v.tensor_scalar(k_eight[:], k_eight[:], ROUND, ROUND, ALU.add, ALU.subtract))
                v.tensor_scalar(pieces[:, 2], k_eight[:], 8.0 * KEY, None, ALU.mult)
                link(v.scalar_tensor_tensor(k_eight[:], k_eight[:], -8.0, k_win[:], ALU.mult, ALU.add))
                v.tensor_scalar(pieces[:, 3], k_eight[:], float(KEY), None, ALU.mult)
                link(v.tensor_copy(pieces[:, 4], k_w[:]))
                link(v.tensor_tensor(k_rest[:], k_w[:], pieces[:, 4], ALU.subtract))
                link(v.tensor_copy(pieces[:, 5], k_rest[:]))
                v.tensor_tensor(pieces[:, 6], k_rest[:], pieces[:, 5], ALU.subtract).then_inc(k_pieces, 1)
                dve.wait_ge(k_flag, 1)
                v.tensor_scalar(is_fast[:], psB[0:1, 2, 0:1], 0.0, None, ALU.is_equal)
                dve.wait_ge(k_count, 1)
                for h, (w0, wn) in enumerate(HALVES):
                    last = v.tensor_copy(first_block[:, w0:w0 + wn], psB[0:PB, h, 0:wn])
                link(last)
                for g in range(GB):
                    v.tensor_scalar(picks[:, g], first_block[:], block_no[0:PB, g:g + 1], None, ALU.is_equal).then_inc(k_picks, 1)
                for n, (f, s) in enumerate(FIELDS):
                    dve.wait_ge(k_out, n + 1)
                    for h, (w0, wn) in enumerate(HALVES):
                        to = slot_f[:, f, 0:SLOTS * NW].rearrange("p (w s) -> p w s", s=SLOTS)[:, w0:w0 + wn, s]
                        if f == F_KEY:
                            last = v.tensor_tensor(to, psK[:, n % 2, h, 0:wn], key_base[:, w0:w0 + wn], ALU.subtract)
                        else:
                            last = v.tensor_copy(to, psK[:, n % 2, h, 0:wn])
                    last.then_inc(k_taken, 1)

            @block.tensor
            def _(pe):
                t = nc.tensor
                pe.wait_ge(k_const, 2)
                pe.wait_ge(k_bad, 1)
                t.matmul(psB[0:1, 2, 0:1], bad_sum[:], ones_f[:], start=True, stop=True).then_inc(k_flag, 1)
                for g in range(GB):
                    pe.wait_ge(k_cmp, g + 1)
                    for h, (w0, wn) in enumerate(HALVES):
                        last = t.matmul(psB[:, h, 0:wn], ones_k[:], picks[:, g, w0:w0 + wn], start=g == 0, stop=g == GB - 1)
                last.then_inc(k_count, 1)
                pe.wait_ge(k_pieces, 1)
                for n, (f, s) in enumerate(FIELDS):
                    if n >= 2:
                        pe.wait_ge(k_taken, n - 1)
                    for g in range(GB):
                        pe.wait_ge(k_picks, g + 1)
                        for k in PARTS_OF[f]:
                            e0 = g * BLOCK + s * 128
                            for h, (w0, wn) in enumerate(HALVES):
                                last = t.matmul(psK[:, n % 2, h, 0:wn], pieces[:, k, e0:e0 + 128], picks[:, g, w0:w0 + wn],
                                                start=g == 0 and k == PARTS_OF[f][0], stop=g == GB - 1 and k == PARTS_OF[f][-1])
                    last.then_inc(k_out, 1)

        blocks_st.close()

        dense = ExitStack()

        def dsb(name, shape, dt=fp32):
            return dense.enter_context(nc.sbuf_tensor(name, shape, dt))

        SB = BW * SLOTS
        src_hot = dsb("src_hot", [128, BT, SB, P], bf16)
        src_w = dsb("src_w", [128, BT, SB, P])
        col_hot = dsb("col_hot", [128, BT, SB, P], bf16)
        col_f = dsb("col_f", [128, BT, SB, P])
        sums = dsb("sums", [P, 2, 2, T, P])
        f_count = dsb("f_count", [P, T, P], bf16)
        f_weight = dsb("f_weight", [P, 2, T, PAD])
        f_log = dsb("f_log", [P, N])
        f_none = dsb("f_none", [P, N])
        f_logm = dsb("f_logm", [P, N])
        tiny = dsb("tiny", [P, 1])
        psN = dense.enter_context(nc.psum_tensor("psN", [128, 2, 3, 512], fp32))
        psV = dense.enter_context(nc.psum_tensor("psV", [128, 2, 512], fp32))

        f_hot = sem("f_hot")
        f_srcw = sem("f_srcw")
        f_colf = sem("f_colf")
        f_used = sem("f_used")
        f_sums = sem("f_sums")
        f_piece = sem("f_piece")
        f_mask = sem("f_mask")
        f_piece_out = sem("f_piece_out")
        f_cast = sem("f_cast")
        f_masked = sem("f_masked")
        f_tiny = sem("f_tiny")
        f_stored = [sem(f"f_stored_{k}") for k in range(2)]
        f_weight_stored = [sem(f"f_weight_stored_{u}") for u in range(2)]
        NPC2 = 2 * len(PIECES)
        PER = -(-NPC2 // BT)

        def dense_tiles(eng):
            yield 0, 0, True, None
            with eng.Fori(0, T // 2) as k:
                yield eng.snap(2 * k + 1, min_val=1, max_val=T - 2), 1, True, k + 1
                yield eng.snap(2 * k + 2, min_val=2, max_val=T - 1), 0, True, k + 1
            yield T, T % 2, False, T // 2 + 1

        with nc.Block() as block:
            @block.vector
            def _(dve):
                v = nc.vector
                with path(dve, 1):
                    v.memset(f_weight[:, :, :, P:PAD], 0.0)
                    v.memset(tiny[:], TINY).then_inc(f_tiny, 1)
                    dve.sem_inc(f_cast, 1)

                    def hot(b, r, to, f):
                        return v.tensor_tensor(
                            to[:, r], iota_p[:].rearrange("p (o c) -> p o c", o=1).broadcast_to([128, SB, P]),
                            slot_f[:, f, ds(b * SB, SB)].rearrange("p (k o) -> p k o", o=1).broadcast_to([128, SB, P]), ALU.is_equal)

                    for b in range(AHEAD):
                        hot(b, b, src_hot, F_SRC)
                        hot(b, b, col_hot, F_KEY).then_inc(f_hot, 1)
                    for i, u, now, before in dense_tiles(dve):
                        for j in range(BT):
                            if now:
                                b = i * BT + (j + AHEAD)
                                dve.wait_ge(f_used, b + 1)
                                alone(dve)
                                hot(b, (j + AHEAD) % BT, src_hot, F_SRC)
                                hot(b, (j + AHEAD) % BT, col_hot, F_KEY).then_inc(f_hot, 1)
                            if before is not None and j == 1:
                                dve.wait_ge(f_sums, i * BT + 2)
                                alone(dve)
                                dve.wait_ge(f_stored[0], i * 16)
                                alone(dve)
                                v.tensor_copy(f_count[:], sums[:, 1 - u, 0]).then_inc(f_cast, 1)
                            if before is not None and j == BT - 2:
                                dve.wait_ge(f_piece_out, (i - 1) * NPC2 + (len(PIECES) + 2))
                                alone(dve)
                                dve.wait_ge(f_masked, 2 * i)
                                alone(dve)
                                v.tensor_scalar(f_none[:], f_log[:], -1.0, MASKED, ALU.is_lt, ALU.mult).then_inc(f_mask, 1)

            @block.gpsimd
            def _(pool):
                g = nc.gpsimd
                with path(pool, 1):
                    pool.sem_inc(f_masked, 2)

                    def weighted(b, r):
                        pool.wait_ge(f_hot, b + 1)
                        alone(pool)
                        g.tensor_tensor(src_w[:, r], src_hot[:, r],
                                        slot_f[:, F_W, ds(b * SB, SB)].rearrange("p (k o) -> p k o", o=1).broadcast_to([128, SB, P]),
                                        ALU.mult).then_inc(f_srcw, 1)

                    for b in range(AHEAD):
                        weighted(b, b)
                    for i, u, now, before in dense_tiles(pool):
                        for j in range(BT):
                            if now:
                                weighted(i * BT + (j + AHEAD), (j + AHEAD) % BT)
                            if before is not None and j >= BT - 2:
                                if j == BT - 2:
                                    pool.wait_ge(f_mask, i)
                                    alone(pool)
                                    pool.wait_ge(f_stored[1], i * 16)
                                    alone(pool)
                                half = slice(0, N // 2) if j == BT - 2 else slice(N // 2, N)
                                g.tensor_tensor(f_logm[:, half], f_log[:, half], f_none[:, half], ALU.add).then_inc(f_masked, 1)

            @block.scalar
            def _(act):
                s = nc.scalar
                act_sets(act)
                with path(act, 1):
                    act.sem_inc(f_sums, 2)
                    act.sem_inc(f_piece_out, 2)
                    act.wait_ge(f_tiny, 1)

                    def columns(b, r):
                        act.wait_ge(f_hot, b + 1)
                        s.copy(col_f[:, r], col_hot[:, r]).then_inc(f_colf, 1)

                    def take_sums(i, u, j, k):
                        h = (BT * u + j) % 2
                        d0 = j * BW * W
                        if k == 0:
                            act.wait_ge(f_used, i * BT + (j + 1 + BT))
                        if k < 2:
                            s.copy(sums[:, u, k, :, d0:d0 + 4 * W].rearrange("p a (w d) -> p w a d", w=4),
                                   psN[0:P, h, k, 0:4 * WC].rearrange("p (w a d) -> p w a d", w=4, a=T))
                        else:
                            s.copy(sums[:, u, :, :, d0 + 4 * W:d0 + 5 * W],
                                   psN[0:P, h, 2, 0:2 * WC].rearrange("p (k a d) -> p k a d", k=2, a=T)).then_inc(f_sums, 1)

                    for b in range(AHEAD):
                        columns(b, b)
                    for i, u, now, before in dense_tiles(act):
                        for j in range(BT):
                            def piece(n):
                                q = PER * j + n
                                if before is not None and q < NPC2:
                                    a0, an = PIECES[q % len(PIECES)]
                                    if q < len(PIECES):
                                        act.wait_ge(f_piece, (i - 1) * NPC2 + q + 1)
                                        ins = s.activation(f_log[:, a0 * P:(a0 + an) * P], psV[0:P, q % 2, 0:an * P], ACT.Ln,
                                                           bias=tiny[:])
                                    else:
                                        if q == len(PIECES):
                                            act.wait_ge(f_weight_stored[1 - u], before * 16)
                                            alone(act)
                                        act.wait_ge(f_piece, (i - 1) * NPC2 + q + 1)
                                        ins = s.copy(f_weight[:, 1 - u, a0:a0 + an, 0:P],
                                                     psV[0:P, q % 2, 0:an * P].rearrange("p (a d) -> p a d", a=an))
                                    ins.then_inc(f_piece_out, 1)

                            if j == 0 and before is not None:
                                for k in range(3):
                                    take_sums(i - 1, 1 - u, BT - 1, k)
                                act.wait_ge(f_masked, 2 * i)
                                alone(act)
                                act.wait_ge(f_cast, i)
                                alone(act)
                            if now and j >= 1:
                                for k in range(3):
                                    take_sums(i, u, j - 1, k)
                            piece(0)
                            if now:
                                columns(i * BT + (j + AHEAD), (j + AHEAD) % BT)
                            piece(1)
                            piece(2)

            @block.tensor
            def _(pe):
                t_ = nc.tensor
                with path(pe, 1):
                    pe.sem_inc(f_used, BT)
                    for i, u, now, before in dense_tiles(pe):
                        for j in range(BT):
                            h = (BT * u + j) % 2

                            def piece(n):
                                q = PER * j + n
                                if before is not None and q < NPC2:
                                    a0, an = PIECES[q % len(PIECES)]
                                    if q == 0:
                                        pe.wait_ge(f_sums, i * BT + 2)
                                        alone(pe)
                                    pe.wait_ge(f_piece_out, (i - 1) * NPC2 + q + 1)
                                    for a in range(an):
                                        last = t_.transpose(psV[0:P, q % 2, a * P:(a + 1) * P],
                                                            sums[:, 1 - u, q // len(PIECES), a0 + a], ident[0:P, 0:P])
                                    last.then_inc(f_piece, 1)

                            def products(w, k, rows, cols):
                                to = psN[0:P, h, k, w * WC:(w + 1) * WC] if w < 4 else psN[0:P, h, 2, k * WC:(k + 1) * WC]
                                for s in range(SLOTS):
                                    x = w * SLOTS + s
                                    last = t_.matmul(to, rows[:, j, x], cols[:, j, x], start=s == 0, stop=s == SLOTS - 1)
                                return last

                            if now:
                                pe.wait_ge(f_sums, i * BT + j + 1)
                                pe.wait_ge(f_colf, i * BT + j + 1)
                                for w in range(BW):
                                    products(w, 0, src_hot, col_hot)
                                pe.wait_ge(f_srcw, i * BT + j + 1)
                                products(0, 1, src_w, col_f)
                            piece(0)
                            if now:
                                for w in (1, 2):
                                    products(w, 1, src_w, col_f)
                            piece(1)
                            if now:
                                for w in (3, 4):
                                    last = products(w, 1, src_w, col_f)
                                last.then_inc(f_used, 1)
                            piece(2)

            @block.sync
            def _(sp):
                with path(sp, 1):
                    for s in f_stored + f_weight_stored:
                        sp.sem_inc(s, 16)
                    for t, u in tiles(sp):
                        sp.wait_ge(f_cast, t + 2)
                        alone(sp)
                        sp.dma_start(count_d[ds(t, 1)].rearrange("o p a d -> (o p) (a d)"), f_count[:].rearrange("p a d -> p (a d)")).then_inc(f_stored[0], 16)
                        sp.wait_ge(f_masked, 2 * t + 4)
                        alone(sp)
                        sp.dma_start(logmask_d[ds(t, 1)].rearrange("o p n -> (o p) n"), f_logm[:]).then_inc(f_stored[1], 16)
                        sp.wait_ge(f_piece_out, t * NPC2 + (NPC2 + 2))
                        alone(sp)
                        sp.dma_start(weight_d[:, :, ds(t, 1)].rearrange("a p o d -> p a (o d)"), f_weight[:, u]).then_inc(f_weight_stored[u], 16)
                    for s, n in zip(f_stored + f_weight_stored, (T, T, T - T // 2, T // 2)):
                        sp.wait_ge(s, (n + 1) * 16)

        dense.close()
        fast_st.close()
        edges_st = ExitStack()

        def esb(name, shape, dt):
            return edges_st.enter_context(nc.sbuf_tensor(name, shape, dt))

        iota_col = esb("iota_col", [128, WC], bf16)
        window_base = esb("window_base", [128, NW], fp32)
        field = esb("field", [128, 5, CP], fp32)
        ranges = esb("ranges", [1, 2, NW], i32)

        prep = ExitStack()

        def psb(name, shape, dt):
            return prep.enter_context(nc.sbuf_tensor(name, shape, dt))

        src_i = psb("src_i", [128, NG, CE], i32)
        dst_i = psb("dst_i", [128, NG, CE], i32)
        w_f = psb("w_f", [128, NG, CE], fp32)
        srcf = psb("srcf", [128, NG, CE], fp32)
        dstf = psb("dstf", [128, NG, CE], fp32)
        tile_f = psb("tile_f", [128, NG, CE], fp32)
        win_f = psb("win_f", [128, NG, CE], fp32)
        tmp_f = psb("tmp_f", [128, NG, CE], fp32)
        part_bf = psb("part_bf", [128, NG, CE], bf16)
        edge_f = psb("edge_f", [128, 5, NG, CE], fp32)
        win_min = psb("win_min", [128, NG], fp32)
        win_max = psb("win_max", [128, NG], fp32)
        bc_max = psb("bc_max", [128, CP], fp32)
        bc_min = psb("bc_min", [128, CP], fp32)
        win_of = psb("win_of", [128, WG], fp32)
        chunk_no = psb("chunk_no", [128, CH], fp32)
        chunk_no1 = psb("chunk_no1", [128, CH], fp32)
        scr = psb("scr", [128, CH], fp32)
        lohi = psb("lohi", [128, 2, WG], fp32)
        psP = prep.enter_context(nc.psum_tensor("psP", [128, 4, 512], fp32))
        ranges_f = psb("ranges_f", [1, 2, NW], fp32)

        s_pad = sem("s_pad")
        s_edges = sem("s_edges")
        s_const = sem("s_const")
        s_fields = sem("s_fields")
        s_ftr = sem("s_ftr")
        s_fev = sem("s_fev")
        s_lohi = sem("s_lohi")
        s_row = sem("s_row")
        s_ranges = sem("s_ranges")
        s_dl = sem("s_dl")
        FULL = (NG - 1) * 128 * CE
        REST = (E - FULL) // CE
        LAST = E - FULL - REST * CE

        with nc.Block() as block:
            @block.sync
            def _(sp):
                with path(sp, 0):
                    sp.wait_ge(s_pad, 1)
                    for tile, a in ((src_i, A["src"]), (dst_i, A["dst"]), (w_f, A["edge_weight"])):
                        sp.dma_start(tile[:, 0:NG - 1, :], a[0:FULL].rearrange("(g p e) -> p g e", g=NG - 1, p=128)).then_inc(s_edges, 16)
                        sp.dma_start(tile[0:REST, NG - 1, :], a[FULL:FULL + REST * CE].rearrange("(p e) -> p e", p=REST)).then_inc(s_edges, 16)
                        sp.dma_start(tile[REST:REST + 1, NG - 1, 0:LAST], a[FULL + REST * CE:E].rearrange("(p e) -> p e", p=1)).then_inc(s_edges, 16)

            @block.gpsimd
            def _(pool):
                with path(pool, 0):
                    nc.gpsimd.iota(iota_col[:], [[1, WC]], base=0, channel_multiplier=0, allow_small_or_imprecise_dtypes=True)
                    nc.gpsimd.iota(window_base[:], [[-WC, NW]], base=0, channel_multiplier=0, allow_small_or_imprecise_dtypes=True)
                    nc.gpsimd.iota(win_of[:], [[P, WG]], base=0, channel_multiplier=1, allow_small_or_imprecise_dtypes=True)
                    nc.gpsimd.iota(chunk_no[:], [[1, CH]], base=0, channel_multiplier=0, allow_small_or_imprecise_dtypes=True)
                    nc.gpsimd.iota(chunk_no1[:], [[1, CH]], base=1, channel_multiplier=0, allow_small_or_imprecise_dtypes=True).then_inc(s_const, 1)

            @block.vector
            def _(dve):
                with path(dve, 0):
                    link = chain(dve, s_dl)
                    v = nc.vector
                    v.memset(src_i[:, NG - 1, :], N)
                    v.memset(dst_i[:, NG - 1, :], N - 1)
                    v.memset(w_f[:, NG - 1, :], 0.0).then_inc(s_pad, 1)
                    dve.wait_ge(s_edges, 9 * 16)
                    v.tensor_copy(srcf[:], src_i[:])
                    link(v.tensor_copy(dstf[:], dst_i[:]))
                    v.tensor_scalar(tile_f[:], srcf[:], (P - 1) / 2, 1.0 / P, ALU.subtract, ALU.mult)
                    link(v.tensor_scalar(win_f[:], dstf[:], (W - 1) / 2, 1.0 / W, ALU.subtract, ALU.mult))
                    v.tensor_scalar(tile_f[:], tile_f[:], ROUND, ROUND, ALU.add, ALU.subtract)
                    link(v.tensor_scalar(win_f[:], win_f[:], ROUND, ROUND, ALU.add, ALU.subtract))
                    v.scalar_tensor_tensor(edge_f[:, 0], tile_f[:], -float(P), srcf[:], ALU.mult, ALU.add)
                    link(v.scalar_tensor_tensor(tmp_f[:], tile_f[:], float(W), dstf[:], ALU.mult, ALU.add))
                    v.scalar_tensor_tensor(edge_f[:, 1], win_f[:], float(WC - W), tmp_f[:], ALU.mult, ALU.add)
                    v.tensor_reduce(win_min[:], win_f[:], AX.X, ALU.min)
                    v.tensor_reduce(win_max[:], win_f[:], AX.X, ALU.max)
                    link(v.tensor_copy(part_bf[:], w_f[:]))
                    v.tensor_copy(edge_f[:, 2], part_bf[:])
                    link(v.tensor_tensor(tmp_f[:], w_f[:], part_bf[:], ALU.subtract))
                    link(v.tensor_copy(part_bf[:], tmp_f[:]))
                    v.tensor_copy(edge_f[:, 3], part_bf[:])
                    link(v.tensor_tensor(tmp_f[:], tmp_f[:], part_bf[:], ALU.subtract))
                    v.tensor_copy(edge_f[:, 4], tmp_f[:]).then_inc(s_fields, 1)
                    n = 0
                    for f in range(5):
                        for h, (g0, gn) in enumerate(((0, 4), (4, NG - 4))):
                            n += 1
                            dve.wait_ge(s_ftr, n)
                            v.tensor_copy(field[:, f, g0 * 128:(g0 + gn) * 128], psP[:, h, 0:gn * 128]).then_inc(s_fev, 1)
                    for t in (bc_min, bc_max):
                        for h, (g0, gn) in enumerate(((0, 4), (4, NG - 4))):
                            n += 1
                            dve.wait_ge(s_ftr, n)
                            last = v.tensor_copy(t[:, g0 * 128:(g0 + gn) * 128], psP[:, h, 0:gn * 128]).then_inc(s_fev, 1)
                    dve.wait_ge(s_fev, n)
                    dve.wait_ge(s_const, 1)
                    for g in range(WG):
                        link(v.tensor_scalar(scr[:], bc_max[:, 0:CH], win_of[:, g:g + 1], float(1 << 20), ALU.is_lt, ALU.mult))
                        link(v.tensor_tensor(scr[:], scr[:], chunk_no[:], ALU.add))
                        link(v.tensor_reduce(lohi[:, 0, g:g + 1], scr[:], AX.X, ALU.min))
                        link(v.scalar_tensor_tensor(scr[:], bc_min[:, 0:CH], win_of[:, g:g + 1], chunk_no1[:], ALU.is_le, ALU.mult))
                        link(v.tensor_reduce(lohi[:, 1, g:g + 1], scr[:], AX.X, ALU.max))
                    link(v.tensor_scalar(lohi[:, 0], lohi[:, 0], float(CH - 1), None, ALU.min))
                    v.scalar_tensor_tensor(lohi[:, 1], lohi[:, 0], 2.0, lohi[:, 1], ALU.add, ALU.max).then_inc(s_lohi, 1)
                    dve.wait_ge(s_row, 1)
                    for b in range(2):
                        v.tensor_copy(ranges_f[:, b, 0:4 * P].rearrange("o (g p) -> o g p", g=4),
                                      psP[0:1, 2 * b, :].rearrange("o (g p) -> o g p", g=4)[:, :, 0:P])
                        last = v.tensor_copy(ranges_f[:, b, 4 * P:5 * P], psP[0:1, 2 * b + 1, 0:P])
                    link(last)
                    v.tensor_copy(ranges[:], ranges_f[:]).then_inc(s_ranges, 1)

            @block.tensor
            def _(pe):
                with path(pe, 0):
                    pe.wait_ge(s_const, 1)
                    pe.wait_ge(s_fields, 1)
                    n = 0
                    for f in range(5):
                        for h, (g0, gn) in enumerate(((0, 4), (4, NG - 4))):
                            if n >= 2:
                                pe.wait_ge(s_fev, n - 1)
                            for g in range(gn):
                                last = nc.tensor.transpose(psP[:, h, g * 128:(g + 1) * 128], edge_f[:, f, g0 + g, :], ident[:])
                            last.then_inc(s_ftr, 1)
                            n += 1
                    for t in (win_min, win_max):
                        for h, (g0, gn) in enumerate(((0, 4), (4, NG - 4))):
                            pe.wait_ge(s_fev, n - 1)
                            for g in range(gn):
                                last = nc.tensor.matmul(psP[:, h, g * 128:(g + 1) * 128],
                                                        t[:, g0 + g:g0 + g + 1].broadcast_to([128, 128]), ident[:],
                                                        start=True, stop=True)
                            last.then_inc(s_ftr, 1)
                            n += 1
                    pe.wait_ge(s_lohi, 1)
                    for b in range(2):
                        for g in range(WG):
                            last = nc.tensor.matmul(psP[0:1, 2 * b + g // 4, (g % 4) * 128:(g % 4) * 128 + P], lohi[0:P, b, g:g + 1],
                                                    ident[0:P, 0:P], start=True, stop=True)
                    last.then_inc(s_row, 1)

        prep.close()

        build = ExitStack()

        def bsb(name, shape, dt):
            return build.enter_context(nc.sbuf_tensor(name, shape, dt))

        onehot = bsb("onehot", [128, RING, 5, 128], bf16)
        stage = bsb("stage", [P, 2, 2, T, P], fp32)
        count_f = bsb("count_f", [P, T, P], fp32)
        count_bf = bsb("count_bf", [P, T, P], bf16)
        rest_bf = bsb("rest_bf", [P, T, P], bf16)
        weight_f = bsb("weight_f", [P, T, P], fp32)
        weight_T = bsb("weight_T", [P, T, PAD], fp32)
        logm = bsb("logm", [P, N], fp32)
        log_f = bsb("log_f", [P, N], fp32)
        none_f = bsb("none_f", [P, N], fp32)
        psW = build.enter_context(nc.psum_tensor("psW", [128, 2, 512], fp32))
        psT = build.enter_context(nc.psum_tensor("psT", [128, 2, 512], fp32))

        s_slot_free = sem("s_slot_free")
        s_hot = sem("s_hot")
        s_window = sem("s_window")
        s_half_free = sem("s_half_free")
        s_stage_free = sem("s_stage_free")
        s_count_f = sem("s_count_f")
        s_count_bf = sem("s_count_bf")
        s_turned = sem("s_turned")
        s_turned_free = sem("s_turned_free")
        s_ln = sem("s_ln")
        s_logmask = sem("s_logmask")
        s_logmask_free = sem("s_logmask_free")
        s_cd = sem("s_cd")
        s_rd = sem("s_rd")
        s_wd = sem("s_wd")
        s_ld = sem("s_ld")
        NP = len(PIECES)

        with nc.Block() as block:
            @block.vector
            def _(dve):
                with path(dve, 0):
                    v = nc.vector
                    dve.sem_inc(s_turned_free, 2)
                    v.memset(weight_T[:, :, P:PAD], 0.0)
                    visit = dve.alloc_register("visit_v")
                    dve.reg_mov(visit, 0)
                    with dve.Fori(0, T) as dt:
                        with dve.Fori(0, WT) as ws:
                            w = dve.snap(dt * WT + ws, min_val=0, max_val=NW - 1)
                            lo = dve.value_load(ranges[0:1, 0, ds(w, 1)], min_val=0, max_val=CH - 1)
                            hi = dve.value_load(ranges[0:1, 1, ds(w, 1)], min_val=2, max_val=CH + 1)
                            with dve.Fori(lo, hi) as c:
                                n = dve.snap(visit, min_val=0, max_val=NW * CP)
                                slot = dve.snap(n & (RING - 1), min_val=0, max_val=RING - 1)
                                dve.wait_ge(s_slot_free, n + 1)
                                v.tensor_scalar(onehot[:, ds(slot, 1), 0, 0:WC], iota_col[:], field[:, 1, ds(c, 1)],
                                                window_base[:, ds(w, 1)], ALU.subtract, ALU.is_equal)
                                v.tensor_scalar(onehot[:, ds(slot, 1), 1, 0:P], iota_col[:, 0:P], field[:, 0, ds(c, 1)], None,
                                                ALU.is_equal)
                                for k in range(3):
                                    last = v.tensor_scalar(onehot[:, ds(slot, 1), 2 + k, 0:P], iota_col[:, 0:P],
                                                           field[:, 0, ds(c, 1)], field[:, 2 + k, ds(c, 1)],
                                                           ALU.is_equal, ALU.mult)
                                last.then_inc(s_hot, 1)
                                dve.reg_add(visit, visit, 1)
                        par = dve.snap(dt & 1, min_val=0, max_val=1)
                        dve.wait_ge(s_half_free, (dt + 1) * WT + 2)
                        v.tensor_copy(weight_f[:], stage[:, ds(par, 1), 1])
                        v.tensor_copy(count_f[:], stage[:, ds(par, 1), 0]).then_inc(s_count_f, 1)
                        dve.wait_ge(s_cd, (dt + 1) * 16)
                        v.tensor_scalar(count_bf[:], stage[:, ds(par, 1), 0].rearrange('p o a d -> p (o a) d'), 1.0, None, ALU.mult).then_inc(s_count_bf, 1)
                        dve.wait_ge(s_count_bf, dt * 2 + 1)
                        alone(dve)
                        dve.wait_ge(s_rd, (dt + 1) * 16)
                        alone(dve)
                        v.tensor_tensor(rest_bf[:], stage[:, ds(par, 1), 0].rearrange('p o a d -> p (o a) d'), count_bf[:],
                                        ALU.subtract).then_inc(s_count_bf, 1)
                        dve.sem_inc(s_stage_free, 1)
                        dve.wait_ge(s_logmask, dt + 1)
                        for j, (a0, an) in enumerate(PIECES):
                            cols = slice(a0 * P, (a0 + an) * P)
                            dve.wait_ge(s_turned, dt * (2 * NP) + j + 1)
                            v.tensor_scalar(none_f[:, cols], psT[0:P, j % 2, 0:an * P], 0.0, MASKED, ALU.is_equal, ALU.mult)
                            v.tensor_scalar(log_f[:, cols], psT[0:P, j % 2, 0:an * P], 1.0, None, ALU.max).then_inc(s_turned_free, 1)
                        dve.wait_ge(s_wd, (dt + 1) * 16)
                        for j, (a0, an) in enumerate(PIECES):
                            dve.wait_ge(s_turned, dt * (2 * NP) + NP + j + 1)
                            v.tensor_copy(weight_T[:, a0:a0 + an, 0:P],
                                          psT[0:P, (NP + j) % 2, 0:an * P].rearrange("p (a d) -> p a d", a=an)).then_inc(s_turned_free, 1)

            @block.tensor
            def _(pe):
                with path(pe, 0):
                    t = nc.tensor
                    pe.sem_inc(s_slot_free, RING)
                    visit = pe.alloc_register("visit_t")
                    pe.reg_mov(visit, 0)

                    def products(w, half, first):
                        n = pe.snap(visit, min_val=0, max_val=NW * CP)
                        slot = pe.snap(n & (RING - 1), min_val=0, max_val=RING - 1)
                        pe.wait_ge(s_hot, n + 1)
                        cols = onehot[:, ds(slot, 1), 0, 0:WC]
                        t.matmul(psW[0:P, ds(half, 1), 0:WC], onehot[:, ds(slot, 1), 1, 0:P], cols,
                                 start=first, stop=True, skip_group_check=True)
                        for k in range(3):
                            last = t.matmul(psW[0:P, ds(half, 1), 128:128 + WC], onehot[:, ds(slot, 1), 2 + k, 0:P], cols,
                                            start=False, stop=True, skip_group_check=True)
                        last.then_inc(s_slot_free, 1)
                        pe.reg_add(visit, visit, 1)

                    with pe.Fori(0, T) as dt:
                        with pe.Fori(0, WT) as ws:
                            w = pe.snap(dt * WT + ws, min_val=0, max_val=NW - 1)
                            half = pe.snap(w & 1, min_val=0, max_val=1)
                            lo = pe.value_load(ranges[0:1, 0, ds(w, 1)], min_val=0, max_val=CH - 1)
                            hi = pe.value_load(ranges[0:1, 1, ds(w, 1)], min_val=2, max_val=CH + 1)
                            pe.wait_ge(s_half_free, w + 1)
                            products(w, half, True)
                            with pe.Fori(lo + 1, hi) as c:
                                products(w, half, False)
                            t.matmul(psW[0:P, ds(half, 1), 384:385], iota_col[:, 0:P], iota_col[:, 0:1],
                                     start=False, stop=True, skip_group_check=True).then_inc(s_window, 1)
                        pe.wait_ge(s_count_f, dt + 1)
                        for k, of in enumerate((count_f, weight_f)):
                            for j, (a0, an) in enumerate(PIECES):
                                pe.wait_ge(s_turned_free, dt * (2 * NP) + (k * NP + j + 1))
                                for a in range(an):
                                    last = t.transpose(psT[0:P, (k * NP + j) % 2, a * P:(a + 1) * P], of[:, a0 + a, :], ident[0:P, 0:P])
                                last.then_inc(s_turned, 1)

            @block.scalar
            def _(act):
                with path(act, 0):
                    act_sets(act)
                    act.sem_inc(s_half_free, 2)
                    act.sem_inc(s_stage_free, 1)
                    with act.Fori(0, T) as dt:
                        par = act.snap(dt & 1, min_val=0, max_val=1)
                        act.wait_ge(s_stage_free, dt + 1)
                        with act.Fori(0, WT) as ws:
                            w = act.snap(dt * WT + ws, min_val=0, max_val=NW - 1)
                            half = act.snap(w & 1, min_val=0, max_val=1)
                            act.wait_ge(s_window, w + 1)
                            for k in range(2):
                                last = nc.scalar.copy(stage[:, ds(par, 1), k, :, ds(ws * W, W)],
                                                      psW[0:P, ds(half, 1), 128 * k:128 * k + WC].rearrange("p o (a d) -> p o a d", a=T))
                            last.then_inc(s_half_free, 1)
                        act.wait_ge(s_turned_free, dt * (2 * NP) + (NP + 2))
                        nc.scalar.activation(log_f[:], log_f[:], ACT.Ln).then_inc(s_ln, 1)

            @block.gpsimd
            def _(pool):
                with path(pool, 0):
                    pool.sem_inc(s_logmask, 1)
                    with pool.Fori(0, T) as dt:
                        pool.wait_ge(s_ln, dt + 1)
                        pool.wait_ge(s_logmask_free, dt + 1)
                        nc.gpsimd.tensor_tensor(logm[:], log_f[:], none_f[:], ALU.add).then_inc(s_logmask, 1)

            @block.sync
            def _(sp):
                with path(sp, 0):
                    sp.sem_inc(s_stage_free, 1)
                    sp.sem_inc(s_cd, 16)
                    sp.sem_inc(s_rd, 16)
                    sp.sem_inc(s_wd, 16)
                    sp.sem_inc(s_logmask_free, 1)
                    with sp.Fori(0, T) as dt:
                        sp.wait_ge(s_count_bf, dt * 2 + 2)
                        alone(sp)
                        sp.dma_start(count_d[ds(dt, 1)].rearrange("o p a d -> p (o a) d"), count_bf[:]).then_inc(s_cd, 16)
                        sp.dma_start(count_rest_d[ds(dt, 1)].rearrange("o p a d -> p (o a) d"), rest_bf[:]).then_inc(s_rd, 16)
                        sp.wait_ge(s_logmask, dt + 2)
                        alone(sp)
                        sp.dma_start(logmask_d[ds(dt, 1)].rearrange("o p n -> (o p) n"), logm[:]).then_inc(s_ld, 16)
                        sp.wait_ge(s_turned_free, (dt + 1) * (2 * NP) + 2)
                        sp.dma_start(weight_d[:, :, ds(dt, 1)].rearrange("a p o d -> p a (o d)"), weight_T[:]).then_inc(s_wd, 16)
                        sp.wait_ge(s_ld, (dt + 1) * 16)
                        sp.sem_inc(s_logmask_free, 1)
                    sp.wait_ge(s_cd, (T + 1) * 16)
                    sp.wait_ge(s_rd, (T + 1) * 16)
                    sp.wait_ge(s_wd, (T + 1) * 16)

        build.close()
        edges_st.close()
        done_with_semaphores()

        x_all = osb("x_all", [P, T, D], fp32)
        inv_deg = osb("inv_deg", [P, T], fp32)
        norm = osb("norm", [P, T], fp32)
        w_sage = osb("w_sage", [128, 4, D], fp32)
        w_n = osb("w_n", [128, D], fp32)
        w_out = osb("w_out", [128, D], fp32)
        w_low = osb("w_low", [128, D], fp32)
        w_1 = osb("w_1", [128, DH], fp32)
        w_2 = osb("w_2", [DH, D], fp32)
        bias = osb("bias", [P, 6, D], fp32)
        bn_col = osb("bn_col", [128, 1], fp32)
        minus_half = osb("minus_half", [128, T], fp32)

        BL1, BL2, BN, BOUT, B1, B2 = range(6)

        def row(ap):
            return ap.rearrange("(o d) -> o d", o=1).broadcast_to([P, ap.shape[0]])

        def column(ap):
            return ap.rearrange("(d o) -> d o", o=1)

        def pipelined(eng, one, two, two_first=False):
            one(0, 0, 1)
            with eng.Fori(0, T // 2) as k:
                for u in (1, 0):
                    j = eng.snap(2 * k + (2 - u), min_val=1, max_val=T - 1)
                    i = eng.snap(2 * k + (1 - u), min_val=0, max_val=T - 2)
                    if two_first:
                        two(i, 1 - u)
                    one(j, u, eng.snap(k + (2 - u), min_val=1, max_val=T // 2 + 1))
                    if not two_first:
                        two(i, 1 - u)
            two(T - 1, 0)

        def flat(ap):
            return ap.rearrange("p o d -> p (o d)")

        class Chain:

            def __init__(self, eng, semaphore, per_tile):
                self.eng, self.sem, self.per_tile = eng, semaphore, per_tile

            def tile(self, i):
                self.base, self.n = i * self.per_tile, 0

            def link(self, ins):
                self.n += 1
                assert self.n <= self.per_tile
                ins.then_inc(self.sem, 1)
                self.eng.wait_ge(self.sem, self.base + self.n)

            def alone(self):
                self.eng.sem_inc(s_passed, 1)

            def end(self):
                assert self.n == self.per_tile, self.n

        def split_parts(v, chain_, parts, i, y, rest, width, scale=None):
            hi = parts[:, ds(i, 1), 0:width]
            mid = parts[:, ds(i, 1), width:2 * width]
            lo = parts[:, ds(i, 1), 2 * width:3 * width]
            if scale is not None:
                chain_.link(v.tensor_scalar(hi, y, scale, None, ALU.mult))
                chain_.link(v.scalar_tensor_tensor(rest, y, scale, hi.rearrange("p o d -> p (o d)"), ALU.mult, ALU.subtract))
            else:
                chain_.link(v.tensor_scalar(hi, y, 1.0, None, ALU.mult))
                chain_.link(v.tensor_tensor(rest, y, hi.rearrange("p o d -> p (o d)"), ALU.subtract))
            chain_.link(v.tensor_scalar(mid, rest, 1.0, None, ALU.mult))
            return v.tensor_tensor(lo, rest, mid.rearrange("p o d -> p (o d)"), ALU.subtract)

        def normalise(v, chain_, x, stats, moments, centered, s_var):
            chain_.link(v.bn_stats(stats, x))
            chain_.alone()
            chain_.link(v.bn_aggr(moments[:, 0:2], stats))
            v.tensor_scalar(moments[:, 2:3], moments[:, 1:2], 1e-5, None, ALU.add).then_inc(s_var, 1)
            return v.tensor_scalar(centered, x, moments[:, 0:1], None, ALU.subtract)

        def rsqrt(pool, moments, s_var, s_rstd, i, u):
            pool.wait_ge(s_var, i + 1)
            nc.gpsimd.tensor_tensor(moments[:, u, 3:4], moments[:, u, 2:3], minus_half[0:P, 0:1], ALU.pow).then_inc(s_rstd, 1)

        PARTS = 3 * D + 1

        h_att = osb("h_att", [P, T, D], fp32)
        hT = osb("hT", [128, T, P], fp32)

        sage = ExitStack()

        def ssb(name, shape, dt):
            return sage.enter_context(nc.sbuf_tensor(name, shape, dt))

        parts_a = ssb("parts_a", [P, T, PARTS], bf16)
        parts_b = ssb("parts_b", [P, T, PARTS], bf16)
        self_a = ssb("self_a", [P, T, D], fp32)
        self_b = ssb("self_b", [P, T, D], fp32)
        w_raw = ssb("w_raw", [128, 4, D], fp32)
        w_nodes = ssb("w_nodes", [P, 2, D], fp32)
        w_turned = ssb("w_turned", [128, 2, P], fp32)
        agg = ssb("agg", [P, 2, D], fp32)
        rest = ssb("rest", [P, 2, D], fp32)
        stats = ssb("stats", [P, 2, 6], fp32)
        moments = ssb("moments", [P, 2, 4], fp32)
        centered = ssb("centered", [P, 2, D], fp32)
        x_new = ssb("x_new", [P, 2, D], fp32)
        deg1 = ssb("deg1", [P, 2, 2], fp32)
        mat = ssb("mat", [P, 2, T, P], bf16)
        rest_counts = ssb("rest_counts", [P, T, P], bf16)
        psA = sage.enter_context(nc.psum_tensor("psA", [128, 2, 512], fp32))
        psY = sage.enter_context(nc.psum_tensor("psY", [128, 2, 512], fp32))
        psX = sage.enter_context(nc.psum_tensor("psX", [128, 2, 512], fp32))

        s_load = sem("s_load")
        s_half = sem("s_half")
        s_wt = sem("s_wt")
        s_wts = sem("s_wts")
        s3_mom = sem("s3_mom")
        s3_var = sem("s3_var")
        s3_rstd = sem("s3_rstd")
        s3_h = sem("s3_h")
        s3_turn = sem("s3_turn")
        s3_turned = sem("s3_turned")
        s3_y = sem("s3_y")
        s3_split = sem("s3_split")
        s3_chain = sem("s3_chain")
        s3_out = sem("s3_out")
        loads = [(x_all[:], A["x"].rearrange("(t p) d -> p t d", p=P)),
                 (w_raw[:, 0], A["L0_gnn_Wl1"]), (w_raw[:, 1], A["L0_gnn_Wr1"]),
                 (w_raw[:, 2], A["L0_gnn_Wl2"]), (w_raw[:, 3], A["L0_gnn_Wr2"]),
                 (w_n[:], A["L1_gnn_Wn"]), (w_out[:], A["L1_gnn_Wout"]), (w_low[:], A["L2_gnn_weight_low"]),
                 (w_1[:], A["L3_gnn_W1"]), (w_2[:], A["L3_gnn_W2"]),
                 (bias[:, BL1], row(A["L0_gnn_bl1"])), (bias[:, BL2], row(A["L0_gnn_bl2"])),
                 (bias[:, BN], row(A["L1_gnn_bn"])), (bias[:, BOUT], row(A["L1_gnn_bout"])),
                 (bias[:, B1, 0:DH], row(A["L3_gnn_b1"])), (bias[:, B2], row(A["L3_gnn_b2"])),
                 (bn_col[:], column(A["L1_gnn_bn"]))]

        with nc.Block() as block:
            @block.sync
            def _(sp):
                for to, a in loads:
                    sp.dma_start(to, a).then_inc(s_load, 16)

            @block.gpsimd
            def _(pool):
                nc.gpsimd.memset(parts_a[:, :, 3 * D:PARTS], 1.0)
                nc.gpsimd.memset(parts_b[:, :, 3 * D:PARTS], 1.0)
                nc.gpsimd.memset(minus_half[:], -0.5).then_inc(s_half, 1)
                pool.wait_ge(s_half, 1)
                for i, u in tiles(pool):
                    rsqrt(pool, moments, s3_var, s3_rstd, i, u)

            @block.vector
            def _(dve):
                v = nc.vector
                dve.wait_ge(s_load, 16 * len(loads))
                dve.wait_ge(s_wt, 1)
                v.tensor_copy(w_sage[:], psA[:, 0, :].rearrange("p (k d) -> p k d", k=4)).then_inc(s_wts, 1)
                chain_, split = Chain(dve, s3_chain, 2), Chain(dve, s3_out, 3)

                def moments_of(i, u, n):
                    chain_.tile(i)
                    xi = x_all[:, ds(i, 1)].rearrange("p o d -> p (o d)")
                    normalise(v, chain_, xi, stats[:, u], moments[:, u], centered[:, u], s3_var).then_inc(s3_mom, 1)
                    chain_.end()

                def outputs_of(i, u):
                    split.tile(i)
                    dve.wait_ge(s3_y, i + 1)
                    v.tensor_tensor(self_a[:, ds(i, 1)].rearrange("p o d -> p (o d)"), psY[0:P, u, D:2 * D], bias[:, BL1], ALU.add)
                    split_parts(v, split, parts_a, i, psY[0:P, u, 0:D], rest[:, u], D).then_inc(s3_split, 1)
                    split.end()

                pipelined(dve, moments_of, outputs_of)

            @block.scalar
            def _(act):
                act_sets(act)

                def scaled(i, u, n):
                    act.wait_ge(s3_mom, i + 1)
                    act.wait_ge(s3_rstd, i + 1)
                    nc.scalar.activation(w_nodes[:, u], centered[:, u], ACT.Relu, scale=moments[:, u, 3:4]).then_inc(s3_h, 1)

                def turned(i, u):
                    act.wait_ge(s3_turn, i + 1)
                    nc.scalar.copy(w_turned[:, u], psX[:, u, 0:P]).then_inc(s3_turned, 1)

                pipelined(act, scaled, turned, two_first=True)

            @block.tensor
            def _(pe):
                t = nc.tensor
                pe.wait_ge(s_load, 16 * len(loads))
                for k in range(4):
                    last = t.transpose(psA[:, 0, k * D:(k + 1) * D], w_raw[:, k], ident[:])
                last.then_inc(s_wt, 1)
                pe.wait_ge(s_wts, 1)

                def turn(i, u, n):
                    pe.wait_ge(s3_h, i + 1)
                    t.transpose(psX[:, u, 0:P], w_nodes[:, u], ident[0:P, 0:P]).then_inc(s3_turn, 1)

                def product(i, u):
                    pe.wait_ge(s3_turned, i + 1)
                    t.matmul(psY[0:P, u, 0:2 * D], w_turned[:, u], w_sage[:, 0:2].rearrange("p k d -> p (k d)"),
                             start=True, stop=True).then_inc(s3_y, 1)

                pipelined(pe, turn, product, two_first=True)

        def counts_of(i):
            return count_d[ds(i, 1)].rearrange("o p a d -> p (o a) d")

        def rests_of(i):
            return count_rest_d[ds(i, 1)].rearrange("o p a d -> p (o a) d")

        def weights_of(i):
            return weight_d[ds(i, 1)].rearrange("o p a d -> p (o a) d")

        def convolution(name, source, tile, rhs, width, tails, dve_work, act_work, pool_work, psum, rest_tile=None):
            s_loaded_rest = sem(f"{name}_loaded_rest")
            s_loaded = [sem(f"{name}_loaded_{u}") for u in range(2)]
            s_loaded_2 = [sem(f"{name}_loaded_2_{u}") for u in range(2)]
            s_mid = sem(f"{name}_mid")
            HALF = T // 2
            s_sum = sem(f"{name}_sum")
            s_sum_free = sem(f"{name}_sum_free")

            with nc.Block() as block:
                def loads(sp, rest):
                    for i, u in tiles(sp):
                        sp.wait_ge(s_mid, i + 1)
                        alone(sp)
                        sp.dma_start(tile[:, u, 0:HALF], source(i)[:, 0:HALF]).then_inc(s_loaded[u], 16)
                        sp.wait_ge(s_sum, i + 1)
                        alone(sp)
                        sp.dma_start(tile[:, u, HALF:T], source(i)[:, HALF:T]).then_inc(s_loaded_2[u], 16)
                        if rest is not None:
                            sp.wait_ge(s_sum, i + 2)
                            alone(sp)
                            sp.dma_start(rest[:], rests_of(i)).then_inc(s_loaded_rest, 16)

                def products(pe, i, u, n, before, rest):
                    pe.wait_ge(s_loaded[u], n * 16)
                    pe.wait_ge(s_sum_free, i + 1)
                    if before > 1:
                        i2 = pe.snap(i - 2, min_val=0, max_val=T - 3)
                    if before > 0:
                        i1 = pe.snap(i - 1, min_val=0, max_val=T - 2)
                    for a in range(T):
                        if a == T // 4 and before > 1:
                            tails[1](pe, i2, u)
                        if a == T - 3 and before > 0:
                            tails[0](pe, i1, 1 - u)
                        if a == HALF:
                            pe.wait_ge(s_loaded_2[u], n * 16)
                        last = nc.tensor.matmul(psum[0:P, u, 0:width], tile[:, u, a, 0:P], rhs[:, a, 0:width],
                                                start=a == 0, stop=a == T - 1 and rest is None)
                        if a == HALF - 1:
                            last.then_inc(s_mid, 1)
                    if rest is not None:
                        pe.wait_ge(s_loaded_rest, (i + 1) * 16)
                        for a in range(T):
                            last = nc.tensor.matmul(psum[0:P, u, 0:width], rest[:, a, :], rhs[:, a, 0:width],
                                                    start=False, stop=a == T - 1)
                    last.then_inc(s_sum, 1)

                def all_products(pe, rest):
                    products(pe, 0, 0, 1, 0, rest)
                    products(pe, 1, 1, 1, 1, rest)
                    with pe.Fori(0, (T - 3) // 2) as k:
                        for u in (0, 1):
                            products(pe, pe.snap(2 * k + (2 + u), min_val=2, max_val=T - 2), u, k + 2, 2, rest)
                    products(pe, T - 1, 0, T // 2 + 1, 2, rest)

                @block.sync
                def _(sp):
                    sp.sem_inc(s_sum, 2)
                    sp.sem_inc(s_mid, 2)
                    if rest_tile is None:
                        loads(sp, None)
                    else:
                        with path(sp, 1):
                            loads(sp, None)
                        with path(sp, 0):
                            loads(sp, rest_tile)

                @block.tensor
                def _(pe):
                    if rest_tile is None:
                        all_products(pe, None)
                    else:
                        with path(pe, 1):
                            all_products(pe, None)
                        with path(pe, 0):
                            all_products(pe, rest_tile)
                    tails[1](pe, T - 2, 1)
                    tails[0](pe, T - 1, 0)
                    tails[1](pe, T - 1, 0)

                @block.vector
                def _(dve):
                    dve.sem_inc(s_sum_free, 2)
                    dve_work(dve, s_sum, s_sum_free)

                @block.scalar
                def _(act):
                    act_sets(act)
                    for i, u in tiles(act):
                        act_work(act, i, u, s_sum)

                @block.gpsimd
                def _(pool):
                    pool_work(pool)

        for layer in (1, 2):
            name = f"sage{layer}"
            parts, self_in = ((parts_a, self_a), (parts_b, self_b))[layer - 1]
            s_hi = sem(name + "_hi")
            s_var = sem(name + "_var")
            s_rstd = sem(name + "_rstd")
            s_mom = sem(name + "_mom")
            s_new = sem(name + "_new")
            s_turn = sem(name + "_turn")
            s_turned = sem(name + "_turned")
            s_y = sem(name + "_y")
            s_kept = sem(name + "_kept")
            s_fin = sem(name + "_fin")
            s_out = sem(name + "_out")

            def dve_work(dve, s_sum, s_sum_free, layer=layer, self_in=self_in, s_hi=s_hi, s_mom=s_mom, s_var=s_var, s_new=s_new, s_y=s_y,
                         s_kept=s_kept, s_fin=s_fin, s_out=s_out):
                v = nc.vector
                fin, outs = Chain(dve, s_fin, 6), Chain(dve, s_out, 3)

                def finish(i, u, n):
                    fin.tile(i)
                    dve.wait_ge(s_sum, i + 3)
                    dve.wait_ge(s_hi, i + 1)
                    if layer == 1:
                        fin.link(v.tensor_scalar(deg1[:, u, 0:1], psA[0:P, u, 3 * D:PARTS], 1.0, None, ALU.max))
                        fin.link(v.reciprocal(deg1[:, u, 1:2], deg1[:, u, 0:1]))
                        fin.link(v.tensor_scalar(inv_deg[:, ds(i, 1)], deg1[:, u, 1:2], 1.0, None, ALU.mult))
                        v.tensor_scalar(norm[:, ds(i, 1)], psA[0:P, u, 3 * D:PARTS], 1.0, None, ALU.add)
                    fin.link(v.tensor_tensor(agg[:, u], psA[0:P, u, D:2 * D], agg[:, u], ALU.add))
                    fin.link(v.tensor_tensor(agg[:, u], psA[0:P, u, 2 * D:3 * D], agg[:, u], ALU.add))
                    fin.link(v.scalar_tensor_tensor(agg[:, u], agg[:, u], inv_deg[:, ds(i, 1)], flat(self_in[:, ds(i, 1)]),
                                                    ALU.mult, ALU.add))
                    if layer == 1:
                        v.tensor_scalar(w_nodes[:, u], agg[:, u], 0.0, None, ALU.max).then_inc(s_new, 1)
                    else:
                        dve.wait_ge(s_kept, i + 1)
                        alone(dve)
                        fin.link(v.scalar_tensor_tensor(x_new[:, u], agg[:, u], 0.0, flat(x_all[:, ds(i, 1)]), ALU.max, ALU.add))
                        normalise(v, fin, x_new[:, u], stats[:, u], moments[:, u], centered[:, u], s_var).then_inc(s_mom, 1)
                    dve.sem_inc(s_sum_free, 1)
                    fin.end()

                def outputs(i, u):
                    outs.tile(i)
                    dve.wait_ge(s_y, i + 1)
                    if layer == 1:
                        v.tensor_tensor(flat(self_b[:, ds(i, 1)]), psY[0:P, u, D:2 * D], bias[:, BL2], ALU.add)
                        split_parts(v, outs, parts_b, i, psY[0:P, u, 0:D], rest[:, u], D)
                        outs.end()
                    else:
                        v.tensor_tensor(flat(h_att[:, ds(i, 1)]), psY[0:P, u, 0:D], bias[:, BN], ALU.add)
                        v.tensor_scalar(hT[:, ds(i, 1)].rearrange("p o d -> p (o d)"), psY[:, u, D:D + P], bn_col[:, 0:1], None, ALU.add)

                pipelined(dve, finish, outputs)

            def act_work(act, i, u, s_sum, layer=layer, s_hi=s_hi, s_mom=s_mom, s_rstd=s_rstd, s_new=s_new, s_turn=s_turn, s_turned=s_turned):
                act.wait_ge(s_sum, i + 3)
                nc.scalar.copy(agg[:, u], psA[0:P, u, 0:D]).then_inc(s_hi, 1)
                if layer == 2:
                    act.wait_ge(s_mom, i + 1)
                    act.wait_ge(s_rstd, i + 1)
                    nc.scalar.activation(w_nodes[:, u], centered[:, u], ACT.Relu, scale=moments[:, u, 3:4]).then_inc(s_new, 1)
                act.wait_ge(s_turn, i + 1)
                nc.scalar.copy(w_turned[:, u], psX[:, u, 0:P]).then_inc(s_turned, 1)

            def pool_work(pool, layer=layer, s_kept=s_kept, s_var=s_var, s_mom=s_mom, s_rstd=s_rstd):
                if layer == 2:
                    pool.sem_inc(s_kept, 2)
                    nc.gpsimd.tensor_tensor(norm[:], norm[:], minus_half[0:P, :], ALU.pow)
                    for i, u in tiles(pool):
                        rsqrt(pool, moments, s_var, s_rstd, i, u)
                        pool.wait_ge(s_mom, i + 1)
                        alone(pool)
                        nc.gpsimd.tensor_copy(flat(x_all[:, ds(i, 1)]), x_new[:, u]).then_inc(s_kept, 1)

            def tail_1(pe, i, u, s_new=s_new, s_turn=s_turn):
                pe.wait_ge(s_new, i + 1)
                nc.tensor.transpose(psX[:, u, 0:P], w_nodes[:, u], ident[0:P, 0:P]).then_inc(s_turn, 1)

            def tail_2(pe, i, u, layer=layer, s_turned=s_turned, s_y=s_y):
                pe.wait_ge(s_turned, i + 1)
                if layer == 1:
                    nc.tensor.matmul(psY[0:P, u, 0:2 * D], w_turned[:, u], w_sage[:, 2:4].rearrange("p k d -> p (k d)"),
                                     start=True, stop=True).then_inc(s_y, 1)
                else:
                    nc.tensor.matmul(psY[0:P, u, 0:D], w_turned[:, u], w_n[:], start=True, stop=True)
                    nc.tensor.matmul(psY[:, u, D:D + P], w_n[:], w_turned[:, u], start=True, stop=True,
                                     skip_group_check=True).then_inc(s_y, 1)

            convolution(name, counts_of, mat, parts, PARTS, (tail_1, tail_2), dve_work, act_work, pool_work, psA, rest_counts)
        sage.close()

        att = ExitStack()

        def asb(name, shape, dt=fp32):
            return att.enter_context(nc.sbuf_tensor(name, shape, dt))

        SCALE = float(D) ** -0.5
        NPC = len(PIECES)
        EVEN = [j for j in range(NPC) if j % 2 == 0]
        ODD = [j for j in range(NPC) if j % 2 == 1]
        EXP = [(0, 3), (3, 5), (5, NPC)]

        wl = asb("wl", [128, 4, D])
        rows_l = asb("rows_l", [P, 3, D])
        cols_l = asb("cols_l", [128, 3])
        wl_next = asb("wl_next", [128, 4, D])
        rows_next = asb("rows_next", [P, 3, D])
        cols_next = asb("cols_next", [128, 3])
        bq_scaled = asb("bq_scaled", [128, 1])
        kT = asb("kT", [128, T, P])
        wv_turned = asb("wv_turned", [128, D])
        wvo = asb("wvo", [128, D])
        bvo = asb("bvo", [P, D])
        vo = asb("vo", [P, T, D])
        qT = asb("qT", [128, 2, P])
        probs = asb("probs", [P, 2, N])
        logm_in = asb("logm_in", [P, 2, N])
        probs_T = asb("probs_T", [P, 3, 4 * P])
        piece_max = asb("piece_max", [P, 2, NPC])
        neg_max = asb("neg_max", [P, 2, 2])
        row_sum = asb("row_sum", [P, 2, 4])
        inv_sum = asb("inv_sum", [P, 2, 2])
        y_att = asb("y_att", [P, 2, D])
        c_att = asb("c_att", [P, 2, D])
        h_new = asb("h_new", [P, 2, D])
        st_att = asb("st_att", [P, 2, 6])
        mo_att = asb("mo_att", [P, 2, 4])
        psS = att.enter_context(nc.psum_tensor("psS", [128, 3, 512], fp32))
        psR = att.enter_context(nc.psum_tensor("psR", [128, 2, 512], fp32))
        psO = att.enter_context(nc.psum_tensor("psO", [128, 512], fp32))
        psQ = att.enter_context(nc.psum_tensor("psQ", [128, 512], fp32))
        psH = att.enter_context(nc.psum_tensor("psH", [128, 512], fp32))

        a_w = sem("a_w")
        a_wl = sem("a_wl")
        a_bq = sem("a_bq")
        a_rows = sem("a_rows")
        a_inv = sem("a_inv")
        a_wvo = sem("a_wvo")
        a_wvo_out = sem("a_wvo_out")
        a_k = sem("a_k")
        a_k_out = sem("a_k_out")
        a_vo = sem("a_vo")
        a_vo_out = sem("a_vo_out")
        a_q = sem("a_q")
        a_q_out = sem("a_q_out")
        a_logm = [sem(f"a_logm_{u}") for u in range(2)]
        a_logm_free = sem("a_logm_free")
        a_s = sem("a_s")
        a_s_out = sem("a_s_out")
        a_max = sem("a_max")
        a_exp = sem("a_exp")
        a_t = sem("a_t")
        a_t_dve = sem("a_t_dve")
        a_t_act = sem("a_t_act")
        a_pv = sem("a_pv")
        a_o = sem("a_o")
        a_var = sem("a_var")
        a_cen = sem("a_cen")
        a_h = sem("a_h")
        a_h_kept = sem("a_h_kept")
        a_hT = sem("a_hT")
        a_hT_out = sem("a_hT_out")
        a_mx_chain = sem("a_mx_chain")
        a_inv_chain = sem("a_inv_chain")
        a_norm = sem("a_norm")
        a_pool_chain = sem("a_pool_chain")
        NLOADS = 10
        ONE_AHEAD = {"pe": (a_pv,), "dve": (a_s_out, a_t_dve, a_o, a_rows, a_inv), "act": (a_q_out, a_t_act, a_hT_out), "pool": (a_h_kept,)}

        def ahead(eng, name):
            for s in ONE_AHEAD[name]:
                eng.sem_inc(s, 1)

        def flat_t(ap):
            return ap.rearrange("p a d -> p (a d)")

        def steps(eng, l):
            def one(s):
                return s, eng.snap(l * T + s, min_val=s, max_val=(LAYERS - 1) * T + s), s % 2
            for s in (0, 1, 2):
                yield one(s)
            with eng.Fori(0, (T - 5) // 2) as k:
                for d in (3, 4):
                    s = eng.snap(2 * k + d, min_val=3, max_val=T - 3)
                    yield s, eng.snap(l * T + s, min_val=3, max_val=(LAYERS - 1) * T + T - 3), d % 2
            for s in range(T - 2, T + 3):
                yield one(s)

        def has(s, back):
            return True if not isinstance(s, int) else 0 <= s - back < T

        with nc.Block() as block:
            @block.sync
            def _(sp):
                def weights(l):
                    sp.wait_ge(a_rows, l + 1)
                    alone(sp)
                    one = ds(l, 1)
                    for k, w in enumerate(("WQ", "WK", "WV", "WO")):
                        sp.dma_start(wl_next[:, k], A["L1_gnn_" + w][one].rearrange("o i j -> (o i) j")).then_inc(a_w, 16)
                    for k, w in enumerate(("bO", "ln_g", "ln_b")):
                        sp.dma_start(rows_next[:, k], A["L1_gnn_" + w][one].broadcast_to([P, D])).then_inc(a_w, 16)
                    for k, w in enumerate(("bQ", "bK", "bV")):
                        sp.dma_start(cols_next[:, k:k + 1], A["L1_gnn_" + w][one].rearrange("o d -> d o")).then_inc(a_w, 16)

                def log_masks(l):
                    for s, g, u in steps(sp, l):
                        if not has(s, 0):
                            continue
                        sp.wait_ge(a_logm_free, g + 2 if isinstance(s, int) and s == 0 else g + 1 if not isinstance(s, int) or s > 1 else g)
                        sp.dma_start(logm_in[:, u], logmask_d[ds(s, 1)].rearrange("o p n -> (o p) n")).then_inc(a_logm[u], 16)

                weights(0)
                with sp.Fori(0, LAYERS - 1) as l:
                    log_masks(l)
                    weights(l + 1)
                log_masks(LAYERS - 1)

            @block.tensor
            def _(pe):
                t = nc.tensor
                ahead(pe, "pe")

                def queries(s1, g1):
                    pe.wait_ge(a_q_out, g1 + 1)
                    alone(pe)
                    t.matmul(psQ[:, 0:P], wl[:, 0], flat(hT[:, ds(s1, 1)]), start=True, stop=True).then_inc(a_q, 1)

                def values(g, u, j):
                    a0, an = PIECES[j]
                    if j == 0:
                        pe.wait_ge(a_o, g + 1)
                    if j % 2 == 0:
                        pe.wait_ge(a_t_dve, g * len(EVEN) + j // 2 + 2)
                    else:
                        pe.wait_ge(a_t_act, g * len(ODD) + j // 2 + 2)
                    for a in range(an):
                        last = t.matmul(psO[0:P, 0:D], probs_T[:, j % 3, a * P:(a + 1) * P], vo[:, a0 + a],
                                        start=a0 + a == 0, stop=a0 + a == T - 1)
                    last.then_inc(a_pv, 1)

                with pe.Fori(0, LAYERS) as l:
                    pe.wait_ge(a_wl, l + 1)
                    pe.wait_ge(a_o, l * T + 1)
                    t.transpose(psO[:, 0:D], wl[:, 2], ident[:]).then_inc(a_wvo, 1)
                    pe.wait_ge(a_wvo_out, l * 2 + 1)
                    alone(pe)
                    t.matmul(psO[:, D:2 * D], wv_turned[:], wl[:, 3], start=True, stop=True)
                    pe.wait_ge(a_bq, l + 1)
                    t.matmul(psO[0:P, 2 * D:3 * D], cols_l[:, 2:3].broadcast_to([128, P]), wl[:, 3],
                             start=True, stop=True).then_inc(a_wvo, 1)
                    pe.wait_ge(a_hT_out, l * T + 1)
                    pe.wait_ge(a_s_out, l * (T * NPC) + 1)
                    for j, (a0, an) in enumerate(PIECES):
                        if j >= 3:
                            pe.wait_ge(a_k_out, l * NPC + j - 2)
                        t.matmul(psS[:, j % 3, 0:an * P], wl[:, 1], flat_t(hT[:, a0:a0 + an]),
                                 start=True, stop=True).then_inc(a_k, 1)
                        if j == 0:
                            pe.wait_ge(a_wvo_out, l * 2 + 2)
                        if j >= 2:
                            pe.wait_ge(a_vo_out, l * NPC + j - 1)
                        for a in range(an):
                            last = t.matmul(psR[0:P, j % 2, a * D:(a + 1) * D], hT[:, a0 + a], wvo[:],
                                            start=True, stop=True)
                        last.then_inc(a_vo, 1)
                    pe.wait_ge(a_k_out, (l + 1) * NPC)
                    pe.wait_ge(a_vo_out, (l + 1) * NPC)
                    queries(0, l * T)
                    for s, g, u in steps(pe, l):
                        if has(s, -1):
                            queries(s + 1, g + 1)
                        gi = pe.snap(g - 2, min_val=0, max_val=LAYERS * T) if has(s, 2) else None
                        for j, (a0, an) in enumerate(PIECES):
                            if has(s, 2):
                                if j == 0:
                                    pe.wait_ge(a_exp, gi + 1)
                                if j % 2 == 0:
                                    pe.wait_ge(a_t_dve, gi * len(EVEN) + j // 2 + 1)
                                else:
                                    pe.wait_ge(a_t_act, gi * len(ODD) + j // 2 + 1)
                                for a in range(an):
                                    last = t.transpose(psR[0:P, j % 2, a * P:(a + 1) * P],
                                                       probs[:, u, (a0 + a) * P:(a0 + a + 1) * P], ident[0:P, 0:P])
                                last.then_inc(a_t, 1)
                            if has(s, 0):
                                if j == 0:
                                    pe.wait_ge(a_q_out, g + 2)
                                if j >= 3:
                                    pe.wait_ge(a_s_out, g * NPC + j - 1)
                                elif not (isinstance(s, int) and s == 0):
                                    pe.wait_ge(a_s_out, g * NPC - (0, 2, 1)[j] + 1)
                                t.matmul(psS[0:P, j % 3, 0:an * P], qT[:, u], flat_t(kT[:, a0:a0 + an]),
                                         start=True, stop=True).then_inc(a_s, 1)
                            if has(s, 2) and j >= 1:
                                values(gi, u, j - 1)
                            if j == NPC - 1 and has(s, 3):
                                pe.wait_ge(a_h, g - 2)
                                pe.wait_ge(a_hT_out, g - 2)
                                t.transpose(psH[:, 0:P], h_new[:, 1 - u], ident[0:P, 0:P]).then_inc(a_hT, 1)
                        if has(s, 2):
                            values(gi, u, NPC - 1)

            @block.vector
            def _(dve):
                v = nc.vector
                mx, inv = Chain(dve, a_mx_chain, 1), Chain(dve, a_inv_chain, 2)
                dve.sem_inc(a_logm_free, 2)
                ahead(dve, "dve")
                with dve.Fori(0, LAYERS) as l:
                    dve.wait_ge(a_w, (l + 1) * (NLOADS * 16))
                    dve.wait_ge(a_q_out, l * T + 1)
                    alone(dve)
                    v.tensor_copy(wl[:], wl_next[:]).then_inc(a_wl, 1)
                    v.tensor_copy(cols_l[:], cols_next[:])
                    v.tensor_scalar(bq_scaled[:], cols_next[:, 0:1], SCALE, None, ALU.mult).then_inc(a_bq, 1)
                    dve.wait_ge(a_h_kept, l * T + 1)
                    alone(dve)
                    v.tensor_copy(rows_l[:], rows_next[:]).then_inc(a_rows, 1)
                    dve.wait_ge(a_rows, l + 2)
                    alone(dve)
                    for j, (a0, an) in enumerate(PIECES):
                        dve.wait_ge(a_vo, l * NPC + j + 1)
                        if j == 0:
                            dve.wait_ge(a_wvo_out, l * 2 + 2)
                            alone(dve)
                        v.tensor_tensor(vo[:, a0:a0 + an], psR[0:P, j % 2, 0:an * D].rearrange("p (a d) -> p a d", a=an),
                                        bvo[:].rearrange("p (o d) -> p o d", o=1).broadcast_to([P, an, D]),
                                        ALU.add).then_inc(a_vo_out, 1)
                    for s, g, u in steps(dve, l):
                        if has(s, 0):
                            n = l * (T // 2 + 1 - u) + (s // 2 + 1)
                            dve.wait_ge(a_logm[u], n * 16)
                            alone(dve)
                        gi = dve.snap(g - 2, min_val=0, max_val=LAYERS * T) if has(s, 2) else None

                        def finish(stage):
                            i, x = s - 3, 1 - u
                            if stage == 0:
                                dve.wait_ge(a_inv, g - 1)
                                alone(dve)
                                dve.wait_ge(a_pv, (g - 2) * NPC + 1)
                                alone(dve)
                                v.scalar_tensor_tensor(y_att[:, x], psO[0:P, 0:D], inv_sum[:, x, 1:2], flat(h_att[:, ds(i, 1)]),
                                                       ALU.mult, ALU.add).then_inc(a_o, 1)
                            elif stage == 1:
                                dve.wait_ge(a_o, g - 1)
                                v.tensor_tensor(y_att[:, x], y_att[:, x], rows_l[:, 0], ALU.add).then_inc(a_norm, 1)
                            elif stage == 2:
                                dve.wait_ge(a_norm, (g - 3) * 3 + 1)
                                v.bn_stats(st_att[:, x], y_att[:, x]).then_inc(a_norm, 1)
                            elif stage == 3:
                                dve.wait_ge(a_norm, (g - 3) * 3 + 2)
                                alone(dve)
                                v.bn_aggr(mo_att[:, x, 0:2], st_att[:, x]).then_inc(a_norm, 1)
                            elif stage == 4:
                                dve.wait_ge(a_norm, (g - 3) * 3 + 3)
                                v.tensor_scalar(mo_att[:, x, 2:3], mo_att[:, x, 1:2], 1e-5, None, ALU.add).then_inc(a_var, 1)
                                v.tensor_scalar(c_att[:, x], y_att[:, x], mo_att[:, x, 0:1], None, ALU.subtract).then_inc(a_cen, 1)

                        for j, (a0, an) in enumerate(PIECES):
                            cols = slice(a0 * P, (a0 + an) * P)
                            if has(s, 3) and j == 0:
                                finish(0)
                            if has(s, 2) and j in EVEN:
                                dve.wait_ge(a_t, gi * NPC + j + 1)
                                dve.wait_ge(a_pv, gi * NPC + (j - 2 if j >= 3 else 0) + 1)
                                v.tensor_copy(probs_T[:, j % 3, 0:an * P], psR[0:P, j % 2, 0:an * P]).then_inc(a_t_dve, 1)
                            if has(s, 0):
                                if has(s, 2):
                                    dve.wait_ge(a_t, gi * NPC + j + 1)
                                    alone(dve)
                                dve.wait_ge(a_s, g * NPC + j + 1)
                                alone(dve)
                                v.tensor_tensor_reduce(out=probs[:, u, cols], in0=psS[0:P, j % 3, 0:an * P], in1=logm_in[:, u, cols],
                                                       scale=1.0, scalar=-3.0e38, op0=ALU.add, op1=ALU.max,
                                                       accum_out=piece_max[:, u, j:j + 1]).then_inc(a_s_out, 1)
                            if has(s, 3) and j > 0:
                                finish(j)
                            if has(s, 2) and j == NPC - 2:
                                inv.tile(gi)
                                dve.wait_ge(a_exp, gi + 1)
                                inv.link(v.tensor_reduce(inv_sum[:, u, 0:1], row_sum[:, u, 0:len(EXP)], AX.X, ALU.add))
                                inv.link(v.tensor_scalar(inv_sum[:, u, 0:1], inv_sum[:, u, 0:1], 1e-30, None, ALU.max))
                                v.reciprocal(inv_sum[:, u, 1:2], inv_sum[:, u, 0:1]).then_inc(a_inv, 1)
                                inv.end()
                        if has(s, 0):
                            mx.tile(g)
                            dve.wait_ge(a_s_out, g * NPC + NPC + 1)
                            mx.link(v.tensor_reduce(neg_max[:, u, 0:1], piece_max[:, u], AX.X, ALU.max, negate=True))
                            v.tensor_scalar(neg_max[:, u, 1:2], neg_max[:, u, 0:1], -MASKED / 10, None, ALU.min).then_inc(a_max, 1)
                            dve.sem_inc(a_logm_free, 1)

            @block.scalar
            def _(act):
                act_sets(act)
                sc = nc.scalar
                ahead(act, "act")

                def queries_out(g1, u1):
                    act.wait_ge(a_q, g1 + 1)
                    sc.activation(qT[:, u1], psQ[:, 0:P], ACT.Identity, bias=bq_scaled[:], scale=SCALE).then_inc(a_q_out, 1)

                with act.Fori(0, LAYERS) as l:
                    act.wait_ge(a_wvo, l * 2 + 1)
                    sc.copy(wv_turned[:], psO[:, 0:D]).then_inc(a_wvo_out, 1)
                    act.wait_ge(a_wvo, l * 2 + 2)
                    sc.copy(wvo[:], psO[:, D:2 * D])
                    sc.copy(bvo[:], psO[0:P, 2 * D:3 * D]).then_inc(a_wvo_out, 1)
                    act.wait_ge(a_bq, l + 1)
                    for j, (a0, an) in enumerate(PIECES):
                        act.wait_ge(a_k, l * NPC + j + 1)
                        sc.activation(flat_t(kT[:, a0:a0 + an]), psS[:, j % 3, 0:an * P], ACT.Identity,
                                      bias=cols_l[:, 1:2]).then_inc(a_k_out, 1)
                    queries_out(l * T, 0)
                    for s, g, u in steps(act, l):
                        if has(s, -1):
                            if has(s, 1):
                                act.wait_ge(a_s, g * NPC)
                            queries_out(g + 1, 1 - u)
                        gi = act.snap(g - 2, min_val=0, max_val=LAYERS * T) if has(s, 2) else None

                        def exponentials(part):
                            p0, p1 = EXP[part]
                            cols = slice(PIECES[p0][0] * P, (PIECES[p1 - 1][0] + PIECES[p1 - 1][1]) * P)
                            ins = sc.activation(probs[:, 1 - u, cols], probs[:, 1 - u, cols], ACT.Exp,
                                                bias=neg_max[:, 1 - u, 1:2], accum_out=row_sum[:, 1 - u, part:part + 1])
                            if part == len(EXP) - 1:
                                ins.then_inc(a_exp, 1)

                        if has(s, 1):
                            if has(s, 3):
                                act.wait_ge(a_inv, g - 1)
                            act.wait_ge(a_max, g)
                        for part in range(len(EXP)):
                            if has(s, 1):
                                exponentials(part)
                            j = 2 * part + 1
                            if has(s, 2):
                                act.wait_ge(a_t, gi * NPC + j + 1)
                                act.wait_ge(a_pv, gi * NPC + (j - 2 if j >= 3 else 0) + 1)
                                a0, an = PIECES[j]
                                sc.copy(probs_T[:, j % 3, 0:an * P], psR[0:P, j % 2, 0:an * P]).then_inc(a_t_act, 1)
                            if part == len(EXP) - 1 and has(s, 3):
                                act.wait_ge(a_hT, g - 2)
                                alone(act)
                                sc.copy(flat(hT[:, ds(s - 3, 1)]), psH[:, 0:P]).then_inc(a_hT_out, 1)

            @block.gpsimd
            def _(pool):
                p = nc.gpsimd
                ahead(pool, "pool")
                link = Chain(pool, a_pool_chain, 3)
                with pool.Fori(0, LAYERS) as l:
                    for i, u in tiles(pool):
                        g = pool.snap(l * T + i, min_val=0, max_val=LAYERS * T)
                        link.tile(g)
                        pool.wait_ge(a_var, g + 1)
                        link.link(p.tensor_tensor(mo_att[:, u, 3:4], mo_att[:, u, 2:3], minus_half[0:P, 0:1], ALU.pow))
                        pool.wait_ge(a_cen, g + 1)
                        link.link(p.tensor_tensor(c_att[:, u], c_att[:, u], mo_att[:, u, 3:4].broadcast_to([P, D]), ALU.mult))
                        link.link(p.tensor_tensor(c_att[:, u], c_att[:, u], rows_l[:, 1], ALU.mult))
                        p.tensor_tensor(h_new[:, u], c_att[:, u], rows_l[:, 2], ALU.add).then_inc(a_h, 1)
                        pool.wait_ge(a_h, g + 1)
                        alone(pool)
                        p.tensor_copy(flat(h_att[:, ds(i, 1)]), h_new[:, u]).then_inc(a_h_kept, 1)
        att.close()

        late = ExitStack()

        def lsb(name, shape, dt=fp32):
            return late.enter_context(nc.sbuf_tensor(name, shape, dt))

        support = lsb("support", [P, T, D])
        parts_c = lsb("parts_c", [P, T, 3 * DH], bf16)
        parts_d = lsb("parts_d", [P, T, 3 * DH], bf16)
        self_c = lsb("self_c", [P, T, DH])
        self_d = lsb("self_d", [P, T, DH])
        l_nodes = lsb("l_nodes", [P, 2, D])
        l_turned = lsb("l_turned", [128, 2, P])
        l_turned2 = lsb("l_turned2", [128, 2, P])
        l_agg = lsb("l_agg", [P, 2, D])
        l_rest = lsb("l_rest", [P, 2, D])
        l_stats = lsb("l_stats", [P, 2, 6])
        l_moments = lsb("l_moments", [P, 2, 4])
        l_centered = lsb("l_centered", [P, 2, D])
        l_x = lsb("l_x", [P, 2, D])
        l_mat = lsb("l_mat", [P, 2, T, PAD])
        l_rest_counts = lsb("l_rest_counts", [P, T, P], bf16)
        l_mat_bf = lsb("l_mat_bf", [P, 2, T, P], bf16)
        psE = late.enter_context(nc.psum_tensor("psE", [128, 2, 512], fp32))
        psF = late.enter_context(nc.psum_tensor("psF", [128, 2, 512], fp32))
        psG = late.enter_context(nc.psum_tensor("psG", [128, 2, 512], fp32))

        def keep_and_scale(pool, s_var, s_rstd, s_mom, s_kept):
            pool.sem_inc(s_kept, 2)
            for i, u in tiles(pool):
                rsqrt(pool, l_moments, s_var, s_rstd, i, u)
                pool.wait_ge(s_mom, i + 1)
                alone(pool)
                nc.gpsimd.tensor_copy(flat(x_all[:, ds(i, 1)]), l_x[:, u]).then_inc(s_kept, 1)

        o_copy = sem("o_copy")
        o_y = sem("o_y")
        o_var = sem("o_var")
        o_rstd = sem("o_rstd")
        o_mom = sem("o_mom")
        o_kept = sem("o_kept")
        o_new = sem("o_new")
        o_turn = sem("o_turn")
        o_turned = sem("o_turned")
        o_sup = sem("o_sup")
        o_chain = sem("o_chain")
        o_done = sem("o_done")

        with nc.Block() as block:
            @block.tensor
            def _(pe):
                def first(i, u, n):
                    pe.wait_ge(o_copy, i + 1)
                    nc.tensor.matmul(psE[0:P, u, 0:D], l_turned[:, u], w_out[:], start=True, stop=True).then_inc(o_y, 1)

                def second(i, u):
                    pe.wait_ge(o_new, i + 1)
                    nc.tensor.transpose(psF[:, u, 0:P], l_nodes[:, u], ident[0:P, 0:P]).then_inc(o_turn, 1)
                    pe.wait_ge(o_turned, i + 1)
                    nc.tensor.matmul(psG[0:P, u, 0:D], l_turned2[:, u], w_low[:], start=True, stop=True).then_inc(o_sup, 1)

                pipelined(pe, first, second)

            @block.vector
            def _(dve):
                v = nc.vector
                chain_ = Chain(dve, o_chain, 4)

                def first(i, u, n):
                    chain_.tile(i)
                    dve.wait_ge(o_kept, i + 1)
                    dve.wait_ge(o_y, i + 1)
                    chain_.link(v.tensor_tensor(l_x[:, u], psE[0:P, u, 0:D], bias[:, BOUT], ALU.add))
                    chain_.link(v.tensor_tensor(l_x[:, u], l_x[:, u], flat(x_all[:, ds(i, 1)]), ALU.add))
                    normalise(v, chain_, l_x[:, u], l_stats[:, u], l_moments[:, u], l_centered[:, u], o_var).then_inc(o_mom, 1)
                    chain_.end()

                def second(i, u):
                    dve.wait_ge(o_sup, i + 1)
                    alone(dve)
                    v.tensor_copy(flat(support[:, ds(i, 1)]), psG[0:P, u, 0:D]).then_inc(o_done, 1)

                pipelined(dve, first, second)

            @block.scalar
            def _(act):
                act_sets(act)

                def first(i, u, n):
                    nc.scalar.copy(l_turned[:, u], flat(hT[:, ds(i, 1)])).then_inc(o_copy, 1)

                def second(i, u):
                    act.wait_ge(o_rstd, i + 1)
                    act.wait_ge(o_mom, i + 1)
                    nc.scalar.activation(l_nodes[:, u], l_centered[:, u], ACT.Relu, scale=l_moments[:, u, 3:4]).then_inc(o_new, 1)
                    act.wait_ge(o_turn, i + 1)
                    nc.scalar.copy(l_turned2[:, u], psF[:, u, 0:P]).then_inc(o_turned, 1)

                pipelined(act, first, second)

            @block.gpsimd
            def _(pool):
                keep_and_scale(pool, o_var, o_rstd, o_mom, o_kept)

        def low_pass():
            s_var, s_rstd, s_mom, s_new = sem("low_var"), sem("low_rstd"), sem("low_mom"), sem("low_new")
            s_turn, s_turned, s_y = sem("low_turn"), sem("low_turned"), sem("low_y")
            s_fin, s_out, s_kept = sem("low_fin"), sem("low_out"), sem("low_kept")

            def dve_work(dve, s_sum, s_sum_free):
                v = nc.vector
                fin, outs = Chain(dve, s_fin, 3), Chain(dve, s_out, 4)

                def finish(i, u, n):
                    fin.tile(i)
                    dve.wait_ge(s_kept, i + 1)
                    dve.wait_ge(s_sum, i + 3)
                    fin.link(v.tensor_tensor(l_x[:, u], psE[0:P, u, 0:D], flat(x_all[:, ds(i, 1)]), ALU.add))
                    normalise(v, fin, l_x[:, u], l_stats[:, u], l_moments[:, u], l_centered[:, u], s_var).then_inc(s_mom, 1)
                    dve.sem_inc(s_sum_free, 1)
                    fin.end()

                def outputs(i, u):
                    outs.tile(i)
                    dve.wait_ge(s_y, i + 1)
                    scale = norm[:, ds(i, 1)]
                    outs.link(v.tensor_scalar(l_agg[:, u, 0:DH], psG[0:P, u, 0:DH], scale, scale, ALU.mult, ALU.mult))
                    v.tensor_tensor(flat(self_c[:, ds(i, 1)]), l_agg[:, u, 0:DH], bias[:, B1, 0:DH], ALU.add)
                    split_parts(v, outs, parts_c, i, psG[0:P, u, 0:DH], l_rest[:, u, 0:DH], DH, scale)
                    outs.end()

                pipelined(dve, finish, outputs)

            def act_work(act, i, u, s_sum):
                act.wait_ge(s_mom, i + 1)
                act.wait_ge(s_rstd, i + 1)
                nc.scalar.activation(l_nodes[:, u], l_centered[:, u], ACT.Relu, scale=l_moments[:, u, 3:4]).then_inc(s_new, 1)
                act.wait_ge(s_turn, i + 1)
                nc.scalar.copy(l_turned[:, u], psF[:, u, 0:P]).then_inc(s_turned, 1)

            def pool_work(pool):
                keep_and_scale(pool, s_var, s_rstd, s_mom, s_kept)

            def tail_1(pe, i, u):
                pe.wait_ge(s_new, i + 1)
                nc.tensor.transpose(psF[:, u, 0:P], l_nodes[:, u], ident[0:P, 0:P]).then_inc(s_turn, 1)

            def tail_2(pe, i, u):
                pe.wait_ge(s_turned, i + 1)
                nc.tensor.matmul(psG[0:P, u, 0:DH], l_turned[:, u], w_1[:], start=True, stop=True).then_inc(s_y, 1)

            convolution("low", weights_of, l_mat, support, D, (tail_1, tail_2), dve_work, act_work, pool_work, psE)

        low_pass()

        def sum_parts(v, chain_, i, u, own):
            chain_.link(v.tensor_tensor(l_agg[:, u, 0:DH], psE[0:P, u, DH:2 * DH], l_agg[:, u, 0:DH], ALU.add))
            chain_.link(v.tensor_tensor(l_agg[:, u, 0:DH], psE[0:P, u, 2 * DH:3 * DH], l_agg[:, u, 0:DH], ALU.add))
            return v.scalar_tensor_tensor(l_nodes[:, u, 0:DH], l_agg[:, u, 0:DH], norm[:, ds(i, 1)], flat(own[:, ds(i, 1)]),
                                          ALU.mult, ALU.add)

        def gcn_first():
            s_hi, s_fin = sem("gcn1_hi"), sem("gcn1_fin")

            def dve_work(dve, s_sum, s_sum_free):
                v = nc.vector
                fin = Chain(dve, s_fin, 7)
                for i, u in tiles(dve):
                    fin.tile(i)
                    dve.wait_ge(s_sum, i + 3)
                    dve.wait_ge(s_hi, i + 1)
                    fin.link(sum_parts(v, fin, i, u, self_c))
                    dve.sem_inc(s_sum_free, 1)
                    fin.link(v.tensor_scalar(l_x[:, u, 0:DH], l_nodes[:, u, 0:DH], 0.0, norm[:, ds(i, 1)], ALU.max, ALU.mult))
                    v.tensor_scalar(flat(self_d[:, ds(i, 1)]), l_x[:, u, 0:DH], norm[:, ds(i, 1)], None, ALU.mult)
                    split_parts(v, fin, parts_d, i, l_x[:, u, 0:DH], l_rest[:, u, 0:DH], DH)
                    fin.end()

            def act_work(act, i, u, s_sum):
                act.wait_ge(s_sum, i + 3)
                nc.scalar.copy(l_agg[:, u, 0:DH], psE[0:P, u, 0:DH]).then_inc(s_hi, 1)

            nothing = lambda pe, i, u: None
            convolution("gcn1", counts_of, l_mat_bf, parts_c, 3 * DH, (nothing, nothing), dve_work, act_work, lambda pool: None, psE,
                        l_rest_counts)

        def gcn_second():
            s_hi, s_fin, s_new, s_turn = sem("gcn2_hi"), sem("gcn2_fin"), sem("gcn2_new"), sem("gcn2_turn")
            s_turned, s_y, s_out = sem("gcn2_turned"), sem("gcn2_y"), sem("gcn2_out")

            def dve_work(dve, s_sum, s_sum_free):
                v = nc.vector
                fin, outs = Chain(dve, s_fin, 2), Chain(dve, s_out, 1)

                def finish(i, u, n):
                    fin.tile(i)
                    dve.wait_ge(s_sum, i + 3)
                    dve.wait_ge(s_hi, i + 1)
                    sum_parts(v, fin, i, u, self_d).then_inc(s_new, 1)
                    dve.sem_inc(s_sum_free, 1)
                    fin.end()

                def outputs(i, u):
                    outs.tile(i)
                    dve.wait_ge(s_y, i + 1)
                    xi = flat(x_all[:, ds(i, 1)])
                    outs.link(v.tensor_tensor(l_x[:, u], psG[0:P, u, 0:D], bias[:, B2], ALU.add))
                    v.tensor_tensor(xi, l_x[:, u], xi, ALU.add)

                pipelined(dve, finish, outputs)

            def act_work(act, i, u, s_sum):
                act.wait_ge(s_sum, i + 3)
                nc.scalar.copy(l_agg[:, u, 0:DH], psE[0:P, u, 0:DH]).then_inc(s_hi, 1)
                act.wait_ge(s_turn, i + 1)
                nc.scalar.copy(l_turned[0:DH, u], psF[0:DH, u, 0:P]).then_inc(s_turned, 1)

            def tail_1(pe, i, u):
                pe.wait_ge(s_new, i + 1)
                alone(pe)
                nc.tensor.transpose(psF[0:DH, u, 0:P], l_nodes[:, u, 0:DH], ident[0:P, 0:P]).then_inc(s_turn, 1)

            def tail_2(pe, i, u):
                pe.wait_ge(s_turned, i + 1)
                nc.tensor.matmul(psG[0:P, u, 0:D], l_turned[0:DH, u], w_2[:], start=True, stop=True).then_inc(s_y, 1)

            convolution("gcn2", counts_of, l_mat_bf, parts_d, 3 * DH, (tail_1, tail_2), dve_work, act_work, lambda pool: None, psE,
                        l_rest_counts)

        gcn_first()
        gcn_second()

        s_stored = sem("s_stored")
        with nc.Block() as block:
            @block.sync
            def _(sp):
                sp.dma_start(out.rearrange("(t p) d -> p t d", p=P), x_all[:]).then_inc(s_stored, 16)
                sp.wait_ge(s_stored, 16)

        late.close()


_INS = ["x", "src", "dst", "edge_weight", "L0_gnn_Wl1", "L0_gnn_bl1", "L0_gnn_Wr1", "L0_gnn_Wl2", "L0_gnn_bl2", "L0_gnn_Wr2",
        "L1_gnn_Wn", "L1_gnn_bn", "L1_gnn_WQ", "L1_gnn_bQ", "L1_gnn_WK", "L1_gnn_bK", "L1_gnn_WV", "L1_gnn_bV",
        "L1_gnn_WO", "L1_gnn_bO", "L1_gnn_ln_g", "L1_gnn_ln_b", "L1_gnn_Wout", "L1_gnn_bout", "L2_gnn_weight_low",
        "L3_gnn_W1", "L3_gnn_b1", "L3_gnn_W2", "L3_gnn_b2"]


def kernel(**inputs):
    import numpy as np
    import concourse.bacc as bacc
    from concourse.bass_utils import run_bass_kernel_spmd

    nc = bacc.Bacc("TRN2", target_bir_lowering=False, num_devices=1)
    arrays, A = {}, {}
    for name in _INS:
        a = np.ascontiguousarray(inputs[name])
        arrays[f"in_{name}"] = a
        A[name] = nc.dram_tensor(f"in_{name}", a.shape, mybir.dt.from_np(a.dtype), kind="ExternalInput").ap()
    scratch = {
        "count": nc.dram_tensor("count", (T, P, T, P), mybir.dt.bfloat16).ap(),
        "count_rest": nc.dram_tensor("count_rest", (T, P, T, P), mybir.dt.bfloat16).ap(),
        "weight": nc.dram_tensor("weight", (T, P, T, PAD), mybir.dt.float32).ap(),
        "logmask": nc.dram_tensor("logmask", (T, P, N), mybir.dt.float32).ap(),
    }
    out = nc.dram_tensor("out", (N, D), mybir.dt.float32, kind="ExternalOutput").ap()
    gnn_program(nc, A, out, scratch)
    r = run_bass_kernel_spmd(nc, [arrays], core_ids=[0])
    return r.results[0]["out"]
```
